# Optimizing a Trainium2 kernel written in Bass

```python
import numpy as np
import jax
import jax.numpy as jnp

def _softmax(x, axis=-1):
    return jax.nn.softmax(x, axis=axis)

def _gelu(x):
    return jax.nn.gelu(x, approximate=True)

def _silu(x):
    return jax.nn.silu(x)

def _sigmoid(x):
    return jax.nn.sigmoid(x)

def _layernorm(x, axis=-1, eps=1e-05):
    m = jnp.mean(x, axis=axis, keepdims=True)
    v = jnp.var(x, axis=axis, keepdims=True)
    return (x - m) / jnp.sqrt(v + eps)

def _scatter_add(tgt, idx, src, axis=0):
    return tgt.at[idx].add(src)

def _segment_sum(src, seg, n):
    return jax.ops.segment_sum(src, seg, n)
kernel_name = 'mk_recurrent_d4_jaxref_r8_eef765'

def setup_inputs(seed: int=0):
    np.random.seed(seed)
    _w = jnp.asarray

    def _L0_attn_setup():
        import jax, jax.numpy as jnp
        import numpy as np
        DIM = 128
        HEADS = 16
        DIM_HEAD = 64
        B, S = (4, 256)
        key = jax.random.key(seed)
        ks = jax.random.split(key, 6)
        sd = 1.0 / np.sqrt(DIM)
        return {'latents': jax.random.normal(ks[0], (B, S, DIM), dtype=jnp.float32), 'ln_gamma': jnp.ones((DIM,), dtype=jnp.float32), 'ln_beta': jnp.zeros((DIM,), dtype=jnp.float32), 'Wq': jax.random.normal(ks[1], (DIM, HEADS * DIM_HEAD), dtype=jnp.float32) * sd, 'Wk': jax.random.normal(ks[2], (DIM, HEADS * DIM_HEAD), dtype=jnp.float32) * sd, 'Wv': jax.random.normal(ks[3], (DIM, HEADS * DIM_HEAD), dtype=jnp.float32) * sd, 'Wo': jax.random.normal(ks[4], (HEADS * DIM_HEAD, DIM), dtype=jnp.float32) * sd}
    _L0_attn_in = _L0_attn_setup()

    def _L0_ffn_setup():
        import jax, jax.numpy as jnp
        import numpy as np
        from jax import lax
        T, B, I, M, O = (32, 64, 128, 128, 128)

        def _xavier(key, shape):
            fan_out, fan_in = shape
            limit = float(np.sqrt(6.0 / (fan_in + fan_out)))
            return jax.random.uniform(key, shape, jnp.float32, -limit, limit)
        key = jax.random.key(seed)
        ks = jax.random.split(key, 9)
        x = jax.random.normal(ks[0], (T, B, I), jnp.float32)
        return {'x': x, 'wf': _xavier(ks[1], (M, I)), 'uf': _xavier(ks[2], (M, M)), 'bf': jnp.zeros((M,), jnp.float32), 'wi': _xavier(ks[3], (M, I)), 'ui': _xavier(ks[4], (M, M)), 'bi': jnp.zeros((M,), jnp.float32), 'wc': _xavier(ks[5], (M, I)), 'uc': _xavier(ks[6], (M, M)), 'bc': jnp.zeros((M,), jnp.float32), 'wo': _xavier(ks[7], (O, I)), 'uo': _xavier(ks[8], (O, M)), 'bo': jnp.zeros((O,), jnp.float32), 'in_c': jnp.zeros((M,), jnp.float32)}
    _L0_ffn_in = _L0_ffn_setup()

    def _L1_attn_setup():
        import jax, jax.numpy as jnp
        import numpy as np
        DIM = 128
        HEADS = 16
        DIM_HEAD = 64
        INNER = HEADS * DIM_HEAD
        EPS = 1e-05

        def layernorm(x, g, b):
            mu = jnp.mean(x, axis=-1, keepdims=True)
            var = jnp.var(x, axis=-1, keepdims=True)
            return (x - mu) * jax.lax.rsqrt(var + EPS) * g + b

        def dynamic_pos_bias(n, pb_w0, pb_b0, pb_ln0_g, pb_ln0_b, pb_w1, pb_b1, pb_ln1_g, pb_ln1_b, pb_w2, pb_b2):
            pos = jnp.arange(-n + 1, n, dtype=jnp.float32)[:, None]
            h = jax.nn.silu(layernorm(pos @ pb_w0 + pb_b0, pb_ln0_g, pb_ln0_b))
            h = jax.nn.silu(layernorm(h @ pb_w1 + pb_b1, pb_ln1_g, pb_ln1_b))
            h = h @ pb_w2 + pb_b2
            i = jnp.arange(n)
            idx = i[:, None] - i[None, :] + (n - 1)
            bias = h[idx]
            return jnp.transpose(bias, (2, 0, 1))

        def attention_fwd(x, ln_g, ln_b, Wq, Wkv, null_kv, null_attn_bias, pb_w0, pb_b0, pb_ln0_g, pb_ln0_b, pb_w1, pb_b1, pb_ln1_g, pb_ln1_b, pb_w2, pb_b2, Wo, out_ln_g, out_ln_b):
            b, n, _ = x.shape
            scale = DIM_HEAD ** (-0.5)
            xn = layernorm(x, ln_g, ln_b)
            q = (xn @ Wq).reshape(b, n, HEADS, DIM_HEAD).transpose(0, 2, 1, 3) * scale
            kv = xn @ Wkv
            k, v = (kv[..., :DIM_HEAD], kv[..., DIM_HEAD:])
            nk = jnp.broadcast_to(null_kv[0], (b, 1, DIM_HEAD))
            nv = jnp.broadcast_to(null_kv[1], (b, 1, DIM_HEAD))
            k = jnp.concatenate([nk, k], axis=1)
            v = jnp.concatenate([nv, v], axis=1)
            sim = jnp.einsum('bhid,bjd->bhij', q, k)
            rel = dynamic_pos_bias(n, pb_w0, pb_b0, pb_ln0_g, pb_ln0_b, pb_w1, pb_b1, pb_ln1_g, pb_ln1_b, pb_w2, pb_b2)
            null_bias = jnp.broadcast_to(null_attn_bias[:, None, None], (HEADS, n, 1))
            attn_bias = jnp.concatenate([null_bias, rel], axis=-1)
            sim = sim + attn_bias[None]
            max_neg = -jnp.finfo(sim.dtype).max
            causal_mask = jnp.triu(jnp.ones((n, n + 1), dtype=bool), k=2)
            sim = jnp.where(causal_mask[None, None], max_neg, sim)
            attn = jax.nn.softmax(sim, axis=-1)
            out = jnp.einsum('bhij,bjd->bhid', attn, v)
            out = out.transpose(0, 2, 1, 3).reshape(b, n, INNER)
            return layernorm(out @ Wo, out_ln_g, out_ln_b)
        key = jax.random.key(seed)
        ks = jax.random.split(key, 16)
        b, n = (2, 256)
        s = 0.02
        inp = {'x': jax.random.normal(ks[0], (b, n, DIM), dtype=jnp.float32), 'ln_g': jnp.ones((DIM,), jnp.float32), 'ln_b': jnp.zeros((DIM,), jnp.float32), 'Wq': jax.random.normal(ks[1], (DIM, INNER), jnp.float32) * s, 'Wkv': jax.random.normal(ks[2], (DIM, 2 * DIM_HEAD), jnp.float32) * s, 'null_kv': jax.random.normal(ks[3], (2, DIM_HEAD), jnp.float32), 'null_attn_bias': jax.random.normal(ks[4], (HEADS,), jnp.float32), 'pb_w0': jax.random.normal(ks[5], (1, DIM), jnp.float32) * s, 'pb_b0': jnp.zeros((DIM,), jnp.float32), 'pb_ln0_g': jnp.ones((DIM,), jnp.float32), 'pb_ln0_b': jnp.zeros((DIM,), jnp.float32), 'pb_w1': jax.random.normal(ks[6], (DIM, DIM), jnp.float32) * s, 'pb_b1': jnp.zeros((DIM,), jnp.float32), 'pb_ln1_g': jnp.ones((DIM,), jnp.float32), 'pb_ln1_b': jnp.zeros((DIM,), jnp.float32), 'pb_w2': jax.random.normal(ks[7], (DIM, HEADS), jnp.float32) * s, 'pb_b2': jnp.zeros((HEADS,), jnp.float32), 'Wo': jax.random.normal(ks[8], (INNER, DIM), jnp.float32) * s, 'out_ln_g': jnp.ones((DIM,), jnp.float32), 'out_ln_b': jnp.zeros((DIM,), jnp.float32)}
        return inp
    _L1_attn_in = _L1_attn_setup()

    def _L1_ffn_setup():
        import jax, jax.numpy as jnp
        import numpy as np
        EMB = 128
        FF = 4 * EMB

        def _ternary(w):
            scale = jnp.maximum(jnp.mean(jnp.abs(w)), 1e-08)
            w_t = jnp.clip(jnp.round(w / scale), -1.0, 1.0)
            return w + jax.lax.stop_gradient(w_t - w)
        key = jax.random.key(seed)
        kx, k1, k2, kb1, kb2 = jax.random.split(key, 5)
        x = jax.random.normal(kx, (4, 256, EMB), dtype=jnp.float32)
        lim1 = 1.0 / np.sqrt(EMB)
        lim2 = 1.0 / np.sqrt(FF)
        W1 = jax.random.uniform(k1, (FF, EMB), jnp.float32, -lim1, lim1)
        b1 = jax.random.uniform(kb1, (FF,), jnp.float32, -lim1, lim1)
        W2 = jax.random.uniform(k2, (EMB, FF), jnp.float32, -lim2, lim2)
        b2 = jax.random.uniform(kb2, (EMB,), jnp.float32, -lim2, lim2)
        return {'x': x, 'W1': W1, 'b1': b1, 'W2': W2, 'b2': b2}
    _L1_ffn_in = _L1_ffn_setup()

    def _L2_attn_setup():
        import jax, jax.numpy as jnp
        import numpy as np
        HIDDEN = 128
        HEADS = 16
        HEAD_DIM = HIDDEN // HEADS
        BETA = 0.9
        CLAMP = 1.0
        STATE_CAP = 10.0
        EPS = 1e-12

        def _l2norm(x):
            n = jnp.sqrt(jnp.sum(x * x, axis=-1, keepdims=True))
            return x / jnp.maximum(n, EPS)

        def _split_heads(x, B, T):
            return x.reshape(B, T, HEADS, HEAD_DIM).transpose(0, 2, 1, 3)

        def _reference_tuple_inner(hidden_states, Wq, bq, Wk, bk, Wv, bv, Wo, bo):
            B, T, _ = hidden_states.shape
            q = _split_heads(hidden_states @ Wq.T + bq, B, T)
            k = _split_heads(hidden_states @ Wk.T + bk, B, T)
            v = _split_heads(hidden_states @ Wv.T + bv, B, T)
            q = _l2norm(q)
            k = _l2norm(k)
            qT = q.transpose(2, 0, 1, 3)
            kT = k.transpose(2, 0, 1, 3)
            vT = v.transpose(2, 0, 1, 3)
            state0 = jnp.zeros((B, HEADS, HEAD_DIM, HEAD_DIM), dtype=hidden_states.dtype)

            def step(state, qkv):
                q_t, k_t, v_t = qkv
                v_old = jnp.einsum('bhd,bhde->bhe', k_t, state)
                delta = jnp.clip(v_t - v_old, -CLAMP, CLAMP)
                update = jnp.clip(BETA * k_t[..., :, None] * delta[..., None, :], -CLAMP, CLAMP)
                state = state + update
                m = jnp.max(jnp.abs(state), axis=(-2, -1), keepdims=True)
                state = jnp.where(m > STATE_CAP, state * 0.9, state)
                o = jnp.clip(jnp.einsum('bhij,bhj->bhi', state, q_t), -CLAMP, CLAMP)
                return (state, o)
            final_state, outs = jax.lax.scan(step, state0, (qT, kT, vT))
            out = outs.transpose(1, 0, 2, 3).reshape(B, T, HIDDEN)
            out = out @ Wo.T + bo
            return (out, final_state)
        key = jax.random.key(seed)
        ks = jax.random.split(key, 9)
        B, T = (4, 128)
        std = 0.1 * float(np.sqrt(2.0 / (HIDDEN + HIDDEN)))
        mkw = lambda k: jax.random.normal(k, (HIDDEN, HIDDEN), dtype=jnp.float32) * std
        return {'hidden_states': jax.random.normal(ks[0], (B, T, HIDDEN), dtype=jnp.float32), 'Wq': mkw(ks[1]), 'bq': jnp.zeros((HIDDEN,), jnp.float32), 'Wk': mkw(ks[2]), 'bk': jnp.zeros((HIDDEN,), jnp.float32), 'Wv': mkw(ks[3]), 'bv': jnp.zeros((HIDDEN,), jnp.float32), 'Wo': mkw(ks[4]), 'bo': jnp.zeros((HIDDEN,), jnp.float32)}
    _L2_attn_in = _L2_attn_setup()

    def _L2_ffn_setup():
        import jax, jax.numpy as jnp
        import numpy as np
        MAX_THRESHOLD = 0.125
        key = jax.random.key(seed)
        ks = jax.random.split(key, 5)
        B, S, D, FF, E = (2, 256, 128, 512, 8)
        sd = 1.0 / np.sqrt(D)
        sf = 1.0 / np.sqrt(FF)
        return {'inputs': jax.random.normal(ks[0], (B, S, D), dtype=jnp.float32), 'Wg': jax.random.normal(ks[1], (D, E), dtype=jnp.float32) * sd, 'bg': jnp.zeros((E,), dtype=jnp.float32), 'Wt': jax.random.normal(ks[2], (D, 1), dtype=jnp.float32) * sd, 'bt': jnp.zeros((1,), dtype=jnp.float32), 'W1': jax.random.normal(ks[3], (E, D, FF), dtype=jnp.float32) * sd, 'b1': jnp.zeros((E, FF), dtype=jnp.float32), 'W2': jax.random.normal(ks[4], (E, FF, D), dtype=jnp.float32) * sf, 'b2': jnp.zeros((E, D), dtype=jnp.float32)}
    _L2_ffn_in = _L2_ffn_setup()

    def _L3_attn_setup():
        import math
        import jax, jax.numpy as jnp
        import numpy as np
        B, S, D, H = (2, 256, 128, 16)
        HD = D // H
        key = jax.random.key(seed)
        k1, k2, k3 = jax.random.split(key, 3)
        h = jax.random.normal(k1, (B, S, D), dtype=jnp.float32)
        Wqvk = jax.random.normal(k2, (D, 3 * D), dtype=jnp.float32) * (1.0 / math.sqrt(D))
        Wo = jax.random.normal(k3, (D, D), dtype=jnp.float32) * (1.0 / math.sqrt(D))
        return {'h': h, 'Wqvk': Wqvk, 'Wo': Wo}
    _L3_attn_in = _L3_attn_setup()

    def _L3_ffn_setup():
        import jax, jax.numpy as jnp
        import numpy as np
        EMBED = 128
        HEADS = 16
        HEAD_DIM = EMBED // HEADS
        NUM_EXPERTS = 8
        TOP_K = 2
        HIDDEN = (int(2 * (4 * EMBED) / 3) + 63) // 64 * 64
        SEQ = 256
        BATCH = 2
        ROPE_BASE = 10000.0
        EPS = 1e-06

        def _rope_tables(seq_len, dim):
            inv_freq = 1.0 / ROPE_BASE ** (np.arange(0, dim, 2, dtype=np.float32) / dim)
            t = np.arange(seq_len, dtype=np.float32)
            freqs = np.einsum('i,j->ij', t, inv_freq)
            emb = np.concatenate([freqs, freqs], axis=-1)
            return (jnp.asarray(np.cos(emb)), jnp.asarray(np.sin(emb)))

        def _rotate_half(x):
            x1, x2 = jnp.split(x, 2, axis=-1)
            return jnp.concatenate([-x2, x1], axis=-1)

        def _rmsnorm(x, w):
            return x * jax.lax.rsqrt(jnp.mean(x * x, axis=-1, keepdims=True) + EPS) * w

        def _attention(x, wq, wk, wv, wo):
            B, S, _ = x.shape
            q = (x @ wq).reshape(B, S, HEADS, HEAD_DIM).transpose(0, 2, 1, 3)
            k = (x @ wk).reshape(B, S, HEADS, HEAD_DIM).transpose(0, 2, 1, 3)
            v = (x @ wv).reshape(B, S, HEADS, HEAD_DIM).transpose(0, 2, 1, 3)
            cos, sin = _rope_tables(S, HEAD_DIM)
            cos = cos[None, None]
            sin = sin[None, None]
            q = q * cos + _rotate_half(q) * sin
            k = k * cos + _rotate_half(k) * sin
            scale = HEAD_DIM ** (-0.5)
            scores = jnp.einsum('bhqd,bhkd->bhqk', q, k) * scale
            causal = jnp.triu(jnp.ones((S, S), bool), k=1)
            scores = jnp.where(causal, -jnp.inf, scores)
            attn = jax.nn.softmax(scores, axis=-1)
            out = jnp.einsum('bhqk,bhkd->bhqd', attn, v)
            out = out.transpose(0, 2, 1, 3).reshape(B, S, EMBED)
            return out @ wo

        def _moe(x, w_router, wg, wu, wd):
            B, S, E = x.shape
            xf = x.reshape(-1, E)
            logits = xf @ w_router
            probs = jax.nn.softmax(logits, axis=-1)
            topw, topi = jax.lax.top_k(probs, TOP_K)
            topw = topw / jnp.sum(topw, axis=-1, keepdims=True)
            combine = jnp.sum(jax.nn.one_hot(topi, NUM_EXPERTS, dtype=xf.dtype) * topw[..., None], axis=1)
            g = jax.nn.silu(jnp.einsum('td,xdh->txh', xf, wg))
            u = jnp.einsum('td,xdh->txh', xf, wu)
            eo = jnp.einsum('txh,xhd->txd', g * u, wd)
            out = jnp.einsum('txd,tx->td', eo, combine)
            return out.reshape(B, S, E)
        key = jax.random.key(seed)
        ks = jax.random.split(key, 12)
        s = 0.02
        return {'x': jax.random.normal(ks[0], (BATCH, SEQ, EMBED), jnp.float32), 'wq': jax.random.normal(ks[1], (EMBED, EMBED), jnp.float32) * s, 'wk': jax.random.normal(ks[2], (EMBED, EMBED), jnp.float32) * s, 'wv': jax.random.normal(ks[3], (EMBED, EMBED), jnp.float32) * s, 'wo': jax.random.normal(ks[4], (EMBED, EMBED), jnp.float32) * s, 'w_router': jax.random.normal(ks[5], (EMBED, NUM_EXPERTS), jnp.float32) * s, 'wg': jax.random.normal(ks[6], (NUM_EXPERTS, EMBED, HIDDEN), jnp.float32) * s, 'wu': jax.random.normal(ks[7], (NUM_EXPERTS, EMBED, HIDDEN), jnp.float32) * s, 'wd': jax.random.normal(ks[8], (NUM_EXPERTS, HIDDEN, EMBED), jnp.float32) * s, 'g1': jnp.ones((EMBED,), jnp.float32), 'g2': jnp.ones((EMBED,), jnp.float32)}
    _L3_ffn_in = _L3_ffn_setup()
    _d = {'L0_attn_latents': _L0_attn_in['latents'], 'L0_attn_ln_gamma': _L0_attn_in['ln_gamma'], 'L0_attn_ln_beta': _L0_attn_in['ln_beta'], 'L0_attn_Wq': _L0_attn_in['Wq'], 'L0_attn_Wk': _L0_attn_in['Wk'], 'L0_attn_Wv': _L0_attn_in['Wv'], 'L0_attn_Wo': _L0_attn_in['Wo'], 'L0_ffn_wf': _L0_ffn_in['wf'], 'L0_ffn_uf': _L0_ffn_in['uf'], 'L0_ffn_bf': _L0_ffn_in['bf'], 'L0_ffn_wi': _L0_ffn_in['wi'], 'L0_ffn_ui': _L0_ffn_in['ui'], 'L0_ffn_bi': _L0_ffn_in['bi'], 'L0_ffn_wc': _L0_ffn_in['wc'], 'L0_ffn_uc': _L0_ffn_in['uc'], 'L0_ffn_bc': _L0_ffn_in['bc'], 'L0_ffn_wo': _L0_ffn_in['wo'], 'L0_ffn_uo': _L0_ffn_in['uo'], 'L0_ffn_bo': _L0_ffn_in['bo'], 'L0_ffn_in_c': _L0_ffn_in['in_c'], 'L1_attn_ln_g': _L1_attn_in['ln_g'], 'L1_attn_ln_b': _L1_attn_in['ln_b'], 'L1_attn_Wq': _L1_attn_in['Wq'], 'L1_attn_Wkv': _L1_attn_in['Wkv'], 'L1_attn_null_kv': _L1_attn_in['null_kv'], 'L1_attn_null_attn_bias': _L1_attn_in['null_attn_bias'], 'L1_attn_pb_w0': _L1_attn_in['pb_w0'], 'L1_attn_pb_b0': _L1_attn_in['pb_b0'], 'L1_attn_pb_ln0_g': _L1_attn_in['pb_ln0_g'], 'L1_attn_pb_ln0_b': _L1_attn_in['pb_ln0_b'], 'L1_attn_pb_w1': _L1_attn_in['pb_w1'], 'L1_attn_pb_b1': _L1_attn_in['pb_b1'], 'L1_attn_pb_ln1_g': _L1_attn_in['pb_ln1_g'], 'L1_attn_pb_ln1_b': _L1_attn_in['pb_ln1_b'], 'L1_attn_pb_w2': _L1_attn_in['pb_w2'], 'L1_attn_pb_b2': _L1_attn_in['pb_b2'], 'L1_attn_Wo': _L1_attn_in['Wo'], 'L1_attn_out_ln_g': _L1_attn_in['out_ln_g'], 'L1_attn_out_ln_b': _L1_attn_in['out_ln_b'], 'L1_ffn_W1': _L1_ffn_in['W1'], 'L1_ffn_b1': _L1_ffn_in['b1'], 'L1_ffn_W2': _L1_ffn_in['W2'], 'L1_ffn_b2': _L1_ffn_in['b2'], 'L2_attn_Wq': _L2_attn_in['Wq'], 'L2_attn_bq': _L2_attn_in['bq'], 'L2_attn_Wk': _L2_attn_in['Wk'], 'L2_attn_bk': _L2_attn_in['bk'], 'L2_attn_Wv': _L2_attn_in['Wv'], 'L2_attn_bv': _L2_attn_in['bv'], 'L2_attn_Wo': _L2_attn_in['Wo'], 'L2_attn_bo': _L2_attn_in['bo'], 'L2_ffn_Wg': _L2_ffn_in['Wg'], 'L2_ffn_bg': _L2_ffn_in['bg'], 'L2_ffn_Wt': _L2_ffn_in['Wt'], 'L2_ffn_bt': _L2_ffn_in['bt'], 'L2_ffn_W1': _L2_ffn_in['W1'], 'L2_ffn_b1': _L2_ffn_in['b1'], 'L2_ffn_W2': _L2_ffn_in['W2'], 'L2_ffn_b2': _L2_ffn_in['b2'], 'L3_attn_Wqvk': _L3_attn_in['Wqvk'], 'L3_attn_Wo': _L3_attn_in['Wo'], 'L3_ffn_wq': _L3_ffn_in['wq'], 'L3_ffn_wk': _L3_ffn_in['wk'], 'L3_ffn_wv': _L3_ffn_in['wv'], 'L3_ffn_wo': _L3_ffn_in['wo'], 'L3_ffn_w_router': _L3_ffn_in['w_router'], 'L3_ffn_wg': _L3_ffn_in['wg'], 'L3_ffn_wu': _L3_ffn_in['wu'], 'L3_ffn_wd': _L3_ffn_in['wd'], 'L3_ffn_g1': _L3_ffn_in['g1'], 'L3_ffn_g2': _L3_ffn_in['g2']}
    _x0 = _d['L0_attn_latents']
    _d['L0_attn_latents'] = jax.random.normal(jax.random.fold_in(jax.random.key(seed), 1), (8, 512, 128), dtype=_x0.dtype)
    del _x0
    return _d

def reference(L0_attn_latents, L0_attn_ln_gamma, L0_attn_ln_beta, L0_attn_Wq, L0_attn_Wk, L0_attn_Wv, L0_attn_Wo, L0_ffn_wf, L0_ffn_uf, L0_ffn_bf, L0_ffn_wi, L0_ffn_ui, L0_ffn_bi, L0_ffn_wc, L0_ffn_uc, L0_ffn_bc, L0_ffn_wo, L0_ffn_uo, L0_ffn_bo, L0_ffn_in_c, L1_attn_ln_g, L1_attn_ln_b, L1_attn_Wq, L1_attn_Wkv, L1_attn_null_kv, L1_attn_null_attn_bias, L1_attn_pb_w0, L1_attn_pb_b0, L1_attn_pb_ln0_g, L1_attn_pb_ln0_b, L1_attn_pb_w1, L1_attn_pb_b1, L1_attn_pb_ln1_g, L1_attn_pb_ln1_b, L1_attn_pb_w2, L1_attn_pb_b2, L1_attn_Wo, L1_attn_out_ln_g, L1_attn_out_ln_b, L1_ffn_W1, L1_ffn_b1, L1_ffn_W2, L1_ffn_b2, L2_attn_Wq, L2_attn_bq, L2_attn_Wk, L2_attn_bk, L2_attn_Wv, L2_attn_bv, L2_attn_Wo, L2_attn_bo, L2_ffn_Wg, L2_ffn_bg, L2_ffn_Wt, L2_ffn_bt, L2_ffn_W1, L2_ffn_b1, L2_ffn_W2, L2_ffn_b2, L3_attn_Wqvk, L3_attn_Wo, L3_ffn_wq, L3_ffn_wk, L3_ffn_wv, L3_ffn_wo, L3_ffn_w_router, L3_ffn_wg, L3_ffn_wu, L3_ffn_wd, L3_ffn_g1, L3_ffn_g2):

    def _L0_attn_ref(latents, ln_gamma, ln_beta, Wq, Wk, Wv, Wo):
        import jax, jax.numpy as jnp
        import numpy as np
        DIM = 128
        HEADS = 16
        DIM_HEAD = 64
        B, S = (4, 256)
        mu = jnp.mean(latents, axis=-1, keepdims=True)
        var = jnp.mean((latents - mu) ** 2, axis=-1, keepdims=True)
        x = (latents - mu) * jax.lax.rsqrt(var + 1e-05) * ln_gamma + ln_beta
        b, s, _ = x.shape
        q = (x @ Wq).reshape(b, s, HEADS, DIM_HEAD).transpose(0, 2, 1, 3)
        k = (x @ Wk).reshape(b, s, HEADS, DIM_HEAD).transpose(0, 2, 1, 3)
        v = (x @ Wv).reshape(b, s, HEADS, DIM_HEAD).transpose(0, 2, 1, 3)
        scale = 1.0 / np.sqrt(np.sqrt(DIM_HEAD))
        scores = jnp.einsum('bhqd,bhkd->bhqk', q * scale, k * scale)
        weights = jax.nn.softmax(scores.astype(jnp.float32), axis=-1).astype(scores.dtype)
        out = jnp.einsum('bhqk,bhkd->bhqd', weights, v)
        out = out.transpose(0, 2, 1, 3).reshape(b, s, HEADS * DIM_HEAD)
        return out @ Wo

    def _L0_ffn_ref(x, wf, uf, bf, wi, ui, bi, wc, uc, bc, wo, uo, bo, in_c):
        import jax, jax.numpy as jnp
        import numpy as np
        from jax import lax
        T, B, I, M, O = (32, 64, 128, 128, 128)

        def _xavier(key, shape):
            fan_out, fan_in = shape
            limit = float(np.sqrt(6.0 / (fan_in + fan_out)))
            return jax.random.uniform(key, shape, jnp.float32, -limit, limit)
        batch = x.shape[1]
        c0 = jnp.broadcast_to(in_c, (batch, in_c.shape[0]))

        def step(c, xt):
            ft = jax.nn.sigmoid(xt @ wf.T + c @ uf.T + bf)
            it = jax.nn.sigmoid(xt @ wi.T + c @ ui.T + bi)
            gt = jnp.tanh(xt @ wc.T + c @ uc.T + bc)
            c = ft * c + it * gt
            return (c, None)
        c_final, _ = lax.scan(step, c0, x)
        h = jnp.tanh(jnp.einsum('tbi,oi->tbo', x, wo) + c_final @ uo.T + bo)
        return h

    def _L1_attn_ref(x, ln_g, ln_b, Wq, Wkv, null_kv, null_attn_bias, pb_w0, pb_b0, pb_ln0_g, pb_ln0_b, pb_w1, pb_b1, pb_ln1_g, pb_ln1_b, pb_w2, pb_b2, Wo, out_ln_g, out_ln_b):
        import jax, jax.numpy as jnp
        import numpy as np
        DIM = 128
        HEADS = 16
        DIM_HEAD = 64
        INNER = HEADS * DIM_HEAD
        EPS = 1e-05

        def layernorm(x, g, b):
            mu = jnp.mean(x, axis=-1, keepdims=True)
            var = jnp.var(x, axis=-1, keepdims=True)
            return (x - mu) * jax.lax.rsqrt(var + EPS) * g + b

        def dynamic_pos_bias(n, pb_w0, pb_b0, pb_ln0_g, pb_ln0_b, pb_w1, pb_b1, pb_ln1_g, pb_ln1_b, pb_w2, pb_b2):
            pos = jnp.arange(-n + 1, n, dtype=jnp.float32)[:, None]
            h = jax.nn.silu(layernorm(pos @ pb_w0 + pb_b0, pb_ln0_g, pb_ln0_b))
            h = jax.nn.silu(layernorm(h @ pb_w1 + pb_b1, pb_ln1_g, pb_ln1_b))
            h = h @ pb_w2 + pb_b2
            i = jnp.arange(n)
            idx = i[:, None] - i[None, :] + (n - 1)
            bias = h[idx]
            return jnp.transpose(bias, (2, 0, 1))

        def attention_fwd(x, ln_g, ln_b, Wq, Wkv, null_kv, null_attn_bias, pb_w0, pb_b0, pb_ln0_g, pb_ln0_b, pb_w1, pb_b1, pb_ln1_g, pb_ln1_b, pb_w2, pb_b2, Wo, out_ln_g, out_ln_b):
            b, n, _ = x.shape
            scale = DIM_HEAD ** (-0.5)
            xn = layernorm(x, ln_g, ln_b)
            q = (xn @ Wq).reshape(b, n, HEADS, DIM_HEAD).transpose(0, 2, 1, 3) * scale
            kv = xn @ Wkv
            k, v = (kv[..., :DIM_HEAD], kv[..., DIM_HEAD:])
            nk = jnp.broadcast_to(null_kv[0], (b, 1, DIM_HEAD))
            nv = jnp.broadcast_to(null_kv[1], (b, 1, DIM_HEAD))
            k = jnp.concatenate([nk, k], axis=1)
            v = jnp.concatenate([nv, v], axis=1)
            sim = jnp.einsum('bhid,bjd->bhij', q, k)
            rel = dynamic_pos_bias(n, pb_w0, pb_b0, pb_ln0_g, pb_ln0_b, pb_w1, pb_b1, pb_ln1_g, pb_ln1_b, pb_w2, pb_b2)
            null_bias = jnp.broadcast_to(null_attn_bias[:, None, None], (HEADS, n, 1))
            attn_bias = jnp.concatenate([null_bias, rel], axis=-1)
            sim = sim + attn_bias[None]
            max_neg = -jnp.finfo(sim.dtype).max
            causal_mask = jnp.triu(jnp.ones((n, n + 1), dtype=bool), k=2)
            sim = jnp.where(causal_mask[None, None], max_neg, sim)
            attn = jax.nn.softmax(sim, axis=-1)
            out = jnp.einsum('bhij,bjd->bhid', attn, v)
            out = out.transpose(0, 2, 1, 3).reshape(b, n, INNER)
            return layernorm(out @ Wo, out_ln_g, out_ln_b)
        return attention_fwd(x, ln_g, ln_b, Wq, Wkv, null_kv, null_attn_bias, pb_w0, pb_b0, pb_ln0_g, pb_ln0_b, pb_w1, pb_b1, pb_ln1_g, pb_ln1_b, pb_w2, pb_b2, Wo, out_ln_g, out_ln_b)

    def _L1_ffn_ref(x, W1, b1, W2, b2):
        import jax, jax.numpy as jnp
        import numpy as np
        EMB = 128
        FF = 4 * EMB

        def _ternary(w):
            scale = jnp.maximum(jnp.mean(jnp.abs(w)), 1e-08)
            w_t = jnp.clip(jnp.round(w / scale), -1.0, 1.0)
            return w + jax.lax.stop_gradient(w_t - w)
        h = jnp.einsum('bsd,fd->bsf', x, _ternary(W1)) + b1
        h = jax.nn.gelu(h, approximate=False)
        out = jnp.einsum('bsf,df->bsd', h, _ternary(W2)) + b2
        return out

    def _L2_attn_ref(hidden_states, Wq, bq, Wk, bk, Wv, bv, Wo, bo):
        import jax, jax.numpy as jnp
        import numpy as np
        HIDDEN = 128
        HEADS = 16
        HEAD_DIM = HIDDEN // HEADS
        BETA = 0.9
        CLAMP = 1.0
        STATE_CAP = 10.0
        EPS = 1e-12

        def _l2norm(x):
            n = jnp.sqrt(jnp.sum(x * x, axis=-1, keepdims=True))
            return x / jnp.maximum(n, EPS)

        def _split_heads(x, B, T):
            return x.reshape(B, T, HEADS, HEAD_DIM).transpose(0, 2, 1, 3)

        def _reference_tuple_inner(hidden_states, Wq, bq, Wk, bk, Wv, bv, Wo, bo):
            B, T, _ = hidden_states.shape
            q = _split_heads(hidden_states @ Wq.T + bq, B, T)
            k = _split_heads(hidden_states @ Wk.T + bk, B, T)
            v = _split_heads(hidden_states @ Wv.T + bv, B, T)
            q = _l2norm(q)
            k = _l2norm(k)
            qT = q.transpose(2, 0, 1, 3)
            kT = k.transpose(2, 0, 1, 3)
            vT = v.transpose(2, 0, 1, 3)
            state0 = jnp.zeros((B, HEADS, HEAD_DIM, HEAD_DIM), dtype=hidden_states.dtype)

            def step(state, qkv):
                q_t, k_t, v_t = qkv
                v_old = jnp.einsum('bhd,bhde->bhe', k_t, state)
                delta = jnp.clip(v_t - v_old, -CLAMP, CLAMP)
                update = jnp.clip(BETA * k_t[..., :, None] * delta[..., None, :], -CLAMP, CLAMP)
                state = state + update
                m = jnp.max(jnp.abs(state), axis=(-2, -1), keepdims=True)
                state = jnp.where(m > STATE_CAP, state * 0.9, state)
                o = jnp.clip(jnp.einsum('bhij,bhj->bhi', state, q_t), -CLAMP, CLAMP)
                return (state, o)
            final_state, outs = jax.lax.scan(step, state0, (qT, kT, vT))
            out = outs.transpose(1, 0, 2, 3).reshape(B, T, HIDDEN)
            out = out @ Wo.T + bo
            return (out, final_state)
        return _reference_tuple_inner(hidden_states, Wq, bq, Wk, bk, Wv, bv, Wo, bo)[0]

    def _L2_ffn_ref(inputs, Wg, bg, Wt, bt, W1, b1, W2, b2):
        import jax, jax.numpy as jnp
        import numpy as np
        MAX_THRESHOLD = 0.125
        x = inputs.reshape(-1, inputs.shape[-1])
        gate = jax.nn.softmax(x @ Wg + bg, axis=-1)
        thr = jax.nn.sigmoid(x @ Wt + bt) * MAX_THRESHOLD
        adapted = gate - thr
        mask = (adapted >= 0).astype(x.dtype)
        w = adapted * mask
        s = jnp.sum(w, axis=-1, keepdims=True)
        s = jnp.where(s == 0, jnp.ones_like(s), s)
        w = w / s
        h = jax.nn.gelu(jnp.einsum('td,edf->etf', x, W1) + b1[:, None, :])
        eo = jnp.einsum('etf,efd->etd', h, W2) + b2[:, None, :]
        out = jnp.einsum('te,etd->td', w, eo)
        return out.reshape(inputs.shape)

    def _L3_attn_ref(h, Wqvk, Wo):
        import math
        import jax, jax.numpy as jnp
        import numpy as np
        B, S, D, H = (2, 256, 128, 16)
        HD = D // H
        b, s, d = h.shape
        qvk = (h @ Wqvk).reshape(b, s, 3, H, HD)
        q, v, k = (qvk[:, :, 0], qvk[:, :, 1], qvk[:, :, 2])
        scores = jnp.einsum('bshi,bthi->bsth', q, k)
        mask = jnp.where(jnp.arange(s)[None, :] > jnp.arange(s)[:, None], jnp.float32(-jnp.inf), jnp.float32(0.0))
        scores = scores + mask[None, :, :, None]
        scores = scores / math.sqrt(d)
        weights = jax.nn.softmax(scores, axis=2)
        wv = jnp.einsum('bsth,bthi->bshi', weights, v).reshape(b, s, d)
        return wv @ Wo

    def _L3_ffn_ref(x, wq, wk, wv, wo, w_router, wg, wu, wd, g1, g2):
        import jax, jax.numpy as jnp
        import numpy as np
        EMBED = 128
        HEADS = 16
        HEAD_DIM = EMBED // HEADS
        NUM_EXPERTS = 8
        TOP_K = 2
        HIDDEN = (int(2 * (4 * EMBED) / 3) + 63) // 64 * 64
        SEQ = 256
        BATCH = 2
        ROPE_BASE = 10000.0
        EPS = 1e-06

        def _rope_tables(seq_len, dim):
            inv_freq = 1.0 / ROPE_BASE ** (np.arange(0, dim, 2, dtype=np.float32) / dim)
            t = np.arange(seq_len, dtype=np.float32)
            freqs = np.einsum('i,j->ij', t, inv_freq)
            emb = np.concatenate([freqs, freqs], axis=-1)
            return (jnp.asarray(np.cos(emb)), jnp.asarray(np.sin(emb)))

        def _rotate_half(x):
            x1, x2 = jnp.split(x, 2, axis=-1)
            return jnp.concatenate([-x2, x1], axis=-1)

        def _rmsnorm(x, w):
            return x * jax.lax.rsqrt(jnp.mean(x * x, axis=-1, keepdims=True) + EPS) * w

        def _attention(x, wq, wk, wv, wo):
            B, S, _ = x.shape
            q = (x @ wq).reshape(B, S, HEADS, HEAD_DIM).transpose(0, 2, 1, 3)
            k = (x @ wk).reshape(B, S, HEADS, HEAD_DIM).transpose(0, 2, 1, 3)
            v = (x @ wv).reshape(B, S, HEADS, HEAD_DIM).transpose(0, 2, 1, 3)
            cos, sin = _rope_tables(S, HEAD_DIM)
            cos = cos[None, None]
            sin = sin[None, None]
            q = q * cos + _rotate_half(q) * sin
            k = k * cos + _rotate_half(k) * sin
            scale = HEAD_DIM ** (-0.5)
            scores = jnp.einsum('bhqd,bhkd->bhqk', q, k) * scale
            causal = jnp.triu(jnp.ones((S, S), bool), k=1)
            scores = jnp.where(causal, -jnp.inf, scores)
            attn = jax.nn.softmax(scores, axis=-1)
            out = jnp.einsum('bhqk,bhkd->bhqd', attn, v)
            out = out.transpose(0, 2, 1, 3).reshape(B, S, EMBED)
            return out @ wo

        def _moe(x, w_router, wg, wu, wd):
            B, S, E = x.shape
            xf = x.reshape(-1, E)
            logits = xf @ w_router
            probs = jax.nn.softmax(logits, axis=-1)
            topw, topi = jax.lax.top_k(probs, TOP_K)
            topw = topw / jnp.sum(topw, axis=-1, keepdims=True)
            combine = jnp.sum(jax.nn.one_hot(topi, NUM_EXPERTS, dtype=xf.dtype) * topw[..., None], axis=1)
            g = jax.nn.silu(jnp.einsum('td,xdh->txh', xf, wg))
            u = jnp.einsum('td,xdh->txh', xf, wu)
            eo = jnp.einsum('txh,xhd->txd', g * u, wd)
            out = jnp.einsum('txd,tx->td', eo, combine)
            return out.reshape(B, S, E)
        h = x + _attention(_rmsnorm(x, g1), wq, wk, wv, wo)
        y = h + _moe(_rmsnorm(h, g2), w_router, wg, wu, wd)
        return y
    x = L0_attn_latents
    xn = _layernorm(x, axis=-1)
    s = _L0_attn_ref(xn, L0_attn_ln_gamma, L0_attn_ln_beta, L0_attn_Wq, L0_attn_Wk, L0_attn_Wv, L0_attn_Wo)
    g = _silu(_L0_ffn_ref(xn, L0_ffn_wf, L0_ffn_uf, L0_ffn_bf, L0_ffn_wi, L0_ffn_ui, L0_ffn_bi, L0_ffn_wc, L0_ffn_uc, L0_ffn_bc, L0_ffn_wo, L0_ffn_uo, L0_ffn_bo, L0_ffn_in_c))
    x = x + s * g
    xn = _layernorm(x, axis=-1)
    s = _L1_attn_ref(xn, L1_attn_ln_g, L1_attn_ln_b, L1_attn_Wq, L1_attn_Wkv, L1_attn_null_kv, L1_attn_null_attn_bias, L1_attn_pb_w0, L1_attn_pb_b0, L1_attn_pb_ln0_g, L1_attn_pb_ln0_b, L1_attn_pb_w1, L1_attn_pb_b1, L1_attn_pb_ln1_g, L1_attn_pb_ln1_b, L1_attn_pb_w2, L1_attn_pb_b2, L1_attn_Wo, L1_attn_out_ln_g, L1_attn_out_ln_b)
    g = _silu(_L1_ffn_ref(xn, L1_ffn_W1, L1_ffn_b1, L1_ffn_W2, L1_ffn_b2))
    x = x + s * g
    xn = _layernorm(x, axis=-1)
    s = _L2_attn_ref(xn, L2_attn_Wq, L2_attn_bq, L2_attn_Wk, L2_attn_bk, L2_attn_Wv, L2_attn_bv, L2_attn_Wo, L2_attn_bo)
    g = _silu(_L2_ffn_ref(xn, L2_ffn_Wg, L2_ffn_bg, L2_ffn_Wt, L2_ffn_bt, L2_ffn_W1, L2_ffn_b1, L2_ffn_W2, L2_ffn_b2))
    x = x + s * g
    xn = _layernorm(x, axis=-1)
    s = _L3_attn_ref(xn, L3_attn_Wqvk, L3_attn_Wo)
    g = _silu(_L3_ffn_ref(xn, L3_ffn_wq, L3_ffn_wk, L3_ffn_wv, L3_ffn_wo, L3_ffn_w_router, L3_ffn_wg, L3_ffn_wu, L3_ffn_wd, L3_ffn_g1, L3_ffn_g2))
    x = x + s * g
    return x

_drawn_inputs = setup_inputs


def setup_inputs(seed=0):
    import zlib

    import numpy as np

    out = dict(_drawn_inputs(seed))
    spreads = {'L0_attn_ln_gamma': (1.0, 0.2),
     'L0_attn_ln_beta': (0.0, 0.1),
     'L0_ffn_bf': (0.0, 0.8),
     'L0_ffn_bi': (0.0, 0.8),
     'L0_ffn_bc': (0.0, 0.1),
     'L0_ffn_bo': (0.0, 0.1),
     'L0_ffn_in_c': (0.0, 0.8),
     'L1_attn_ln_g': (1.0, 0.2),
     'L1_attn_ln_b': (0.0, 0.1),
     'L1_attn_pb_b0': (0.0, 0.435),
     'L1_attn_pb_ln0_g': (1.0, 0.6),
     'L1_attn_pb_ln0_b': (0.0, 0.592),
     'L1_attn_pb_b1': (0.0, 0.288),
     'L1_attn_pb_ln1_g': (1.0, 0.6),
     'L1_attn_pb_ln1_b': (0.0, 0.8),
     'L1_attn_pb_b2': (0.0, 0.1),
     'L1_attn_out_ln_g': (1.0, 0.2),
     'L1_attn_out_ln_b': (0.0, 0.1),
     'L2_attn_bq': (0.0, 0.8),
     'L2_attn_bk': (0.0, 0.8),
     'L2_attn_bv': (0.0, 0.8),
     'L2_attn_bo': (0.0, 0.8),
     'L2_ffn_bg': (0.0, 0.8),
     'L2_ffn_b1': (0.0, 0.8),
     'L2_ffn_b2': (0.0, 0.8),
     'L3_ffn_g1': (1.0, 0.6),
     'L3_ffn_g2': (1.0, 0.6)}
    factors = {'L0_ffn_uf': 3.657,
     'L0_ffn_ui': 3.383,
     'L1_ffn_b1': 8.0,
     'L1_ffn_b2': 8.0,
     'L2_attn_Wq': 8.0,
     'L2_attn_Wk': 8.0,
     'L2_attn_Wv': 8.0,
     'L2_attn_Wo': 8.0,
     'L2_ffn_Wg': 8.0,
     'L2_ffn_Wt': 8.0,
     'L2_ffn_W1': 8.0,
     'L2_ffn_W2': 8.0,
     'L3_attn_Wqvk': 8.0,
     'L3_attn_Wo': 8.0,
     'L3_ffn_wq': 8.0,
     'L3_ffn_wk': 8.0,
     'L3_ffn_wv': 8.0,
     'L3_ffn_wo': 8.0,
     'L3_ffn_w_router': 8.0,
     'L3_ffn_wg': 8.0,
     'L3_ffn_wu': 8.0,
     'L3_ffn_wd': 8.0}
    for name, (base, spread) in spreads.items():
        noise = np.random.default_rng([zlib.crc32(name.encode()), seed]).standard_normal(out[name].shape)
        drawn = base * np.exp(spread * noise) if base else spread * noise
        out[name] = jnp.asarray(drawn.astype(out[name].dtype))
    for name, factor in factors.items():
        out[name] = (out[name] * factor).astype(out[name].dtype)
    return out
```

```python
from contextlib import ExitStack

import numpy as np

import concourse.bass as bass
from concourse import mybir

F32 = mybir.dt.float32
BF16 = mybir.dt.bfloat16
F32R = mybir.dt.float32r
I32 = mybir.dt.int32
UPPER = -4096
ALU = mybir.AluOpType
ACT = mybir.ActivationFunctionType
AX = mybir.AxisListType.X

P = 128
NB, S, D = 8, 512, 128
QB = S // P
TB = NB * QB
H = 16
DH = 64
DN = D // H
FF = 512
E = 8
PACK = 4 * DN
HID = 384
LN_EPS = 1e-5
RMS_EPS = 1e-6
FIRST_SEM = 120
MASKED = 1e30
NPOS = 640


class Stage:

    def __init__(self, nc, ctx, name):
        self.nc, self.ctx, self.name, self.nums = nc, ctx, name, []

    def sems(self, *names):
        handles = []
        for n in names:
            num = FIRST_SEM + len(self.nums)
            handles.append(self.ctx.enter_context(self.nc.semaphore(f"{self.name}_{n}", num=num)))
            self.nums.append(num)
        return handles

    def sb(self, name, shape, dt=F32):
        return self.ctx.enter_context(self.nc.sbuf_tensor(f"{self.name}_{name}", shape, dt))

    def end(self):
        self.nc.all_engine_barrier(sems_to_clear=range(self.nums[0], self.nums[-1] + 1))


class Chain:

    def __init__(self, eng, sem):
        self.eng, self.sem, self.n = eng, sem, 0

    def mark(self, ins):
        ins.then_inc(self.sem, 1)
        self.n += 1

    def wait(self):
        self.eng.wait_ge(self.sem, self.n)

    def link(self, ins):
        self.mark(ins)
        self.wait()


def row_bcast(ap, n, parts=P):
    return bass.AP(tensor=ap.tensor, offset=ap.offset, ap=[[0, parts], [1, n]])


def column(ap):
    return ap.rearrange("(p o) -> p o", o=1)


def over_tokens(stat, n=D):
    return stat.broadcast_to([P, stat.shape[1], n])


def over_blocks(row, n=TB):
    return row.unsqueeze(1).broadcast_to([P, n, row.shape[1]])


def load_all(st, loaded, pairs, clear=()):
    nc = st.nc
    with nc.Block() as block:
        @block.sync
        def _(sp):
            for dst, src in pairs:
                sp.dma_start(dst, src).then_inc(loaded, 16)
            sp.wait_ge(loaded, 16 * len(pairs))

        if clear:
            @block.vector
            def _(dve):
                for part, zeroed in clear:
                    nc.vector.memset(part, 0.0).then_inc(zeroed, 1)
    st.end()


def make_constants(nc, c):
    with ExitStack() as ctx:
        st = Stage(nc, ctx, "const")
        filled, shaped, narrowed = st.sems("filled", "shaped", "narrowed")
        mask = st.sb("mask", [P, P])
        with nc.Block() as block:
            @block.gpsimd
            def _(pool):
                nc.gpsimd.memset(c.ident[:], 0.0).then_inc(filled, 1)
                nc.gpsimd.memset(mask[:], 0.0).then_inc(filled, 1)
                nc.gpsimd.memset(c.ones[:], 1.0).then_inc(filled, 1)
                pool.wait_ge(filled, 3)
                nc.gpsimd.affine_select(out=c.ident[:], in_=c.ident[:], compare_op=ALU.not_equal, fill=1.0,
                                        base=0, pattern=[[-1, P]], channel_multiplier=1).then_inc(shaped, 1)
                nc.gpsimd.affine_select(out=mask[:], in_=mask[:], compare_op=ALU.is_ge, fill=-MASKED,
                                        base=0, pattern=[[-1, P]], channel_multiplier=1).then_inc(shaped, 1)

            @block.vector
            def _(dve):
                dve.wait_ge(shaped, 2)
                nc.vector.tensor_copy(c.ident16[:], c.ident[:]).then_inc(narrowed, 1)
                nc.vector.tensor_copy(c.mask16[:], mask[:]).then_inc(narrowed, 1)
        st.end()


def layer_norm(nc, dve, chain, src, dst, stats, mv, rstd, var_ready, root_ready, eps, count):
    for t in range(TB):
        chain.mark(nc.vector.bn_stats(stats[:, t, :], src[:, t, :]))
    chain.wait()
    for t in range(TB):
        chain.mark(nc.vector.bn_aggr(mv[:, t, :], stats[:, t, :]))
    chain.wait()
    nc.vector.tensor_scalar(rstd[:], mv[:, :, 1:2], eps, None, ALU.add).then_inc(var_ready, 1)
    dve.wait_ge(root_ready, count)
    chain.link(nc.vector.reciprocal(rstd[:], rstd[:]))
    for t in range(TB):
        chain.mark(nc.vector.tensor_scalar(dst[:, t, :], src[:, t, :], mv[:, t, 0:1], rstd[:, t, :],
                                           ALU.subtract, ALU.mult))
    chain.wait()


def root_of(nc, act, rstd, var_ready, root_ready, count):
    act.wait_ge(var_ready, count)
    nc.scalar.activation(rstd[:], rstd[:], ACT.Sqrt).then_inc(root_ready, 1)


def norm_stage(nc, c, name, combine, affine_s=None, second=None):
    with ExitStack() as ctx:
        st = Stage(nc, ctx, name)
        var_ready, root_ready, dve_done, normed, turned, copied, loaded = st.sems(
            "var_ready", "root_ready", "dve_done", "normed", "turned", "copied", "loaded")
        stats = st.sb("stats", [P, TB, 6])
        mv = st.sb("mv", [P, TB, 2])
        rstd = st.sb("rstd", [P, TB, 1])
        again = st.sb("again", [P, TB, D]) if second else None
        norms = int(affine_s is not None) + 1 + int(second is not None)
        sides = 1 + int(second is not None)
        rows = []
        if affine_s is not None:
            rows = [(st.sb("s_gain", [P, D]), row_bcast(affine_s[0], D)),
                    (st.sb("s_shift", [P, D]), row_bcast(affine_s[1], D))]
        if second is not None:
            rows += [(st.sb("a_gain", [P, 1]), column(second[0])), (st.sb("a_shift", [P, 1]), column(second[1]))]
        with nc.Block() as block:
            @block.sync
            def _(sp):
                for dst, src in rows:
                    sp.dma_start(dst[:], src).then_inc(loaded, 16)

            @block.vector
            def _(dve):
                chain = Chain(dve, dve_done)
                k = 0
                if affine_s is not None:
                    k += 1
                    layer_norm(nc, dve, chain, c.s, c.s, stats, mv, rstd, var_ready, root_ready, LN_EPS, k)
                    dve.wait_ge(loaded, 16 * len(rows))
                    chain.link(nc.vector.tensor_tensor(c.s[:], c.s[:], over_blocks(rows[0][0][:]), ALU.mult))
                    chain.link(nc.vector.tensor_tensor(c.s[:], c.s[:], over_blocks(rows[1][0][:]), ALU.add))
                if combine:
                    chain.link(nc.vector.tensor_tensor(c.g[:], c.s[:], c.g[:], ALU.mult))
                    chain.link(nc.vector.tensor_tensor(c.x[:], c.x[:], c.g[:], ALU.add))
                k += 1
                layer_norm(nc, dve, chain, c.x, c.xn, stats, mv, rstd, var_ready, root_ready, LN_EPS, k)
                nc.vector.tensor_copy(mv[:, 0, 0:1], mv[:, 0, 0:1]).then_inc(normed, 1)
                if second is not None:
                    chain.link(nc.vector.tensor_copy(mv[:, 0, 1:2], mv[:, 0, 1:2]))
                    k += 1
                    layer_norm(nc, dve, chain, c.xn, again, stats, mv, rstd, var_ready, root_ready, LN_EPS, k)
                    nc.vector.tensor_copy(mv[:, 0, 0:1], mv[:, 0, 0:1]).then_inc(normed, 1)

            @block.tensor
            def _(pe):
                for side in range(sides):
                    pe.wait_ge(normed, side + 1)
                    src = (c.xn, again)[side]
                    for b in range(NB):
                        n = side * NB + b
                        if n >= 4:
                            pe.wait_ge(copied, n - 3)
                        for q in range(QB):
                            last = nc.tensor.transpose(c.ps[n % 4][:, q * P:(q + 1) * P],
                                                       src[:, b * QB + q, :], c.ident[:])
                        last.then_inc(turned, 1)

            @block.scalar
            def _(act):
                for k in range(norms - sides + 1):
                    root_of(nc, act, rstd, var_ready, root_ready, k + 1)
                if second is not None:
                    root_of(nc, act, rstd, var_ready, root_ready, norms)
                    act.wait_ge(loaded, 16 * len(rows))
                for side in range(sides):
                    for b in range(NB):
                        n = side * NB + b
                        act.wait_ge(turned, n + 1)
                        if side == 0:
                            nc.scalar.activation(c.xnT[:, b, :], c.ps[n % 4][:], ACT.Copy).then_inc(copied, 1)
                        else:
                            nc.scalar.activation(c.xaT[:, b, :], c.ps[n % 4][:], ACT.Identity,
                                                 bias=rows[-1][0][:], scale=rows[-2][0][:]).then_inc(copied, 1)
        st.end()


def final_stage(nc, c, out):
    with ExitStack() as ctx:
        st = Stage(nc, ctx, "final")
        product, ready, stored = st.sems("product", "ready", "stored")
        with nc.Block() as block:
            @block.vector
            def _(dve):
                for b in range(NB):
                    g, s, x = (t[:, b * QB:(b + 1) * QB, :] for t in (c.g, c.s, c.x))
                    nc.vector.tensor_tensor(g, s, g, ALU.mult).then_inc(product, 1)
                    dve.wait_ge(product, b + 1)
                    nc.vector.tensor_tensor(x, x, g, ALU.add).then_inc(ready, 1)

            @block.sync
            def _(sp):
                for b in range(NB):
                    sp.wait_ge(ready, b + 1)
                    sp.dma_start(out[b].rearrange("(q p) d -> p q d", p=P),
                                 c.x[:, b * QB:(b + 1) * QB, :]).then_inc(stored, 16)
                sp.wait_ge(stored, 16 * NB)
        st.end()


def recurrent_gate(nc, c, w):
    with ExitStack() as ctx:
        st = Stage(nc, ctx, "g0")
        loaded, xpart, cpart, gated, dve_done, cready, cu_ready, cu_added, h_ready, h_added, tanhed = st.sems(
            "loaded", "xpart", "cpart", "gated", "dve_done", "cready", "cu_ready", "cu_added", "h_ready", "h_added",
            "tanhed")
        names = ["wf", "uf", "wi", "ui", "wc", "uc", "wo", "uo"]
        wt = {n: st.sb(n, [P, D]) for n in names}
        bias = {n: st.sb(n, [P, 1]) for n in ("bf", "bi", "bc")}
        bo_row = st.sb("bo_row", [P, D])
        c_first = st.sb("c_first", [P, 1])
        cT = st.sb("cT", [P, 2, S])
        gate = st.sb("gate", [P, 2, 3, S])
        keep = st.sb("keep", [P, S])
        cu = st.sb("cu", [P, QB, D])
        n_loads = len(names) + 3 + 2

        with nc.Block() as block:
            @block.sync
            def _(sp):
                for n in names:
                    sp.dma_start(wt[n][:], w[f"L0_ffn_{n}T"]).then_inc(loaded, 16)
                for n in bias:
                    sp.dma_start(bias[n][:], column(w[f"L0_ffn_{n}"])).then_inc(loaded, 16)
                sp.dma_start(c_first[:], column(w["L0_ffn_in_c"])).then_inc(loaded, 16)
                sp.dma_start(bo_row[:], row_bcast(w["L0_ffn_bo"], D)).then_inc(loaded, 16)

            @block.tensor
            def _(pe):
                pe.wait_ge(loaded, 16 * n_loads)
                for t in range(NB):
                    if t >= 2:
                        pe.wait_ge(gated, 3 * (t - 1))
                    pe.wait_ge(cready, t + 1)
                    for k, n in enumerate("fic"):
                        bank = c.ps[3 * (t % 2) + k]
                        nc.tensor.matmul(bank[:], wt["w" + n][:], c.xnT[:, t, :], start=True, stop=False)
                        nc.tensor.matmul(bank[:], wt["u" + n][:], cT[:, t % 2, :], start=False,
                                         stop=True).then_inc(cpart, 1)
                pe.wait_ge(cready, NB + 1)
                for q in range(QB):
                    last = nc.tensor.matmul(c.ps[6][:, q * P:(q + 1) * P], cT[:, NB % 2, q * P:(q + 1) * P],
                                            wt["uo"][:], start=True, stop=True)
                last.then_inc(cu_ready, 1)
                for b in range(NB):
                    if b == 0:
                        pe.wait_ge(gated, 3 * NB)
                    if b >= 4:
                        pe.wait_ge(h_added, b - 3)
                    for q in range(QB):
                        last = nc.tensor.matmul(c.ps[b % 4][:, q * P:(q + 1) * P], c.xnT[:, b, q * P:(q + 1) * P],
                                                wt["wo"][:], start=True, stop=True)
                    last.then_inc(h_ready, 1)

            @block.scalar
            def _(act):
                act.wait_ge(loaded, 16 * n_loads)
                for t in range(NB):
                    for k, n in enumerate("fic"):
                        act.wait_ge(cpart, 3 * t + k + 1)
                        if t >= 2 and k == 0:
                            act.wait_ge(cready, t)
                        nc.scalar.activation(gate[:, t % 2, k, :], c.ps[3 * (t % 2) + k][:],
                                             ACT.Tanh if n == "c" else ACT.Sigmoid,
                                             bias=bias["b" + n][:]).then_inc(gated, 1)
                for b in range(NB):
                    act.wait_ge(h_added, b + 1)
                    g = c.g[:, b * QB:(b + 1) * QB, :]
                    nc.scalar.activation(g, g, ACT.Tanh).then_inc(tanhed, 1)
                act.wait_ge(tanhed, NB)
                nc.scalar.activation(c.g[:], c.g[:], ACT.Silu).then_inc(tanhed, 1)

            @block.vector
            def _(dve):
                chain = Chain(dve, dve_done)
                dve.wait_ge(loaded, 16 * n_loads)
                chain.link(nc.vector.memset(keep[:], 0.0))
                nc.vector.tensor_scalar(cT[:, 0, :], keep[:], c_first[:], None, ALU.add).then_inc(cready, 1)
                for t in range(NB):
                    f, i, g = (gate[:, t % 2, k, :] for k in range(3))
                    dve.wait_ge(gated, 3 * t + 1)
                    dve.wait_ge(cready, t + 1)
                    chain.mark(nc.vector.tensor_tensor(keep[:], f, cT[:, t % 2, :], ALU.mult))
                    dve.wait_ge(gated, 3 * t + 3)
                    chain.link(nc.vector.tensor_tensor(i, i, g, ALU.mult))
                    nc.vector.tensor_tensor(cT[:, (t + 1) % 2, :], keep[:], i, ALU.add).then_inc(cready, 1)
                dve.wait_ge(cu_ready, 1)
                nc.vector.tensor_tensor(cu[:], c.ps[6][:].rearrange("p (q d) -> p q d", d=D),
                                        over_blocks(bo_row[:], QB), ALU.add).then_inc(cu_added, 1)
                dve.wait_ge(cu_added, 1)
                for b in range(NB):
                    dve.wait_ge(h_ready, b + 1)
                    nc.vector.tensor_tensor(c.g[:, b * QB:(b + 1) * QB, :],
                                            c.ps[b % 4][:].rearrange("p (q d) -> p q d", d=D), cu[:],
                                            ALU.add).then_inc(h_added, 1)
        st.end()


UNITS = QB * H
GROUP = 4
LAG_T, LAG_AV = 2, 3
S_BANKS, T_BANK, O_BANK, Y_BANK = 3, 3, 5, 7


class Heads:

    def __init__(self, name, width, causal, bias=None, shared_kv=False, projected=False, dst=None):
        self.name, self.width, self.causal = name, width, causal
        self.bias = bias
        self.shared_kv = shared_kv
        self.projected = projected
        self.dst = dst
        self.inner = H * width
        self.tiles = self.inner // P
        self.rounds = max(1, self.tiles // 4)
        self.batches = 1 if projected else 2

    def keys(self, n):
        return n % UNITS // H + 1 if self.causal else QB

    def events(self):
        out = {}
        for block in range(self.batches * QB):
            done = H * (block + 1) + LAG_AV
            for r in range(self.rounds + 1):
                out[done + 2 + 2 * r] = (block, r)
        return out

    def scores(self, k, n):
        batch, (qb, h) = n // UNITS, divmod(n % UNITS, H)
        queries, keys = slice(qb * P, (qb + 1) * P), slice(0, self.keys(n) * P)
        if not self.projected:
            rows = slice(PACK * (h % 4), PACK * (h % 4 + 1))
            return k.QT[batch][rows, h // 4, queries].bitcast(F32R), k.KT[batch][rows, h // 4, keys].bitcast(F32R)
        return k.QT[:, h // 2, queries], k.KT[h % 2][:, 0 if self.shared_kv else h // 2, keys]

    def values(self, k, n, block):
        h = n % H
        if not self.projected:
            return k.V[n // UNITS][:, block, :]
        return k.V[:, block, :] if self.shared_kv else k.V[:, block, h // 2 * P:(h // 2 + 1) * P]

    def outputs(self, bank, group):
        if not self.projected:
            offset, step = group % (H // GROUP) * GROUP * self.width, P + self.width
        else:
            offset, step = 0, P
        odd = P + DH if self.projected and not self.shared_kv else step
        return bass.AP(tensor=bank[:].tensor, offset=offset, ap=[[512, P], [2 * step, 2], [odd, 2], [1, self.width]])


def attention_stage(nc, c, a, b, w, load_qkv=None, tag=""):
    R = a.rounds + 1
    units, groups = a.batches * UNITS, a.batches * UNITS // GROUP
    steps = units + LAG_AV + 3 + 2 * R
    events = a.events()
    with ExitStack() as ctx:
        st = Stage(nc, ctx, a.name + "u")
        (x_ready, loaded, projected, act_copied, dve_copied, scored, maxed, exped, turned, pt_ready, av_done,
         dve_done, o_ready, y_made, y_copied) = st.sems(
            "x_ready", "loaded", "projected", "act_copied", "dve_copied", "scored", "maxed", "exped", "turned",
            "pt_ready", "av_done", "dve_done", "o_ready", "y_made", "y_copied")
        if load_qkv is not None:
            (loaded_next,) = st.sems("loaded_next")
        if a.shared_kv:
            null_scored, null_gap, null_exped, null_spread = st.sems(
                "null_scored", "null_gap", "null_exped", "null_spread")
        QT, KT, V, probs, PT, sums, top, O, OT, rinv = w.QT, w.KT, w.V, w.probs, w.PT, w.sums, w.top, w.O, w.OT, w.rinv

        jobs = []
        if a.projected:
            jobs = [("q", t) for t in range(a.tiles)]
            if a.shared_kv:
                jobs += [("k1", 0), ("v1", 0)]
            else:
                jobs += [("k", t) for t in range(a.tiles)]
                jobs += [("v", t) for t in range(2 * QB)]
        bank_of = (0, 1, 2, Y_BANK)

        def copied_before(eng, j):
            if j > 0:
                eng.wait_ge(act_copied, (j + 1) // 2)
            if j > 1:
                eng.wait_ge(dve_copied, j // 2)

        def copies(kind, t, j):
            bank = c.ps[bank_of[j % 4]]
            if kind == "q":
                return [(QT[:, t, :], bank[:])]
            if kind in ("k", "k1"):
                return [(KT[i][DH * i:DH * (i + 1), t, :], bank[DH * i:DH * (i + 1), :]) for i in range(2)]
            if kind == "v1":
                return [(V[:].rearrange("p q d -> p (q d)"), bank[:])]
            return [(V[:, t // 2, (t % 2) * 512:(t % 2 + 1) * 512], bank[:])]

        with nc.Block(no_gpsimd_drain=True) as block:
            if load_qkv is not None:
                @block.sync
                def _(sp):
                    load_qkv(sp, b + 1, 1, loaded)
                    sp.wait_ge(scored, UNITS)
                    load_qkv(sp, b + 2, 0, loaded_next)
                    sp.wait_ge(loaded_next, 16 * w.n_loads)

            @block.gpsimd
            def _(pool):
                if a.projected:
                    nc.gpsimd.tensor_copy(w.xT[:], w.source[:, b, :]).then_inc(x_ready, 1)
                else:
                    for i in range(a.batches):
                        nc.gpsimd.tensor_copy(V[i][:], w.source[:, bass.ts(b + i, QB), :]).then_inc(x_ready, 1)
                if a.shared_kv:
                    for hf in range(groups):
                        pool.wait_ge(null_exped, hf + 1)
                        if hf >= 2:
                            pool.wait_ge(o_ready, hf - 1)
                        nc.gpsimd.tensor_tensor(
                            w.null_part[:, hf % 2, :, :],
                            w.null_weight[:, hf % 2, :].unsqueeze(2).broadcast_to([P, GROUP, DH]),
                            w.null_v[:].unsqueeze(1).broadcast_to([P, GROUP, DH]), ALU.mult).then_inc(null_spread, 1)

            @block.tensor
            def _(pe):
                if a.projected:
                    pe.wait_ge(x_ready, 1)
                for j, (kind, t) in enumerate(jobs):
                    if j >= 4:
                        copied_before(pe, j - 3)
                    bank = c.ps[bank_of[j % 4]]
                    if kind == "q":
                        last = nc.tensor.matmul(bank[:], w.wq[:, t * P:(t + 1) * P], w.xT[:], start=True, stop=True)
                    elif kind in ("k", "k1"):
                        last = nc.tensor.matmul(bank[:], w.wk[:, t * P:(t + 1) * P], w.xT[:], start=True, stop=True)
                    elif kind == "v":
                        q, half = t // 2, t % 2
                        last = nc.tensor.matmul(bank[:], w.xT[:, q * P:(q + 1) * P],
                                                w.wv[:, half * 512:(half + 1) * 512], start=True, stop=True)
                    else:
                        for q in range(QB):
                            last = nc.tensor.matmul(bank[:, q * P:(q + 1) * P], w.xT[:, q * P:(q + 1) * P],
                                                    w.wv[:], start=True, stop=True)
                    last.then_inc(projected, 1)
                copied_before(pe, len(jobs))
                if a.shared_kv:
                    for q in range(QB):
                        for t in range(a.tiles):
                            last = nc.tensor.matmul(c.ps[Y_BANK][:, q * H + 2 * t:q * H + 2 * t + 2],
                                                    QT[:, t, q * P:(q + 1) * P], w.null_k[:], start=True, stop=True)
                    last.then_inc(null_scored, 1)

                for n in range(steps):
                    if n < units:
                        if load_qkv is not None and n == UNITS:
                            pe.wait_ge(loaded, 16 * w.n_loads)
                        qb = n % UNITS // H
                        queries, keys = a.scores(w, n)
                        bank = c.ps[n % S_BANKS]
                        if n >= S_BANKS:
                            pe.wait_ge(maxed if a.bias is not None else exped, n - S_BANKS + 1)
                        last = nc.tensor.matmul(bank[:, 0:a.keys(n) * P], queries, keys, start=True,
                                                stop=not a.causal or a.bias is not None)
                        if a.causal and a.bias is None:
                            last = nc.tensor.matmul(bank[:, qb * P:(qb + 1) * P], c.ident16[:], c.mask16[:],
                                                    start=False, stop=True)
                        last.then_inc(scored, 1)
                    m = n - LAG_T
                    if 0 <= m < units:
                        pe.wait_ge(exped, m + 1)
                        if m >= 2:
                            pe.wait_ge(pt_ready, m - 1)
                        for k in range(a.keys(m)):
                            last = nc.tensor.transpose(c.ps[T_BANK + m % 2][:, k * P:(k + 1) * P],
                                                       probs[:, m % 3, k * P:(k + 1) * P], c.ident[:])
                        last.then_inc(turned, 1)
                    m = n - LAG_AV
                    if 0 <= m < units:
                        hf = m // GROUP
                        if not a.projected and m % UNITS == 0:
                            pe.wait_ge(x_ready, m // UNITS + 1)
                        pe.wait_ge(pt_ready, m + 1)
                        if m % GROUP == 0 and hf >= 2:
                            pe.wait_ge(o_ready, hf - 1)
                        for k in range(a.keys(m)):
                            last = nc.tensor.matmul(
                                c.ps[O_BANK + hf % 2][:, (m % GROUP) * P:(m % GROUP + 1) * P],
                                PT[:, m % 2, k * P:(k + 1) * P], a.values(w, m, k), start=k == 0, stop=k == a.keys(m) - 1)
                        last.then_inc(av_done, 1)
                    if n in events:
                        qb, r = events[n]
                        if qb == 0 and r == 0 and a.shared_kv:
                            pe.wait_ge(null_gap, 1)
                        if R * qb + r > 0:
                            pe.wait_ge(y_copied, R * qb + r)
                        y = c.ps[Y_BANK]
                        if r < a.rounds:
                            pe.wait_ge(o_ready, H // GROUP * (qb + 1))
                            count = min(4, a.tiles)
                            for k in range(count):
                                t = 4 * r + k
                                last = nc.tensor.transpose(y[:, k * P:(k + 1) * P], O[:, qb % 2, t * P:(t + 1) * P],
                                                           c.ident[:])
                        else:
                            for t in range(a.tiles):
                                last = nc.tensor.matmul(y[:, 0:D], OT[:, t, :], w.wo[:, t, :],
                                                        start=t == 0, stop=t == a.tiles - 1)
                        last.then_inc(y_made, 1)

            @block.scalar
            def _(act):
                for j in range(0, len(jobs), 2):
                    kind, t = jobs[j]
                    act.wait_ge(projected, j + 1)
                    for dst, src in copies(kind, t, j):
                        last = nc.scalar.activation(dst, src, ACT.Copy, scale=w.q_scale if kind == "q" else 1.0)
                    last.then_inc(act_copied, 1)
                for n in range(steps + 1):
                    if n < units:
                        width = a.keys(n) * P
                        act.wait_ge(maxed, n + 1)
                        if n >= 3:
                            act.wait_ge(turned, n - 2)
                        src = w.biased[:, n % 3, 0:width] if a.bias is not None else c.ps[n % S_BANKS][:, 0:width]
                        nc.scalar.activation(probs[:, n % 3, 0:width], src, ACT.Exp, bias=top[:, n:n + 1],
                                             scale=-1.0 if a.bias is not None else 1.0,
                                             accum_out=sums[:, n:n + 1]).then_inc(exped, 1)
                    if a.shared_kv and n % GROUP == 2 and n >= GROUP:
                        hf = n // GROUP - 1
                        if hf < groups:
                            act.wait_ge(null_gap, hf + 2)
                            if hf >= 2:
                                act.wait_ge(o_ready, hf - 1)
                            nc.scalar.activation(w.null_weight[:, hf % 2, :], w.null_less[:, hf, :],
                                                 ACT.Exp).then_inc(null_exped, 1)
                    if n - 1 in events:
                        qb, r = events[n - 1]
                        act.wait_ge(y_made, R * qb + r + 1)
                        y = c.ps[Y_BANK]
                        if r < a.rounds:
                            count = min(4, a.tiles)
                            nc.scalar.activation(OT[:, 4 * r:4 * r + count, :].rearrange("p t q -> p (t q)"),
                                                 y[:, 0:count * P], ACT.Copy).then_inc(y_copied, 1)
                        else:
                            nc.scalar.activation(a.dst[:, b * QB + qb, :], y[:, 0:D], ACT.Copy).then_inc(y_copied, 1)

            @block.vector
            def _(dve):
                chain = Chain(dve, dve_done)
                for j in range(1, len(jobs), 2):
                    kind, t = jobs[j]
                    dve.wait_ge(projected, j + 1)
                    for dst, src in copies(kind, t, j):
                        last = nc.vector.tensor_scalar(dst, src, w.q_scale if kind == "q" else 1.0, None, ALU.mult)
                    last.then_inc(dve_copied, 1)
                if a.shared_kv:
                    dve.wait_ge(null_scored, 1)
                    nc.vector.tensor_tensor(w.null_s[:], c.ps[Y_BANK][:, 0:UNITS], w.null_bias[:],
                                            ALU.add).then_inc(null_gap, 1)
                    dve.wait_ge(null_gap, 1)
                for n in range(steps + 1):
                    if n < units:
                        h = n % H
                        width = a.keys(n) * P
                        dve.wait_ge(scored, n + 1)
                        if a.bias is not None:
                            if n >= 3:
                                dve.wait_ge(exped, n - 2)
                            nc.vector.tensor_tensor_reduce(
                                out=w.biased[:, n % 3, 0:width], in0=c.ps[n % S_BANKS][:, 0:width],
                                in1=a.bias[:, h, S - width:S], scale=1.0, scalar=w.null_s[:, n:n + 1],
                                op0=ALU.add, op1=ALU.min, accum_out=top[:, n:n + 1]).then_inc(maxed, 1)
                        else:
                            nc.vector.tensor_reduce(top[:, n:n + 1], c.ps[n % S_BANKS][:, 0:width], AX, ALU.max,
                                                    negate=True).then_inc(maxed, 1)
                    m = n - LAG_T
                    if 0 <= m < units:
                        width = a.keys(m) * P
                        dve.wait_ge(turned, m + 1)
                        if m >= 2:
                            dve.wait_ge(av_done, m - 1)
                        nc.vector.tensor_copy(PT[:, m % 2, 0:width],
                                              c.ps[T_BANK + m % 2][:, 0:width]).then_inc(pt_ready, 1)
                    if a.shared_kv and n % GROUP == 1 and n >= GROUP and n // GROUP - 1 < groups:
                        hf = n // GROUP - 1
                        dve.wait_ge(maxed, GROUP * (hf + 1))
                        nc.vector.tensor_tensor(w.null_less[:, hf, :], top[:, hf * GROUP:(hf + 1) * GROUP],
                                                w.null_s[:, hf * GROUP:(hf + 1) * GROUP],
                                                ALU.subtract).then_inc(null_gap, 1)
                    if n % GROUP == LAG_AV and n >= GROUP and n // GROUP - 1 < groups:
                        hf = n // GROUP - 1
                        block_, g = divmod(hf, H // GROUP)
                        dve.wait_ge(av_done, GROUP * (hf + 1))
                        if block_ >= 2 and g == 0:
                            dve.wait_ge(y_made, R * (block_ - 2) + a.rounds)
                        n4 = slice(hf * GROUP, (hf + 1) * GROUP)
                        heads = a.outputs(c.ps[O_BANK + hf % 2], hf)
                        if a.shared_kv:
                            dve.wait_ge(null_spread, hf + 1)
                            part = w.null_part[:, hf % 2, :, :].rearrange("p (a b) d -> p a b d", b=2)
                            chain.mark(nc.vector.tensor_tensor(part, part, heads, ALU.add))
                            chain.link(nc.vector.tensor_tensor(sums[:, n4], sums[:, n4],
                                                               w.null_weight[:, hf % 2, :], ALU.add))
                            heads = part
                        chain.link(nc.vector.reciprocal(rinv[:, hf % 2, :], sums[:, n4]))
                        span = GROUP * a.width
                        over_sum = rinv[:, hf % 2, :].rearrange("p (a b) -> p a b", b=2).unsqueeze(3)
                        nc.vector.tensor_tensor(
                            O[:, block_ % 2, g * span:(g + 1) * span].rearrange("p (a b d) -> p a b d", b=2,
                                                                               d=a.width),
                            heads, over_sum.broadcast_to([P, 2, 2, a.width]), ALU.mult).then_inc(o_ready, 1)
        st.end()


class Work:

    def __init__(self, nc, ctx, a):
        def sb(name, shape, dt=F32):
            return ctx.enter_context(nc.sbuf_tensor(f"{a.name}_{name}", shape, dt))

        self.sb = sb
        self.probs = sb("probs", [P, 3, S])
        self.PT = sb("PT", [P, 2, S])
        self.sums = sb("sums", [P, a.batches * UNITS])
        self.top = sb("top", [P, a.batches * UNITS])
        self.rinv = sb("rinv", [P, 2, GROUP])
        self.O = sb("O", [P, 2, a.inner])
        self.OT = sb("OT", [P, a.tiles, P])
        self.wo = sb("wo", [P, a.tiles, D])
        self.n_loads = 0


def attention0(nc, c, w, xaT):
    with ExitStack() as ctx:
        a = Heads("a0", DH, causal=False, projected=True, dst=c.s)
        k = Work(nc, ctx, a)
        k.xT = k.sb("xT", [P, S])
        k.QT = k.sb("QT", [P, a.tiles, S])
        k.KT = [k.sb("KT", [P, a.tiles, S]), c.xn[:].rearrange("p t d -> p (t d)").rearrange(
            "p (t m) -> p t m", m=S)]
        k.V = k.sb("V", [P, QB, a.inner])
        k.wq, k.wk, k.wv = (k.sb(n, [P, a.inner]) for n in ("wq", "wk", "wv"))
        k.q_scale = DH ** -0.5
        k.source = xaT
        with ExitStack() as ld:
            st = Stage(nc, ld, "a0l")
            loaded, zeroed = st.sems("loaded", "zeroed")
            load_all(st, loaded, [(k.wq[:], w["L0_attn_Wq"]), (k.wk[:], w["L0_attn_Wk"]), (k.wv[:], w["L0_attn_Wv"]),
                                  (k.wo[:], w["L0_attn_Wo"].rearrange("(t p) d -> p t d", p=P))],
                     clear=[(k.KT[0][DH:P, :, :], zeroed), (k.KT[1][0:DH, :, :], zeroed)])
        with nc.Fori(0, NB) as b:
            attention_stage(nc, c, a, b, k)


def position_bias(nc, c, w, bias):
    tiles = NPOS // P
    with ExitStack() as ctx:
        st = Stage(nc, ctx, "pb")
        (loaded, pos_ready, dve_done, var_ready, root_ready, silued, turned, copied, h_ready, table, written, spread,
         reversal, placed, act_placed, dve_placed) = st.sems(
            "loaded", "pos_ready", "dve_done", "var_ready", "root_ready", "silued", "turned", "copied",
            "h_ready", "table", "written", "spread", "reversal", "placed", "act_placed", "dve_placed")
        reverse = st.sb("reverse", [P, P])
        rows = [t[:].rearrange("p t d -> p (t d)").rearrange("p (h m) -> p h m", m=S) for t in (c.xn, c.s)]
        names = ["w0", "b0", "ln0_g", "ln0_b", "b1", "ln1_g", "ln1_b"]
        row = {n: st.sb(n, [P, D]) for n in names}
        w1 = st.sb("w1", [P, D])
        w2 = st.sb("w2", [P, H])
        b2 = st.sb("b2", [H, 1])
        pos = st.sb("pos", [P, tiles])
        hid = st.sb("hid", [P, tiles, D])
        hidT = st.sb("hidT", [P, NPOS])
        stats = st.sb("stats", [P, tiles, 6])
        mv = st.sb("mv", [P, tiles, 2])
        rstd = st.sb("rstd", [P, tiles, 1])
        minus = st.sb("minus", [H, NPOS])
        n_loads = len(names) + 3

        with nc.Block() as block:
            @block.sync
            def _(sp):
                for n in names:
                    sp.dma_start(row[n][:], row_bcast(w["L1_attn_pb_" + n], D)).then_inc(loaded, 16)
                sp.dma_start(w1[:], w["L1_attn_pb_w1"]).then_inc(loaded, 16)
                sp.dma_start(w2[:], w["L1_attn_pb_w2"]).then_inc(loaded, 16)
                sp.dma_start(b2[:], column(w["L1_attn_pb_b2"])).then_inc(loaded, 16)
                sp.wait_ge(table, 2)
                sp.dma_start(c.table, minus[:]).then_inc(written, 16)
                sp.wait_ge(written, 16)
                for h in range(H):
                    src = bass.AP(tensor=c.table.tensor, offset=c.table.offset + h * NPOS, ap=[[1, P], [1, S]])
                    sp.dma_start(rows[h // 8][:, h % 8, :], src).then_inc(spread, 16)

            @block.gpsimd
            def _(pool):
                nc.gpsimd.iota(pos[:], pattern=[[-P, tiles]], base=S - 1, channel_multiplier=-1,
                               allow_small_or_imprecise_dtypes=True).then_inc(pos_ready, 1)
                nc.gpsimd.memset(reverse[:], 0.0).then_inc(reversal, 1)
                pool.wait_ge(reversal, 1)
                nc.gpsimd.affine_select(out=reverse[:], in_=reverse[:], compare_op=ALU.not_equal, fill=1.0,
                                        base=-(P - 1), pattern=[[1, P]], channel_multiplier=1).then_inc(reversal, 1)
                pool.wait_ge(act_placed, H // 2)
                pool.wait_ge(dve_placed, H // 2)
                for h in range(H):
                    diag = bias[:, h, S - P:S]
                    nc.gpsimd.affine_select(out=diag, in_=diag, compare_op=ALU.is_ge, fill=MASKED, base=0,
                                            pattern=[[-1, P]], channel_multiplier=1)

            @block.vector
            def _(dve):
                chain = Chain(dve, dve_done)
                dve.wait_ge(loaded, 16 * n_loads)
                dve.wait_ge(pos_ready, 1)
                for t in range(tiles):
                    chain.mark(nc.vector.scalar_tensor_tensor(out=hid[:, t, :], in0=row["w0"][:],
                                                              scalar=pos[:, t:t + 1], in1=row["b0"][:],
                                                              op0=ALU.mult, op1=ALU.add))
                chain.wait()
                for layer in range(2):
                    gain, shift = row[f"ln{layer}_g"], row[f"ln{layer}_b"]
                    if layer == 1:
                        dve.wait_ge(h_ready, tiles)
                        for t in range(tiles):
                            chain.mark(nc.vector.tensor_tensor(hid[:, t, :], c.ps[4 + t // 4][:, (t % 4) * P:(t % 4 + 1) * P],
                                                               row["b1"][:], ALU.add))
                        chain.wait()
                    for t in range(tiles):
                        chain.mark(nc.vector.bn_stats(stats[:, t, :], hid[:, t, :]))
                    chain.wait()
                    for t in range(tiles):
                        chain.mark(nc.vector.bn_aggr(mv[:, t, :], stats[:, t, :]))
                    chain.wait()
                    nc.vector.tensor_scalar(rstd[:], mv[:, :, 1:2], LN_EPS, None, ALU.add).then_inc(var_ready, 1)
                    dve.wait_ge(root_ready, layer + 1)
                    chain.link(nc.vector.reciprocal(rstd[:], rstd[:]))
                    for t in range(tiles):
                        chain.mark(nc.vector.tensor_scalar(hid[:, t, :], hid[:, t, :], mv[:, t, 0:1], rstd[:, t, :],
                                                           ALU.subtract, ALU.mult))
                    chain.wait()
                    chain.link(nc.vector.tensor_tensor(hid[:], hid[:], over_blocks(gain[:], tiles), ALU.mult))
                    nc.vector.tensor_tensor(hid[:], hid[:], over_blocks(shift[:], tiles),
                                            ALU.add).then_inc(var_ready, 1)
                for h in range(1, H, 2):
                    dve.wait_ge(placed, h + 1)
                    nc.vector.tensor_copy(bias[:, h, :], c.ps[4 + h % 4][:]).then_inc(dve_placed, 1)

            @block.scalar
            def _(act):
                for layer in range(2):
                    act.wait_ge(var_ready, 2 * layer + 1)
                    nc.scalar.activation(rstd[:], rstd[:], ACT.Sqrt).then_inc(root_ready, 1)
                    act.wait_ge(var_ready, 2 * layer + 2)
                    nc.scalar.activation(hid[:], hid[:], ACT.Silu).then_inc(silued, 1)
                    act.wait_ge(turned, 5 * (layer + 1))
                    nc.scalar.activation(hidT[:, 0:512], c.ps[0][:], ACT.Copy).then_inc(copied, 1)
                    nc.scalar.activation(hidT[:, 512:NPOS], c.ps[1][:, 0:P], ACT.Copy).then_inc(copied, 1)
                act.wait_ge(loaded, 16 * n_loads)
                act.wait_ge(h_ready, tiles + 2)
                nc.scalar.activation(minus[:, 0:512], c.ps[2][0:H, :], ACT.Identity,
                                     bias=b2[:]).then_inc(copied, 1)
                nc.scalar.activation(minus[:, 512:NPOS], c.ps[3][0:H, 0:P], ACT.Identity,
                                     bias=b2[:]).then_inc(copied, 1)
                act.wait_ge(copied, 6)
                nc.scalar.activation(minus[:], minus[:], ACT.Copy, scale=-1.0).then_inc(table, 2)
                for h in range(0, H, 2):
                    act.wait_ge(placed, h + 1)
                    nc.scalar.activation(bias[:, h, :], c.ps[4 + h % 4][:], ACT.Copy).then_inc(act_placed, 1)

            @block.tensor
            def _(pe):
                pe.wait_ge(loaded, 16 * n_loads)
                for layer in range(2):
                    pe.wait_ge(silued, layer + 1)
                    for t in range(tiles):
                        nc.tensor.transpose(c.ps[t // 4][:, (t % 4) * P:(t % 4 + 1) * P], hid[:, t, :],
                                            c.ident[:]).then_inc(turned, 1)
                    pe.wait_ge(copied, 2 * (layer + 1))
                    if layer == 0:
                        for t in range(tiles):
                            nc.tensor.matmul(c.ps[4 + t // 4][:, (t % 4) * P:(t % 4 + 1) * P],
                                             hidT[:, t * P:(t + 1) * P], w1[:], start=True,
                                             stop=True).then_inc(h_ready, 1)
                    else:
                        nc.tensor.matmul(c.ps[2][0:H, :], w2[:], hidT[:, 0:512], start=True,
                                         stop=True).then_inc(h_ready, 1)
                        nc.tensor.matmul(c.ps[3][0:H, 0:P], w2[:], hidT[:, 512:NPOS], start=True,
                                         stop=True).then_inc(h_ready, 1)
                pe.wait_ge(reversal, 2)
                pe.wait_ge(spread, 16 * H)
                for h in range(H):
                    if h >= 4:
                        pe.wait_ge(dve_placed if h % 2 else act_placed, (h - 4) // 2 + 1)
                    nc.tensor.matmul(c.ps[4 + h % 4][:], reverse[:], rows[h // 8][:, h % 8, :], start=True,
                                     stop=True).then_inc(placed, 1)
        st.end()


def ternary_gate(nc, c, w):
    f_tiles = FF // P
    with ExitStack() as ctx:
        st = Stage(nc, ctx, "g1")
        loaded, dve_done, summed, spread, weights, up_done, gelued, down_done, g_ready, silued = st.sems(
            "loaded", "dve_done", "summed", "spread", "weights", "up_done", "gelued", "down_done", "g_ready", "silued")
        w1 = st.sb("w1", [P, FF])
        w2 = st.sb("w2", [P, f_tiles, D])
        b1 = st.sb("b1", [P, f_tiles])
        b2 = st.sb("b2", [P, D])
        row_sum = st.sb("row_sum", [P, 2])
        half_scale = st.sb("half_scale", [P, 2])
        minus_half = st.sb("minus_half", [P, 2])
        above = st.sb("above", [P, FF])
        below = st.sb("below", [P, FF])
        hT = st.sb("hT", [P, 2, f_tiles, S])

        with nc.Block() as block:
            @block.sync
            def _(sp):
                sp.dma_start(w1[:], w["L1_ffn_W1T"]).then_inc(loaded, 16)
                sp.dma_start(w2[:], w["L1_ffn_W2T"].rearrange("(t p) d -> p t d", p=P)).then_inc(loaded, 16)
                sp.dma_start(b1[:], w["L1_ffn_b1T"]).then_inc(loaded, 16)
                sp.dma_start(b2[:], row_bcast(w["L1_ffn_b2"], D)).then_inc(loaded, 16)

            @block.vector
            def _(dve):
                chain = Chain(dve, dve_done)
                dve.wait_ge(loaded, 64)
                mats = [w1[:], w2[:].rearrange("p t d -> p (t d)")]
                for i, m in enumerate(mats):
                    chain.mark(nc.vector.tensor_reduce(row_sum[:, i:i + 1], m, AX, ALU.add,
                                                       apply_absolute_value=True))
                chain.wait()
                nc.vector.tensor_copy(row_sum[:], row_sum[:]).then_inc(summed, 1)
                dve.wait_ge(spread, 1)
                chain.link(nc.vector.tensor_scalar(half_scale[:], c.ps[0][:, 0:2], 1.0 / (FF * D), 1e-8,
                                                   ALU.mult, ALU.max))
                chain.link(nc.vector.tensor_scalar(half_scale[:], half_scale[:], 0.5, None, ALU.mult))
                chain.link(nc.vector.tensor_scalar(minus_half[:], half_scale[:], -1.0, None, ALU.mult))
                for i, m in enumerate(mats):
                    chain.mark(nc.vector.tensor_scalar(above[:], m, half_scale[:, i:i + 1], None, ALU.is_gt))
                    chain.link(nc.vector.tensor_scalar(below[:], m, minus_half[:, i:i + 1], None, ALU.is_lt))
                    chain.link(nc.vector.tensor_tensor(above[:], above[:], below[:], ALU.subtract))
                    chain.link(nc.vector.tensor_tensor(above[:], above[:], m, ALU.subtract))
                    chain.link(nc.vector.tensor_tensor(m, m, above[:], ALU.add))
                nc.vector.tensor_copy(row_sum[:], row_sum[:]).then_inc(weights, 1)
                for b in range(NB):
                    dve.wait_ge(down_done, b + 1)
                    nc.vector.tensor_tensor(c.g[:, b * QB:(b + 1) * QB, :],
                                            c.ps[6 + b % 2][:].rearrange("p (q d) -> p q d", d=D),
                                            over_blocks(b2[:], QB), ALU.add).then_inc(g_ready, 1)

            @block.tensor
            def _(pe):
                pe.wait_ge(summed, 1)
                nc.tensor.matmul(c.ps[0][:, 0:2], c.ones[:], row_sum[:], start=True, stop=True).then_inc(spread, 1)
                pe.wait_ge(weights, 1)
                for b in range(NB + 1):
                    if b < NB:
                        for f in range(f_tiles):
                            n = b * f_tiles + f
                            if n >= 4:
                                pe.wait_ge(gelued, n - 3)
                            nc.tensor.matmul(c.ps[n % 4][:], w1[:, f * P:(f + 1) * P], c.xnT[:, b, :], start=True,
                                             stop=True).then_inc(up_done, 1)
                    if b > 0:
                        d = b - 1
                        pe.wait_ge(gelued, f_tiles * (d + 1))
                        if d >= 2:
                            pe.wait_ge(g_ready, d - 1)
                        for q in range(QB):
                            for f in range(f_tiles):
                                last = nc.tensor.matmul(c.ps[6 + d % 2][:, q * P:(q + 1) * P],
                                                        hT[:, d % 2, f, q * P:(q + 1) * P], w2[:, f, :],
                                                        start=f == 0, stop=f == f_tiles - 1)
                        last.then_inc(down_done, 1)

            @block.scalar
            def _(act):
                act.wait_ge(loaded, 64)
                for b in range(NB):
                    if b >= 2:
                        act.wait_ge(down_done, b - 1)
                    for f in range(f_tiles):
                        n = b * f_tiles + f
                        act.wait_ge(up_done, n + 1)
                        nc.scalar.activation(hT[:, b % 2, f, :], c.ps[n % 4][:], ACT.Gelu,
                                             bias=b1[:, f:f + 1]).then_inc(gelued, 1)
                act.wait_ge(g_ready, NB)
                nc.scalar.activation(c.g[:], c.g[:], ACT.Silu).then_inc(silued, 1)
        st.end()


def attention1(nc, c, w, xaT):
    with ExitStack() as ctx:
        bias = ctx.enter_context(nc.sbuf_tensor("bias", [P, H, S], F32))
        position_bias(nc, c, w, bias)
        a = Heads("a1", DH, causal=True, bias=bias, shared_kv=True, projected=True, dst=c.s)
        k = Work(nc, ctx, a)
        k.xT = k.sb("xT", [P, S])
        k.QT = k.sb("QT", [P, a.tiles, S])
        k.KT = [k.sb(f"KT{i}", [P, 1, S]) for i in range(2)]
        k.V = k.sb("V", [P, QB, P])
        k.wq = k.sb("wq", [P, a.inner])
        k.wk = k.sb("wk", [P, P])
        k.wv = k.sb("wv", [P, P])
        k.q_scale = -DH ** -0.5
        k.source = xaT
        k.biased = k.sb("biased", [P, 3, S])
        k.null_k = k.sb("null_k", [P, 2])
        k.null_v = k.sb("null_v", [P, DH])
        k.null_bias = k.sb("null_bias", [P, UNITS])
        k.null_s = k.sb("null_s", [P, UNITS])
        k.null_less = k.sb("null_less", [P, UNITS // GROUP, GROUP])
        k.null_weight = k.sb("null_weight", [P, 2, GROUP])
        k.null_part = k.sb("null_part", [P, 2, GROUP, DH])
        with ExitStack() as ld:
            st = Stage(nc, ld, "a1l")
            zeroed, loaded, negated = st.sems("zeroed", "loaded", "negated")
            wkv = w["L1_attn_Wkv"]
            null_kv = w["L1_attn_null_kv"]
            pairs = [(k.wq[:], w["L1_attn_Wq"]), (k.wk[:, 0:DH], wkv[:, 0:DH]), (k.wk[:, DH:P], wkv[:, 0:DH]),
                     (k.wv[:, 0:DH], wkv[:, DH:2 * DH]), (k.wv[:, DH:P], wkv[:, DH:2 * DH]),
                     (k.null_v[:], row_bcast(null_kv[1], DH)),
                     (k.wo[:], w["L1_attn_Wo"].rearrange("(t p) d -> p t d", p=P)),
                     (k.null_k[0:DH, 0:1], column(null_kv[0])), (k.null_k[DH:P, 1:2], column(null_kv[0]))]
            pairs += [(k.null_bias[:, q * H:(q + 1) * H], row_bcast(w["L1_attn_null_attn_bias"], H))
                      for q in range(QB)]
            with nc.Block() as block:
                @block.sync
                def _(sp):
                    sp.wait_ge(zeroed, 1)
                    for dst, src in pairs:
                        sp.dma_start(dst, src).then_inc(loaded, 16)

                @block.vector
                def _(dve):
                    nc.vector.memset(k.null_k[:], 0.0).then_inc(zeroed, 1)
                    nc.vector.memset(k.KT[0][DH:P, :, :], 0.0).then_inc(zeroed, 1)
                    nc.vector.memset(k.KT[1][0:DH, :, :], 0.0).then_inc(zeroed, 1)
                    dve.wait_ge(loaded, 16 * len(pairs))
                    nc.vector.tensor_scalar(k.null_bias[:], k.null_bias[:], -1.0, None, ALU.mult).then_inc(negated, 1)
            st.end()
        with nc.Fori(0, NB) as b:
            attention_stage(nc, c, a, b, k)


def project_stage(nc, c, name, srcT, transposed, value=None, rope=None, split=False):
    with ExitStack() as ctx:
        st = Stage(nc, ctx, name)
        loaded, made, act_copied, dve_copied, dve_done, v_made, v_copied, parted, *stored = st.sems(
            "loaded", "made", "act_copied", "dve_copied", "dve_done", "v_made", "v_copied", "parted", "stored_even",
            "stored_odd")
        mats, biases, tables = [], [], []
        pairs = []
        for i, (weight, bias, scale, _) in enumerate(transposed):
            group = []
            for k, src in enumerate(weight if rope else (weight,)):
                m = st.sb(f"w{i}{k}", [P, D])
                group.append(m)
                pairs.append((m[:], src))
            mats.append(group)
            biases.append(None)
            if bias is not None:
                biases[i] = st.sb(f"b{i}", [P, 1])
                pairs.append((biases[i][:], column(bias)))
            if rope:
                tables.append([st.sb(f"t{i}{k}", [P, S]) for k in range(2)])
                pairs += [(t[:], src) for t, src in zip(tables[i], scale)]
        if value is not None:
            wv = st.sb("wv", [P, D])
            pairs.append((wv[:], value[0]))
        n = len(transposed)
        kept = st.sb("kept", [P, n, S * 2])
        turned = st.sb("rotated", [P, 2, S]) if rope else None
        upper = st.sb("upper", [P, n, S * 2]) if split else None
        copied = dve_copied if rope else act_copied
        half_stores = [16 * n * (NB // 2) * (2 if split else 1) + (32 * n if split and i == 0 else 0) for i in range(2)]

        def stores_before(b):
            return 16 * n * (b // 2) * (2 if split else 1) + (32 * n if split and b % 2 == 0 and b > 0 else 0)

        with nc.Block() as block:
            @block.sync
            def _(sp):
                for dst, src in pairs:
                    sp.dma_start(dst, src).then_inc(loaded, 16)
                for b in range(NB):
                    for i, (_, _, _, dram) in enumerate(transposed):
                        j = b * n + i
                        now = slice((b % 2) * S, (b % 2 + 1) * S)
                        sp.wait_ge(parted if split else copied, j + 1)
                        if not split:
                            sp.dma_start(dram[:, b, :], kept[:, i, now]).then_inc(stored[b % 2], 16)
                            continue
                        for to in (b, NB) if b == 0 else (b,):
                            sp.dma_start(dram[0, :, to, :], upper[:, i, now]).then_inc(stored[b % 2], 16)
                            sp.dma_start(dram[1, :, to, :], kept[:, i, now]).then_inc(stored[b % 2], 16)
                for half, total in zip(stored, half_stores):
                    sp.wait_ge(half, total)

            @block.tensor
            def _(pe):
                pe.wait_ge(loaded, 16 * len(pairs))
                for b in range(NB):
                    for i in range(n):
                        j = b * n + i
                        if j >= 2:
                            pe.wait_ge(copied, j - 1)
                        for k, m in enumerate(mats[i]):
                            last = nc.tensor.matmul(c.ps[2 * k + j % 2][:], m[:], srcT[:, b, :], start=True, stop=True)
                        last.then_inc(made, 1)
                    if value is not None:
                        if b >= 2:
                            pe.wait_ge(v_copied, b - 1)
                        for q in range(QB):
                            last = nc.tensor.matmul(c.ps[4 + b % 2][:, q * P:(q + 1) * P],
                                                    srcT[:, b, q * P:(q + 1) * P], wv[:], start=True, stop=True)
                        last.then_inc(v_made, 1)

            @block.scalar
            def _(act):
                act.wait_ge(loaded, 16 * len(pairs))
                for b in range(NB):
                    if not rope:
                        for i, (_, _, scale, _) in enumerate(transposed):
                            j = b * n + i
                            act.wait_ge(made, j + 1)
                            if b >= 2:
                                act.wait_ge(stored[b % 2], stores_before(b))
                            bias = {} if biases[i] is None else {"bias": biases[i][:]}
                            nc.scalar.activation(kept[:, i, (b % 2) * S:(b % 2 + 1) * S], c.ps[j % 2][:],
                                                 ACT.Identity, scale=scale, **bias).then_inc(act_copied, 1)
                    if value is not None:
                        act.wait_ge(v_made, b + 1)
                        nc.scalar.activation(value[1][:, b * QB:(b + 1) * QB, :].rearrange("p q d -> p (q d)"),
                                             c.ps[4 + b % 2][:], ACT.Copy).then_inc(v_copied, 1)

            if rope or split:
                @block.vector
                def _(dve):
                    chain = Chain(dve, dve_done)
                    dve.wait_ge(loaded, 16 * len(pairs))
                    for b in range(NB):
                        for i in range(n):
                            j = b * n + i
                            now = slice((b % 2) * S, (b % 2 + 1) * S)
                            if rope:
                                dve.wait_ge(made, j + 1)
                                if j > 0:
                                    dve.wait_ge(dve_copied, j)
                                if b >= 2:
                                    dve.wait_ge(stored[b % 2], stores_before(b))
                                for k in range(2):
                                    chain.mark(nc.vector.tensor_tensor(turned[:, k, :], c.ps[2 * k + j % 2][:],
                                                                       tables[i][k][:], ALU.mult))
                                chain.wait()
                                nc.vector.tensor_tensor(kept[:, i, now], turned[:, 0, :], turned[:, 1, :],
                                                        ALU.add).then_inc(dve_copied, 1)
                            if split:
                                dve.wait_ge(copied, j + 1)
                                chain.link(nc.vector.tensor_scalar(upper[:, i, now].bitcast(I32),
                                                                   kept[:, i, now].bitcast(I32), UPPER, None,
                                                                   ALU.bitwise_and))
                                nc.vector.tensor_tensor(kept[:, i, now], kept[:, i, now], upper[:, i, now],
                                                        ALU.subtract).then_inc(parted, 1)
        st.end()


def unit_length(nc, c, q, k, v, dram):
    with ExitStack() as ctx:
        st = Stage(nc, ctx, "len")
        loaded, dve_done, squared, rooted = st.sems("loaded", "dve_done", "squared", "rooted")
        square = st.sb("square", [P, DN, S])
        length = st.sb("length", [P, 2, S])
        with nc.Block() as block:
            @block.sync
            def _(sp):
                for dst, src in zip((q, k, v), dram):
                    sp.dma_start(dst, src.rearrange("b (h d) t -> (b h) d t", d=DN)).then_inc(loaded, 16)

            @block.scalar
            def _(act):
                act.wait_ge(squared, 1)
                nc.scalar.activation(length[:], length[:], ACT.Sqrt).then_inc(rooted, 1)

            @block.vector
            def _(dve):
                chain = Chain(dve, dve_done)
                dve.wait_ge(loaded, 48)
                for i, m in enumerate((q, k)):
                    chain.link(nc.vector.tensor_tensor(square[:], m, m, ALU.mult))
                    chain.link(nc.vector.tensor_reduce(length[:, i, :], square[:].rearrange("p d t -> p t d"), AX,
                                                       ALU.add))
                nc.vector.tensor_copy(square[:, 0, 0:1], square[:, 0, 0:1]).then_inc(squared, 1)
                dve.wait_ge(rooted, 1)
                chain.link(nc.vector.tensor_scalar(length[:], length[:], 1e-12, None, ALU.max))
                chain.link(nc.vector.reciprocal(length[:], length[:]))
                for i, m in enumerate((q, k)):
                    nc.vector.tensor_tensor(m, m, length[:, i, :].unsqueeze(1).broadcast_to([P, DN, S]),
                                            ALU.mult).then_inc(dve_done, 1)
        st.end()


def threshold_routing(nc, c, w, weight):
    with ExitStack() as ctx:
        st = Stage(nc, ctx, "r2")
        loaded, made, dve_done, less, exped, ready, turned, copied, b_made, b_copied = st.sems(
            "loaded", "made", "dve_done", "less", "exped", "ready", "turned", "copied", "b_made", "b_copied")
        wgt = st.sb("wgt", [P, E + 1])
        bgt = st.sb("bgt", [P, E + 1])
        b2 = st.sb("b2", [E, D])
        logit = st.sb("logit", [P, TB, E + 1])
        top = st.sb("top", [P, TB, 1])
        total = st.sb("total", [P, TB, 1])
        none = st.sb("none", [P, TB, 1])
        weightT = st.sb("weightT", [E, 2, S])
        gate, thr = logit[:, :, 0:E], logit[:, :, E:E + 1]

        def spread(t):
            return t[:].broadcast_to([P, TB, E])

        with nc.Block() as block:
            @block.sync
            def _(sp):
                sp.dma_start(wgt[:, 0:E], w["L2_ffn_Wg"]).then_inc(loaded, 16)
                sp.dma_start(wgt[:, E:E + 1], w["L2_ffn_Wt"]).then_inc(loaded, 16)
                sp.dma_start(bgt[:, 0:E], row_bcast(w["L2_ffn_bg"], E)).then_inc(loaded, 16)
                sp.dma_start(bgt[:, E:E + 1], row_bcast(w["L2_ffn_bt"], 1)).then_inc(loaded, 16)
                sp.dma_start(b2[:], w["L2_ffn_b2"]).then_inc(loaded, 16)

            def biases(pe, b):
                pe.wait_ge(copied, b + 1)
                if b >= 2:
                    pe.wait_ge(b_copied, b - 1)
                for q in range(QB):
                    last = nc.tensor.matmul(c.ps[3 + b % 2][:, q * P:(q + 1) * P],
                                            weightT[:, b % 2, q * P:(q + 1) * P], b2[:], start=True, stop=True)
                last.then_inc(b_made, 1)

            @block.tensor
            def _(pe):
                pe.wait_ge(loaded, 80)
                for t in range(TB):
                    last = nc.tensor.matmul(c.ps[0][:, t * (E + 1):(t + 1) * (E + 1)],
                                            c.xnT[:, t // QB, (t % QB) * P:(t % QB + 1) * P], wgt[:],
                                            start=True, stop=True)
                last.then_inc(made, 1)
                pe.wait_ge(ready, 1)
                for b in range(NB):
                    if b >= 2:
                        pe.wait_ge(copied, b - 1)
                    for q in range(QB):
                        last = nc.tensor.transpose(c.ps[1 + b % 2][0:E, q * P:(q + 1) * P], weight[:, b * QB + q, :],
                                                   c.ident[:])
                    last.then_inc(turned, 1)
                    if b >= 1:
                        biases(pe, b - 1)
                biases(pe, NB - 1)

            @block.scalar
            def _(act):
                act.wait_ge(less, 1)
                nc.scalar.activation(gate, gate, ACT.Exp).then_inc(exped, 1)
                nc.scalar.activation(thr, thr, ACT.Tanh, scale=0.5).then_inc(exped, 1)
                for b in range(NB):
                    act.wait_ge(turned, b + 1)
                    if b >= 2:
                        act.wait_ge(b_made, b - 1)
                    nc.scalar.activation(weightT[:, b % 2, :], c.ps[1 + b % 2][0:E, :], ACT.Copy).then_inc(copied, 1)

            @block.vector
            def _(dve):
                chain = Chain(dve, dve_done)
                dve.wait_ge(loaded, 80)
                dve.wait_ge(made, 1)
                chain.link(nc.vector.tensor_tensor(
                    logit[:], c.ps[0][:, 0:TB * (E + 1)].rearrange("p (t e) -> p t e", e=E + 1),
                    over_blocks(bgt[:]), ALU.add))
                chain.link(nc.vector.tensor_reduce(top[:], gate, AX, ALU.max))
                nc.vector.tensor_tensor(gate, gate, spread(top), ALU.subtract).then_inc(less, 1)
                dve.wait_ge(exped, 2)
                chain.link(nc.vector.tensor_reduce(total[:], gate, AX, ALU.add))
                chain.link(nc.vector.reciprocal(total[:], total[:]))
                chain.link(nc.vector.tensor_tensor(gate, gate, spread(total), ALU.mult))
                chain.link(nc.vector.tensor_scalar(top[:], thr, 1.0, 0.0625, ALU.add, ALU.mult))
                chain.link(nc.vector.tensor_tensor(gate, gate, spread(top), ALU.subtract))
                chain.link(nc.vector.tensor_scalar(gate, gate, 0.0, None, ALU.max))
                chain.link(nc.vector.tensor_reduce(total[:], gate, AX, ALU.add))
                chain.link(nc.vector.tensor_scalar(none[:], total[:], 0.0, None, ALU.is_equal))
                chain.link(nc.vector.tensor_tensor(total[:], total[:], none[:], ALU.add))
                chain.link(nc.vector.reciprocal(total[:], total[:]))
                nc.vector.tensor_tensor(weight[:], gate, spread(total), ALU.mult).then_inc(ready, 1)
                for b in range(NB):
                    dve.wait_ge(b_made, b + 1)
                    nc.vector.tensor_copy(c.g[:, b * QB:(b + 1) * QB, :].rearrange("p q d -> p (q d)"),
                                          c.ps[3 + b % 2][:]).then_inc(b_copied, 1)
        st.end()


STEPS = S // NB
PART = STEPS // 2
BETA, CLAMP, STATE_CAP, SHRINK = 0.9, 1.0, 10.0, 0.9


def delta_and_experts(nc, c, w, b, k, o_dram):
    f_tiles = FF // P
    with ExitStack() as ctx:
        st = Stage(nc, ctx, "d2")
        (ready, taken, stepped, dve_done, o_done, o_ready, stored, up_done, gelued, down_done, scaled,
         added) = st.sems("ready", "taken", "stepped", "dve_done", "o_done", "o_ready", "stored", "up_done", "gelued",
                          "down_done", "scaled", "added")
        with nc.Block() as block:
            @block.vector
            def _(dve):
                chain = Chain(dve, dve_done)
                nc.vector.tensor_copy(k.v_now[:], k.v[:, :, bass.ts(b, STEPS)].rearrange("p d t -> p t d")).then_inc(
                    taken, 1)
                dve.wait_ge(ready, 3)
                dve.wait_ge(taken, 1)
                for t in range(STEPS):
                    raw = k.raw[:, t // PART, t % PART]
                    before = k.raw[:, (t - 1) % STEPS // PART, (t - 1) % PART]
                    shrink = k.shrink[:, (t - 1) % STEPS:(t - 1) % STEPS + 1]
                    key = k.k_now[:, t, :].unsqueeze(1).broadcast_to([P, DN, DN])
                    chain.link(nc.vector.tensor_tensor(k.prod[:], before, key, ALU.mult))
                    chain.link(nc.vector.tensor_reduce(k.delta[:], k.prod[:], AX, ALU.add))
                    chain.link(nc.vector.scalar_tensor_tensor(out=k.delta[:], in0=k.delta[:], scalar=shrink,
                                                              in1=k.v_now[:, t, :], op0=ALU.mult, op1=ALU.subtract))
                    chain.link(nc.vector.tensor_scalar(k.delta[:], k.delta[:], -CLAMP, CLAMP, ALU.max, ALU.min))
                    chain.link(nc.vector.tensor_tensor(
                        k.prod[:], k.delta[:].unsqueeze(2).broadcast_to([P, DN, DN]),
                        k.nk_now[:, t, :].unsqueeze(1).broadcast_to([P, DN, DN]), ALU.mult))
                    chain.link(nc.vector.scalar_tensor_tensor(out=raw, in0=before, scalar=shrink, in1=k.prod[:],
                                                              op0=ALU.mult, op1=ALU.add))
                    chain.link(nc.vector.tensor_reduce(k.peak[:], raw.rearrange("p e d -> p (e d)"), AX, ALU.max,
                                                       apply_absolute_value=True))
                    chain.link(nc.vector.tensor_scalar(k.shrink[:, t:t + 1], k.peak[:], STATE_CAP, SHRINK, ALU.is_le,
                                                       ALU.max))
                    if t % PART == PART - 1:
                        nc.vector.tensor_copy(k.peak[:], k.peak[:]).then_inc(stepped, 1)

            @block.gpsimd
            def _(pool):
                def outputs(part):
                    chain = Chain(pool, o_done)
                    chain.n = 5 * part
                    pool.wait_ge(stepped, part + 1)
                    tmp = k.o_part
                    q = k.q_now[:, part * PART:(part + 1) * PART, :].unsqueeze(3).broadcast_to([P, PART, DN, DN])
                    chain.link(nc.gpsimd.tensor_tensor(tmp[:], k.raw[:, part], q, ALU.mult))
                    for half in (4, 2, 1):
                        chain.link(nc.gpsimd.tensor_tensor(tmp[:, :, 0:half, :], tmp[:, :, 0:half, :],
                                                           tmp[:, :, half:2 * half, :], ALU.add))
                    o = k.o_now[:, :, part * PART:(part + 1) * PART].rearrange("p d t -> p t d")
                    shrink = k.shrink[:, part * PART:(part + 1) * PART].unsqueeze(2).broadcast_to([P, PART, DN])
                    chain.link(nc.gpsimd.tensor_tensor(tmp[:, :, 0, :], tmp[:, :, 0, :], shrink, ALU.mult))
                    nc.gpsimd.tensor_scalar(o, tmp[:, :, 0, :], CLAMP, -CLAMP, ALU.min, ALU.max).then_inc(o_ready, 1)

                nc.gpsimd.tensor_copy(k.k_now[:], k.k[:, :, bass.ts(b, STEPS)].rearrange("p d t -> p t d")).then_inc(
                    ready, 1)
                pool.wait_ge(ready, 1)
                nc.gpsimd.tensor_scalar(k.nk_now[:], k.k_now[:], -BETA, 1.0, ALU.mult, ALU.mult).then_inc(ready, 1)
                nc.gpsimd.tensor_copy(k.w_now[:], k.weight[:, bass.ts(b, QB), :]).then_inc(ready, 1)
                nc.gpsimd.tensor_copy(k.q_now[:], k.q[:, :, bass.ts(b, STEPS)].rearrange("p d t -> p t d")).then_inc(
                    ready, 1)
                pool.wait_ge(ready, 4)
                for e in range(E):
                    pool.wait_ge(scaled, QB * (e + 1))
                    if e >= 1:
                        pool.wait_ge(added, e)
                    g = c.g[:, bass.ts(b, QB), :]
                    nc.gpsimd.tensor_tensor(g, g, k.weighted[:, e % 2, :, :], ALU.add).then_inc(added, 1)
                    if e == E // 2 + 1:
                        outputs(0)
                outputs(1)

            @block.sync
            def _(sp):
                sp.wait_ge(o_ready, 2)
                sp.dma_start(o_dram[:, :, bass.ts(b, STEPS)], k.o_now[:]).then_inc(stored, 16)
                sp.wait_ge(stored, 16)

            @block.tensor
            def _(pe):
                for e in range(E + 1):
                    if e < E:
                        for f in range(f_tiles):
                            n = e * f_tiles + f
                            if n >= 4:
                                pe.wait_ge(gelued, n - 3)
                            nc.tensor.matmul(c.ps[n % 4][:], k.w1[:, e, f * P:(f + 1) * P], c.xnT[:, b, :],
                                             start=True, stop=True).then_inc(up_done, 1)
                    if e > 0:
                        d = e - 1
                        pe.wait_ge(gelued, f_tiles * (d + 1))
                        if d >= 2:
                            pe.wait_ge(scaled, QB * (d - 1))
                        for q in range(QB):
                            for f in range(f_tiles):
                                last = nc.tensor.matmul(c.ps[4 + d % 2][:, q * P:(q + 1) * P],
                                                        k.hT[:, d % 2, f, q * P:(q + 1) * P], k.w2[:, d, f, :],
                                                        start=f == 0, stop=f == f_tiles - 1)
                        last.then_inc(down_done, 1)

            @block.scalar
            def _(act):
                for e in range(E + 1):
                    if e < E:
                        if e >= 2:
                            act.wait_ge(down_done, e - 1)
                        for f in range(f_tiles):
                            act.wait_ge(up_done, e * f_tiles + f + 1)
                            nc.scalar.activation(k.hT[:, e % 2, f, :], c.ps[f % 4][:], ACT.Gelu_apprx_tanh,
                                                 bias=k.b1[:, e, f:f + 1]).then_inc(gelued, 1)
                    if e > 0:
                        d = e - 1
                        act.wait_ge(down_done, d + 1)
                        if d == 0:
                            act.wait_ge(ready, 3)
                        if d >= 2:
                            act.wait_ge(added, d - 1)
                        for q in range(QB):
                            nc.scalar.activation(k.weighted[:, d % 2, q, :], c.ps[4 + d % 2][:, q * P:(q + 1) * P],
                                                 ACT.Copy, scale=k.w_now[:, q, d:d + 1]).then_inc(scaled, 1)
        st.end()


def delta_output(nc, c, w, o_dram):
    with ExitStack() as ctx:
        st = Stage(nc, ctx, "o2")
        loaded, made, added, silued = st.sems("loaded", "made", "added", "silued")
        oT = st.sb("oT", [P, NB, S])
        wo = st.sb("wo", [P, D])
        bo = st.sb("bo", [P, D])
        with nc.Block() as block:
            @block.sync
            def _(sp):
                sp.dma_start(wo[:], w["L2_attn_WoT"]).then_inc(loaded, 16)
                sp.dma_start(bo[:], row_bcast(w["L2_attn_bo"], D)).then_inc(loaded, 16)
                sp.dma_start(oT[:], bass.AP(tensor=o_dram.tensor, offset=o_dram.offset,
                                            ap=[[S, P], [P * S, NB], [1, S]])).then_inc(loaded, 16)

            @block.scalar
            def _(act):
                nc.scalar.activation(c.g[:], c.g[:], ACT.Silu).then_inc(silued, 1)

            @block.tensor
            def _(pe):
                pe.wait_ge(loaded, 48)
                for b in range(NB):
                    if b >= 2:
                        pe.wait_ge(added, b - 1)
                    for q in range(QB):
                        last = nc.tensor.matmul(c.ps[b % 2][:, q * P:(q + 1) * P], oT[:, b, q * P:(q + 1) * P], wo[:],
                                                start=True, stop=True)
                    last.then_inc(made, 1)

            @block.vector
            def _(dve):
                dve.wait_ge(loaded, 48)
                for b in range(NB):
                    dve.wait_ge(made, b + 1)
                    nc.vector.tensor_tensor(c.s[:, b * QB:(b + 1) * QB, :],
                                            c.ps[b % 2][:].rearrange("p (q d) -> p q d", d=D),
                                            over_blocks(bo[:], QB), ALU.add).then_inc(added, 1)
        st.end()


class DeltaWork:
    pass


def layer2(nc, c, w):
    with ExitStack() as ctx:
        def sb(name, shape, dt=F32):
            return ctx.enter_context(nc.sbuf_tensor(f"l2_{name}", shape, dt))

        k = DeltaWork()
        k.q = c.xn[:].rearrange("p t d -> p (t d)").rearrange("p (d t) -> p d t", t=S)
        k.k = c.s[:].rearrange("p t d -> p (t d)").rearrange("p (d t) -> p d t", t=S)
        k.v = sb("v", [P, DN, S])
        dram = [nc.dram_tensor(f"l2_{n}T", (NB, D, S), F32, kind="Internal").ap() for n in "qkv"]
        o_dram = nc.dram_tensor("l2_o", (P, DN, S), F32, kind="Internal").ap()
        project_stage(nc, c, "p2", c.xnT, [(w[f"L2_attn_W{n}T"], w[f"L2_attn_b{n}"], 1.0,
                                            d.rearrange("b d t -> d b t")) for n, d in zip("qkv", dram)])
        unit_length(nc, c, k.q, k.k, k.v[:], dram)
        k.weight = sb("weight", [P, TB, E])
        threshold_routing(nc, c, w, k.weight)
        k.w1 = sb("w1", [P, E, FF])
        k.w2 = sb("w2", [P, E, FF // P, D])
        k.b1 = sb("b1", [P, E, FF // P])
        k.hT = sb("hT", [P, 2, FF // P, S])
        k.weighted = sb("weighted", [P, 2, QB, D])
        k.raw = sb("raw", [P, 2, PART, DN, DN])
        k.shrink = sb("shrink", [P, STEPS])
        k.q_now, k.k_now, k.nk_now, k.v_now = (sb(n, [P, STEPS, DN]) for n in ("q_now", "k_now", "nk_now", "v_now"))
        k.w_now = sb("w_now", [P, QB, E])
        k.prod = sb("prod", [P, DN, DN])
        k.delta = sb("delta", [P, DN])
        k.peak = sb("peak", [P, 1])
        k.o_part = sb("o_part", [P, PART, DN, DN])
        k.o_now = sb("o_now", [P, DN, STEPS])
        with ExitStack() as ld:
            st = Stage(nc, ld, "l2l")
            loaded, zeroed = st.sems("loaded", "zeroed")
            pairs = [(k.w1[:, e, :], w["L2_ffn_W1"][e]) for e in range(E)]
            pairs += [(k.w2[:, e, :, :], w["L2_ffn_W2"][e].rearrange("(f p) d -> p f d", p=P)) for e in range(E)]
            pairs += [(k.b1[:], w["L2_ffn_b1T"])]
            with nc.Block() as block:
                @block.sync
                def _(sp):
                    for dst, src in pairs:
                        sp.dma_start(dst, src).then_inc(loaded, 16)
                    sp.wait_ge(loaded, 16 * len(pairs))

                @block.vector
                def _(dve):
                    nc.vector.memset(k.raw[:, 1, PART - 1], 0.0).then_inc(zeroed, 1)
                    nc.vector.memset(k.shrink[:, STEPS - 1:STEPS], 1.0).then_inc(zeroed, 1)
            st.end()
        with nc.Fori(0, NB) as b:
            delta_and_experts(nc, c, w, b, k, o_dram)
    delta_output(nc, c, w, o_dram)


def rms_stage(nc, c, w, name, add, gain):
    with ExitStack() as ctx:
        st = Stage(nc, ctx, name)
        loaded, summed, squared, var_ready, rooted, dve_done, normed, turned, copied = st.sems(
            "loaded", "summed", "squared", "var_ready", "rooted", "dve_done", "normed", "turned", "copied")
        gain_col = st.sb("gain", [P, 1])
        squares = st.sb("squares", [P, D])
        mean = st.sb("mean", [P, TB])
        scaled = st.sb("scaled", [P, TB, D])
        src = c.g if add else c.xn
        with nc.Block() as block:
            @block.sync
            def _(sp):
                sp.dma_start(gain_col[:], column(gain)).then_inc(loaded, 16)

            @block.vector
            def _(dve):
                chain = Chain(dve, dve_done)
                if add:
                    nc.vector.tensor_tensor(c.g[:], c.g[:], c.xn[:], ALU.add).then_inc(summed, 1)
                dve.wait_ge(squared, TB)
                nc.vector.tensor_scalar(mean[:], mean[:], 1.0 / D, RMS_EPS, ALU.mult, ALU.add).then_inc(var_ready, 1)
                dve.wait_ge(rooted, 1)
                chain.link(nc.vector.reciprocal(mean[:], mean[:]))
                for t in range(TB):
                    nc.vector.tensor_scalar(scaled[:, t, :], src[:, t, :], mean[:, t:t + 1], None,
                                            ALU.mult).then_inc(normed, 1)

            @block.tensor
            def _(pe):
                for b in range(NB):
                    pe.wait_ge(normed, QB * (b + 1))
                    if b >= 4:
                        pe.wait_ge(copied, b - 3)
                    for q in range(QB):
                        last = nc.tensor.transpose(c.ps[b % 4][:, q * P:(q + 1) * P], scaled[:, b * QB + q, :],
                                                   c.ident[:])
                    last.then_inc(turned, 1)

            @block.scalar
            def _(act):
                if add:
                    act.wait_ge(summed, 1)
                for t in range(TB):
                    if t > 0:
                        act.wait_ge(squared, t)
                    nc.scalar.activation(squares[:], src[:, t, :], ACT.Square,
                                         accum_out=mean[:, t:t + 1]).then_inc(squared, 1)
                act.wait_ge(var_ready, 1)
                nc.scalar.activation(mean[:], mean[:], ACT.Sqrt).then_inc(rooted, 1)
                act.wait_ge(loaded, 16)
                for b in range(NB):
                    act.wait_ge(turned, b + 1)
                    nc.scalar.activation(c.xnT[:, b, :], c.ps[b % 4][:], ACT.Copy,
                                         scale=gain_col[:]).then_inc(copied, 1)
        st.end()


def load_heads(q_dram, k_dram, k):
    def load(sp, b, buffer, loaded):
        for dram, dst, part_of in ((q_dram, k.QT[buffer], lambda p: p // 2), (k_dram, k.KT[buffer], lambda p: p % 2)):
            for j in range(4):
                for p in range(4):
                    rows = slice(PACK * j + DN * p, PACK * j + DN * (p + 1))
                    heads = dram[part_of(p)].rearrange("(g j d) b t -> j d g b t", j=4, d=DN)[j]
                    sp.dma_start(dst[rows, :, :], heads[:, :, b, :]).then_inc(loaded, 16)
    return load


def narrow_attention(nc, c, name, project, wo, dst):
    with ExitStack() as ctx:
        a = Heads(name, DN, causal=True, dst=dst)
        q_dram, k_dram = (nc.dram_tensor(f"{name}_{n}T", (2, D, NB + 1, S), F32, kind="Internal").ap() for n in "qk")
        values = ctx.enter_context(nc.sbuf_tensor(f"{name}_values", [P, TB, D], F32))
        project(q_dram, k_dram, values)
        k = Work(nc, ctx, a)
        k.QT = [k.sb(f"QT{i}", [P, 4, S]) for i in range(2)]
        k.KT = [k.sb(f"KT{i}", [P, 4, S]) for i in range(2)]
        k.V = [k.sb(f"V{i}", [P, QB, D]) for i in range(2)]
        k.source = values
        k.n_loads = 32
        load = load_heads(q_dram, k_dram, k)
        with ExitStack() as ld:
            st = Stage(nc, ld, name + "l")
            (loaded,) = st.sems("loaded")
            with nc.Block() as block:
                @block.sync
                def _(sp):
                    sp.dma_start(k.wo[:], wo.rearrange("(t p) d -> p t d", p=P)).then_inc(loaded, 16)
                    load(sp, 0, 0, loaded)
                    sp.wait_ge(loaded, 16 * (k.n_loads + 1))
            st.end()
        with nc.Fori(0, NB // a.batches) as pair:
            attention_stage(nc, c, a, pair * a.batches, k, load_qkv=load)


def top2_routing(nc, c, w, weight):
    with ExitStack() as ctx:
        st = Stage(nc, ctx, "r3")
        loaded, made, dve_done, less, exped = st.sems("loaded", "made", "dve_done", "less", "exped")
        router = st.sb("router", [P, E])
        prob = st.sb("prob", [P, TB, E])
        rank = st.sb("rank", [P, TB, E])
        over = st.sb("over", [P, TB, E])
        total = st.sb("total", [P, TB, 1])

        def spread(t, n=E):
            return t.broadcast_to([P, TB, n])

        with nc.Block() as block:
            @block.sync
            def _(sp):
                sp.dma_start(router[:], w["L3_ffn_w_router"]).then_inc(loaded, 16)

            @block.tensor
            def _(pe):
                pe.wait_ge(loaded, 16)
                for t in range(TB):
                    last = nc.tensor.matmul(c.ps[0][:, t * E:(t + 1) * E],
                                            c.xnT[:, t // QB, (t % QB) * P:(t % QB + 1) * P], router[:],
                                            start=True, stop=True)
                last.then_inc(made, 1)

            @block.scalar
            def _(act):
                act.wait_ge(less, 1)
                nc.scalar.activation(prob[:], prob[:], ACT.Exp).then_inc(exped, 1)

            @block.vector
            def _(dve):
                chain = Chain(dve, dve_done)
                dve.wait_ge(made, 1)
                logits = c.ps[0][:, 0:TB * E].rearrange("p (t e) -> p t e", e=E)
                chain.link(nc.vector.tensor_reduce(total[:], logits, AX, ALU.max))
                nc.vector.tensor_tensor(prob[:], logits, spread(total[:]), ALU.subtract).then_inc(less, 1)
                dve.wait_ge(exped, 1)
                chain.link(nc.vector.tensor_reduce(total[:], prob[:], AX, ALU.add))
                chain.link(nc.vector.reciprocal(total[:], total[:]))
                chain.link(nc.vector.tensor_tensor(prob[:], prob[:], spread(total[:]), ALU.mult))
                chain.link(nc.vector.memset(rank[:], 0.0))
                for j in range(E):
                    pj = prob[:, :, j:j + 1]
                    chain.link(nc.vector.tensor_tensor(over[:], spread(pj), prob[:], ALU.is_gt))
                    chain.link(nc.vector.tensor_tensor(rank[:], rank[:], over[:], ALU.add))
                    if j < E - 1:
                        behind = slice(j + 1, E)
                        chain.link(nc.vector.tensor_tensor(over[:, :, behind], spread(pj, E - 1 - j),
                                                           prob[:, :, behind], ALU.is_equal))
                        chain.link(nc.vector.tensor_tensor(rank[:, :, behind], rank[:, :, behind],
                                                           over[:, :, behind], ALU.add))
                chain.link(nc.vector.tensor_scalar(rank[:], rank[:], 2.0, None, ALU.is_lt))
                chain.link(nc.vector.tensor_tensor(prob[:], prob[:], rank[:], ALU.mult))
                chain.link(nc.vector.tensor_reduce(total[:], prob[:], AX, ALU.add))
                chain.link(nc.vector.reciprocal(total[:], total[:]))
                nc.vector.tensor_tensor(weight[:], prob[:], spread(total[:]), ALU.mult).then_inc(dve_done, 1)
        st.end()


def gated_experts(nc, c, b, k):
    h_tiles = HID // P
    with ExitStack() as ctx:
        st = Stage(nc, ctx, "m3")
        staged, up_done, silued, hid_ready, down_done, acc_done = st.sems(
            "staged", "up_done", "silued", "hid_ready", "down_done", "acc_done")
        with nc.Block(no_gpsimd_drain=True) as block:
            @block.tensor
            def _(pe):
                for e in range(E + 1):
                    if e < E:
                        for f in range(h_tiles):
                            n = e * h_tiles + f
                            if n >= 2:
                                pe.wait_ge(hid_ready, n - 1)
                            cols = slice(f * P, (f + 1) * P)
                            nc.tensor.matmul(c.ps[n % 2][:], k.wg[:, e, cols], c.xnT[:, b, :], start=True,
                                             stop=True).then_inc(up_done, 1)
                            nc.tensor.matmul(c.ps[2 + n % 2][:], k.wu[:, e, cols], c.xnT[:, b, :], start=True,
                                             stop=True).then_inc(up_done, 1)
                    if e > 0:
                        d = e - 1
                        pe.wait_ge(hid_ready, h_tiles * (d + 1))
                        if d >= 2:
                            pe.wait_ge(acc_done, QB * (d - 1))
                        for q in range(QB):
                            for f in range(h_tiles):
                                last = nc.tensor.matmul(c.ps[4 + d % 2][:, q * P:(q + 1) * P],
                                                        k.hT[:, d % 2, f, q * P:(q + 1) * P], k.wd[:, d, f, :],
                                                        start=f == 0, stop=f == h_tiles - 1)
                        last.then_inc(down_done, 1)

            @block.scalar
            def _(act):
                for n in range(E * h_tiles):
                    act.wait_ge(up_done, 2 * n + 1)
                    if n >= 2:
                        act.wait_ge(hid_ready, n - 1)
                    nc.scalar.activation(k.act[:, n % 2, :], c.ps[n % 2][:], ACT.Silu).then_inc(silued, 1)

            @block.vector
            def _(dve):
                nc.vector.tensor_copy(k.w_now[:], k.weight[:, bass.ts(b, QB), :]).then_inc(staged, 1)
                nc.vector.tensor_copy(k.acc[:], c.g[:, bass.ts(b, QB), :]).then_inc(staged, 1)
                dve.wait_ge(staged, 2)
                for e in range(E + 1):
                    if e < E:
                        for f in range(h_tiles):
                            n = e * h_tiles + f
                            dve.wait_ge(silued, n + 1)
                            dve.wait_ge(up_done, 2 * n + 2)
                            if e >= 2 and f == 0:
                                dve.wait_ge(down_done, e - 1)
                            nc.vector.tensor_tensor(k.hT[:, e % 2, f, :], c.ps[2 + n % 2][:], k.act[:, n % 2, :],
                                                    ALU.mult).then_inc(hid_ready, 1)
                    if e > 0:
                        d = e - 1
                        dve.wait_ge(down_done, d + 1)
                        if d >= 1:
                            dve.wait_ge(acc_done, QB * d)
                        for q in range(QB):
                            last = nc.vector.scalar_tensor_tensor(out=k.acc[:, q, :],
                                                                  in0=c.ps[4 + d % 2][:, q * P:(q + 1) * P],
                                                                  scalar=k.w_now[:, q, d:d + 1], in1=k.acc[:, q, :],
                                                                  op0=ALU.mult, op1=ALU.add)
                            last.then_inc(acc_done, 1)
                dve.wait_ge(acc_done, QB * E)
                nc.vector.tensor_copy(c.g[:, bass.ts(b, QB), :], k.acc[:]).then_inc(staged, 1)
        st.end()


class ExpertWork:
    pass


def layer3(nc, c, w):
    def plain(q_dram, k_dram, values):
        project_stage(nc, c, "p3", c.xnT, [(w["L3_attn_Wqvk"][:, 0:D], None, D ** -0.5, q_dram),
                                           (w["L3_attn_Wqvk"][:, 2 * D:3 * D], None, 1.0, k_dram)],
                      value=(w["L3_attn_Wqvk"][:, D:2 * D], values), split=True)

    def rotary(q_dram, k_dram, values):
        rms_stage(nc, c, w, "rms1", False, w["L3_ffn_g1"])
        tables = [w["rope_q_cos"], w["rope_q_sin"]], [w["rope_k_cos"], w["rope_k_sin"]]
        project_stage(nc, c, "p4", c.xnT,
                      [((w["L3_ffn_wq"], w["L3_ffn_wq_turned"]), None, tables[0], q_dram),
                       ((w["L3_ffn_wk"], w["L3_ffn_wk_turned"]), None, tables[1], k_dram)],
                      value=(w["L3_ffn_wv"], values), rope=True, split=True)

    narrow_attention(nc, c, "a3", plain, w["L3_attn_Wo"], c.s)
    narrow_attention(nc, c, "a4", rotary, w["L3_ffn_wo"], c.g)
    rms_stage(nc, c, w, "rms2", True, w["L3_ffn_g2"])
    with ExitStack() as ctx:
        def sb(name, shape, dt=F32):
            return ctx.enter_context(nc.sbuf_tensor(f"l3_{name}", shape, dt))

        h_tiles = HID // P
        k = ExpertWork()
        k.weight = sb("weight", [P, TB, E])
        top2_routing(nc, c, w, k.weight)
        k.wg, k.wu = sb("wg", [P, E, HID]), sb("wu", [P, E, HID])
        k.wd = sb("wd", [P, E, h_tiles, D])
        k.hT = sb("hT", [P, 2, h_tiles, S])
        k.act = sb("act", [P, 2, S])
        k.acc = sb("acc", [P, QB, D])
        k.w_now = sb("w_now", [P, QB, E])
        with ExitStack() as ld:
            st = Stage(nc, ld, "l3l")
            (loaded,) = st.sems("loaded")
            pairs = []
            for e in range(E):
                pairs += [(k.wg[:, e, :], w["L3_ffn_wg"][e]), (k.wu[:, e, :], w["L3_ffn_wu"][e]),
                          (k.wd[:, e, :, :], w["L3_ffn_wd"][e].rearrange("(f p) d -> p f d", p=P))]
            load_all(st, loaded, pairs)
        with nc.Fori(0, NB) as b:
            gated_experts(nc, c, b, k)
    with ExitStack() as ctx:
        st = Stage(nc, ctx, "g3")
        (silued,) = st.sems("silued")
        with nc.Block() as block:
            @block.scalar
            def _(act):
                nc.scalar.activation(c.g[:], c.g[:], ACT.Silu).then_inc(silued, 1)
        st.end()


class Buffers:

    def __init__(self, nc, ctx):
        def sb(name, shape, dt=F32):
            return ctx.enter_context(nc.sbuf_tensor(name, shape, dt))

        self.x = sb("x", [P, TB, D])
        self.xn = sb("xn", [P, TB, D])
        self.xnT = sb("xnT", [P, NB, S])
        self.s = sb("s", [P, TB, D])
        self.g = sb("g", [P, TB, D])
        self.ident = sb("ident", [P, P])
        self.ident16 = sb("ident16", [P, P], BF16)
        self.mask16 = sb("mask16", [P, P], BF16)
        self.ones = sb("ones", [P, P])
        self.table = nc.dram_tensor("table", (H, NPOS), F32, kind="Internal").ap()
        self.ps = [ctx.enter_context(nc.psum_tensor(f"ps{i}", [P, 512], F32)) for i in range(8)]


def build(nc, w, out):
    with ExitStack() as ctx:
        c = Buffers(nc, ctx)
        with ExitStack() as ld:
            st = Stage(nc, ld, "load")
            (loaded,) = st.sems("loaded")
            load_all(st, loaded, [(c.x[:, b * QB:(b + 1) * QB, :],
                                   w["L0_attn_latents"][b].rearrange("(q p) d -> p q d", p=P)) for b in range(NB)])
        make_constants(nc, c)

        with ExitStack() as early:
            c.xaT = early.enter_context(nc.sbuf_tensor("xaT", [P, NB, S], F32))
            norm_stage(nc, c, "n0", False, second=(w["L0_attn_ln_gamma"], w["L0_attn_ln_beta"]))
            recurrent_gate(nc, c, w)
            attention0(nc, c, w, c.xaT)

            norm_stage(nc, c, "n1", True, second=(w["L1_attn_ln_g"], w["L1_attn_ln_b"]))
            ternary_gate(nc, c, w)
            attention1(nc, c, w, c.xaT)

        norm_stage(nc, c, "n2", True, affine_s=(w["L1_attn_out_ln_g"], w["L1_attn_out_ln_b"]))
        layer2(nc, c, w)

        norm_stage(nc, c, "n3", True)
        layer3(nc, c, w)
        final_stage(nc, c, out)


_TRANSPOSED = ([f"L0_ffn_{n}" for n in ("wf", "uf", "wi", "ui", "wc", "uc", "wo", "uo")]
               + ["L1_ffn_W1", "L1_ffn_W2"] + [f"L2_attn_W{n}" for n in "qkvo"])
_TILED_BIASES = ("L1_ffn_b1", "L2_ffn_b1")


def _rope_tables():
    inv_freq = 1.0 / 10000.0 ** (np.arange(0, DN, 2, dtype=np.float32) / DN)
    freqs = np.einsum("i,j->ij", np.arange(S, dtype=np.float32), inv_freq)
    emb = np.concatenate([freqs, freqs], axis=-1).astype(np.float32)
    sign = np.where(np.arange(DN) < DN // 2, -1.0, 1.0).astype(np.float32)
    cos = np.tile(np.cos(emb).T, (H, 1)).astype(np.float32)
    sin = np.tile(np.sin(emb).T * sign[:, None], (H, 1)).astype(np.float32)
    scale = np.float32(DN ** -0.5)
    return {"rope_k_cos": cos, "rope_k_sin": sin, "rope_q_cos": cos * scale, "rope_q_sin": sin * scale}


def kernel(**inputs):
    import concourse.bacc as _bacc
    from concourse.bass_utils import run_bass_kernel_spmd as _run

    nc = _bacc.Bacc("TRN2", target_bir_lowering=False, num_devices=1)
    laid = {}
    for name, value in inputs.items():
        a = np.asarray(value)
        if name in _TRANSPOSED:
            laid[name + "T"] = a.T
        elif name in _TILED_BIASES:
            tiled = a.reshape(a.shape[:-1] + (a.shape[-1] // P, P))
            laid[name + "T"] = np.moveaxis(tiled, -1, 0)
        else:
            laid[name] = a
        if name in ("L3_ffn_wq", "L3_ffn_wk"):
            laid[name + "_turned"] = a.reshape(D, H, 2, DN // 2)[:, :, ::-1, :].reshape(D, D)
    laid.update(_rope_tables())
    arrays, w = {}, {}
    for name, a in laid.items():
        a = np.ascontiguousarray(a)
        arrays[f"in_{name}_dram"] = a
        w[name] = nc.dram_tensor(f"in_{name}_dram", a.shape, mybir.dt.from_np(a.dtype), kind="ExternalInput").ap()
    out = nc.dram_tensor("out_0_dram", (NB, S, D), F32, kind="ExternalOutput").ap()
    build(nc, w, out)
    r = _run(nc, [arrays], core_ids=[0])
    return r.results[0]["out_0_dram"]
```

```python
from contextlib import ExitStack

import numpy as np

import concourse.bass as bass
from concourse import mybir

F32 = mybir.dt.float32
BF16 = mybir.dt.bfloat16
F32R = mybir.dt.float32r
I32 = mybir.dt.int32
UPPER = -4096
ALU = mybir.AluOpType
ACT = mybir.ActivationFunctionType
AX = mybir.AxisListType.X

P = 128
NB, S, D = 8, 512, 128
QB = S // P
TB = NB * QB
H = 16
DH = 64
DN = D // H
FF = 512
E = 8
PACK = 4 * DN
HID = 384
LN_EPS = 1e-5
RMS_EPS = 1e-6
FIRST_SEM = 120
MASKED = 1e30
NPOS = 640


class Stage:

    def __init__(self, nc, ctx, name):
        self.nc, self.ctx, self.name, self.nums = nc, ctx, name, []

    def sems(self, *names):
        handles = []
        for n in names:
            num = FIRST_SEM + len(self.nums)
            handles.append(self.ctx.enter_context(self.nc.semaphore(f"{self.name}_{n}", num=num)))
            self.nums.append(num)
        return handles

    def sb(self, name, shape, dt=F32):
        return self.ctx.enter_context(self.nc.sbuf_tensor(f"{self.name}_{name}", shape, dt))

    def end(self):
        self.nc.all_engine_barrier(sems_to_clear=range(self.nums[0], self.nums[-1] + 1))


class Chain:

    def __init__(self, eng, sem):
        self.eng, self.sem, self.n = eng, sem, 0

    def mark(self, ins):
        ins.then_inc(self.sem, 1)
        self.n += 1

    def wait(self):
        self.eng.wait_ge(self.sem, self.n)

    def link(self, ins):
        self.mark(ins)
        self.wait()


def row_bcast(ap, n, parts=P):
    return bass.AP(tensor=ap.tensor, offset=ap.offset, ap=[[0, parts], [1, n]])


def column(ap):
    return ap.rearrange("(p o) -> p o", o=1)


def over_tokens(stat, n=D):
    return stat.broadcast_to([P, stat.shape[1], n])


def over_blocks(row, n=TB):
    return row.unsqueeze(1).broadcast_to([P, n, row.shape[1]])


def load_all(st, loaded, pairs, clear=()):
    nc = st.nc
    with nc.Block() as block:
        @block.sync
        def _(sp):
            for dst, src in pairs:
                sp.dma_start(dst, src).then_inc(loaded, 16)
            sp.wait_ge(loaded, 16 * len(pairs))

        if clear:
            @block.vector
            def _(dve):
                for part, zeroed in clear:
                    nc.vector.memset(part, 0.0).then_inc(zeroed, 1)
    st.end()


def make_constants(nc, c):
    with ExitStack() as ctx:
        st = Stage(nc, ctx, "const")
        filled, shaped, narrowed = st.sems("filled", "shaped", "narrowed")
        mask = st.sb("mask", [P, P])
        with nc.Block() as block:
            @block.gpsimd
            def _(pool):
                nc.gpsimd.memset(c.ident[:], 0.0).then_inc(filled, 1)
                nc.gpsimd.memset(mask[:], 0.0).then_inc(filled, 1)
                nc.gpsimd.memset(c.ones[:], 1.0).then_inc(filled, 1)
                pool.wait_ge(filled, 3)
                nc.gpsimd.affine_select(out=c.ident[:], in_=c.ident[:], compare_op=ALU.not_equal, fill=1.0,
                                        base=0, pattern=[[-1, P]], channel_multiplier=1).then_inc(shaped, 1)
                nc.gpsimd.affine_select(out=mask[:], in_=mask[:], compare_op=ALU.is_ge, fill=-MASKED,
                                        base=0, pattern=[[-1, P]], channel_multiplier=1).then_inc(shaped, 1)

            @block.vector
            def _(dve):
                dve.wait_ge(shaped, 2)
                nc.vector.tensor_copy(c.ident16[:], c.ident[:]).then_inc(narrowed, 1)
                nc.vector.tensor_copy(c.mask16[:], mask[:]).then_inc(narrowed, 1)
        st.end()


GROUPS = 4
BLOCKS = TB // GROUPS
BY_DVE = BLOCKS // 4


def norm_stage(nc, c, name, combine, affine_s=None, second=None):
    if affine_s is not None:
        items = [("s", 0), ("s", 1), ("s", 2), ("x", 0), ("s", 3), ("x", 1), ("x", 2), ("x", 3)]
    elif second is not None:
        items = [("x", 0), ("x", 1), ("x", 2), ("a", 0), ("x", 3), ("a", 1), ("a", 2), ("a", 3)]
    else:
        items = [("x", g) for g in range(GROUPS)]
    place = {item: i for i, item in enumerate(items)}
    turns = [item for item in items if item[0] != "s"]
    with ExitStack() as ctx:
        st = Stage(nc, ctx, name)
        (var_ready, root_ready, factor_ready, dve_applied, act_applied, dve_done, pool_done, summed, turned, copied, loaded) = st.sems(
            "var_ready", "root_ready", "factor_ready", "dve_applied", "act_applied", "dve_done", "pool_done", "summed", "turned",
            "copied", "loaded")
        again = st.sb("again", [P, TB, D]) if second else None
        source = {"s": c.s, "x": c.x, "a": c.xn}
        target = {"s": c.s, "x": c.xn, "a": again}
        kinds = {kind for kind, _ in items}
        stats = {kind: st.sb("stats_" + kind, [P, TB, 6]) for kind in kinds}
        mv = {kind: st.sb("mv_" + kind, [P, TB, 2]) for kind in kinds}
        root = {kind: st.sb("root_" + kind, [P, TB, 1]) for kind in kinds}
        factor = {kind: st.sb("factor_" + kind, [P, TB, 1]) for kind in kinds}
        shift = {kind: st.sb("shift_" + kind, [P, TB, 1]) for kind in kinds}
        rows = []
        if affine_s is not None:
            rows = [(st.sb("s_gain", [P, D]), row_bcast(affine_s[0], D)),
                    (st.sb("s_shift", [P, D]), row_bcast(affine_s[1], D))]
        if second is not None:
            rows += [(st.sb("a_gain", [P, 1]), column(second[0])), (st.sb("a_shift", [P, 1]), column(second[1]))]

        def span(g):
            return slice(g * BLOCKS, (g + 1) * BLOCKS)

        def wait_normed(eng, item):
            eng.wait_ge(dve_applied, place[item] + 1)
            eng.wait_ge(act_applied, place[item] + 1)

        with nc.Block() as block:
            @block.sync
            def _(sp):
                for dst, src in rows:
                    sp.dma_start(dst[:], src).then_inc(loaded, 16)

            if combine:
                @block.gpsimd
                def _(pool):
                    if affine_s is not None:
                        pool.wait_ge(loaded, 16 * len(rows))
                    for g in range(GROUPS):
                        s, gate = c.s[:, span(g), :], c.g[:, span(g), :]
                        if affine_s is not None:
                            wait_normed(pool, ("s", g))
                            nc.gpsimd.tensor_tensor(s, s, over_blocks(rows[0][0][:], BLOCKS),
                                                    ALU.mult).then_inc(pool_done, 1)
                        else:
                            nc.gpsimd.tensor_tensor(gate, s, gate, ALU.mult).then_inc(pool_done, 1)

            @block.vector
            def _(dve):
                chain = Chain(dve, dve_done)
                if affine_s is not None:
                    dve.wait_ge(loaded, 16 * len(rows))

                def add_up(g):
                    s, gate, x = (t[:, span(g), :] for t in (c.s, c.g, c.x))
                    dve.wait_ge(pool_done, g + 1)
                    if affine_s is not None:
                        chain.link(nc.vector.tensor_tensor(s, s, over_blocks(rows[1][0][:], BLOCKS), ALU.add))
                        chain.link(nc.vector.tensor_tensor(gate, s, gate, ALU.mult))
                    chain.link(nc.vector.tensor_tensor(x, x, gate, ALU.add))

                def finish(i):
                    kind, g = items[i]
                    at = span(g)
                    dve.wait_ge(root_ready, i + 1)
                    chain.link(nc.vector.reciprocal(factor[kind][:, at], root[kind][:, at]))
                    nc.vector.scalar_tensor_tensor(out=shift[kind][:, at], in0=mv[kind][:, at, 0:1], scalar=-1.0,
                                                   in1=factor[kind][:, at], op0=ALU.mult,
                                                   op1=ALU.mult).then_inc(factor_ready, 1)
                    dve.wait_ge(factor_ready, i + 1)
                    for t in range(g * BLOCKS, g * BLOCKS + BY_DVE):
                        last = nc.vector.tensor_scalar(target[kind][:, t, :], source[kind][:, t, :],
                                                       factor[kind][:, t, :], shift[kind][:, t, :], ALU.mult, ALU.add)
                    last.then_inc(dve_applied, 1)

                for i, (kind, g) in enumerate(items):
                    if kind == "a":
                        wait_normed(dve, ("x", g))
                    if kind == "x" and combine:
                        add_up(g)
                    for t in range(g * BLOCKS, (g + 1) * BLOCKS):
                        chain.mark(nc.vector.bn_stats(stats[kind][:, t, :], source[kind][:, t, :]))
                    chain.wait()
                    for t in range(g * BLOCKS, (g + 1) * BLOCKS):
                        chain.mark(nc.vector.bn_aggr(mv[kind][:, t, :], stats[kind][:, t, :]))
                    chain.wait()
                    nc.vector.tensor_scalar(root[kind][:, span(g)], mv[kind][:, span(g), 1:2], LN_EPS, None,
                                            ALU.add).then_inc(var_ready, 1)
                    if i > 0:
                        finish(i - 1)
                finish(len(items) - 1)

            @block.tensor
            def _(pe):
                n = 0
                for kind, g in turns:
                    wait_normed(pe, (kind, g))
                    for b in range(g * BLOCKS // QB, (g + 1) * BLOCKS // QB):
                        if n >= 4:
                            pe.wait_ge(copied, n - 3)
                        for q in range(QB):
                            last = nc.tensor.transpose(c.ps[n % 4][:, q * P:(q + 1) * P],
                                                       target[kind][:, b * QB + q, :], c.ident[:])
                        last.then_inc(turned, 1)
                        n += 1

            @block.scalar
            def _(act):
                if second is not None:
                    act.wait_ge(loaded, 16 * len(rows))
                n = 0
                for i in range(len(items) + 2):
                    if i < len(items):
                        kind, g = items[i]
                        act.wait_ge(var_ready, i + 1)
                        nc.scalar.activation(root[kind][:, span(g)], root[kind][:, span(g)],
                                             ACT.Sqrt).then_inc(root_ready, 1)
                    if 0 < i <= len(items):
                        kind, g = items[i - 1]
                        act.wait_ge(factor_ready, i)
                        for t in range(g * BLOCKS + BY_DVE, (g + 1) * BLOCKS):
                            last = nc.scalar.activation(target[kind][:, t, :], source[kind][:, t, :], ACT.Identity,
                                                        bias=shift[kind][:, t, :], scale=factor[kind][:, t, :])
                        last.then_inc(act_applied, 1)
                    if i > 1 and items[i - 2] in turns:
                        kind, g = items[i - 2]
                        for b in range(g * BLOCKS // QB, (g + 1) * BLOCKS // QB):
                            act.wait_ge(turned, n + 1)
                            if kind == "x":
                                nc.scalar.activation(c.xnT[:, b, :], c.ps[n % 4][:], ACT.Copy).then_inc(copied, 1)
                            else:
                                nc.scalar.activation(c.xaT[:, b, :], c.ps[n % 4][:], ACT.Identity,
                                                     bias=rows[-1][0][:], scale=rows[-2][0][:]).then_inc(copied, 1)
                            n += 1
        st.end()


def final_stage(nc, c, out):
    with ExitStack() as ctx:
        st = Stage(nc, ctx, "final")
        silued, product, ready, stored = st.sems("silued", "product", "ready", "stored")
        with nc.Block() as block:
            @block.scalar
            def _(act):
                for b in range(NB):
                    g = c.g[:, b * QB:(b + 1) * QB, :]
                    nc.scalar.activation(g, g, ACT.Silu).then_inc(silued, 1)

            @block.vector
            def _(dve):
                for b in range(NB):
                    g, s, x = (t[:, b * QB:(b + 1) * QB, :] for t in (c.g, c.s, c.x))
                    dve.wait_ge(silued, b + 1)
                    nc.vector.tensor_tensor(g, s, g, ALU.mult).then_inc(product, 1)
                    dve.wait_ge(product, b + 1)
                    nc.vector.tensor_tensor(x, x, g, ALU.add).then_inc(ready, 1)

            @block.sync
            def _(sp):
                for b in range(NB):
                    sp.wait_ge(ready, b + 1)
                    sp.dma_start(out[b].rearrange("(q p) d -> p q d", p=P),
                                 c.x[:, b * QB:(b + 1) * QB, :]).then_inc(stored, 16)
                sp.wait_ge(stored, 16 * NB)
        st.end()


def recurrent_gate(nc, c, w):
    with ExitStack() as ctx:
        st = Stage(nc, ctx, "g0")
        loaded, xpart, cpart, gated, dve_done, cready, cu_ready, cu_added, h_ready, h_added, tanhed = st.sems(
            "loaded", "xpart", "cpart", "gated", "dve_done", "cready", "cu_ready", "cu_added", "h_ready", "h_added",
            "tanhed")
        names = ["wf", "uf", "wi", "ui", "wc", "uc", "wo", "uo"]
        wt = {n: st.sb(n, [P, D]) for n in names}
        bias = {n: st.sb(n, [P, 1]) for n in ("bf", "bi", "bc")}
        bo_row = st.sb("bo_row", [P, D])
        c_first = st.sb("c_first", [P, 1])
        cT = st.sb("cT", [P, 2, S])
        gate = st.sb("gate", [P, 2, 3, S])
        keep = st.sb("keep", [P, S])
        cu = st.sb("cu", [P, QB, D])
        n_loads = len(names) + 3 + 2

        with nc.Block() as block:
            @block.sync
            def _(sp):
                for n in names:
                    sp.dma_start(wt[n][:], w[f"L0_ffn_{n}T"]).then_inc(loaded, 16)
                for n in bias:
                    sp.dma_start(bias[n][:], column(w[f"L0_ffn_{n}"])).then_inc(loaded, 16)
                sp.dma_start(c_first[:], column(w["L0_ffn_in_c"])).then_inc(loaded, 16)
                sp.dma_start(bo_row[:], row_bcast(w["L0_ffn_bo"], D)).then_inc(loaded, 16)

            @block.tensor
            def _(pe):
                pe.wait_ge(loaded, 16 * n_loads)
                for t in range(NB):
                    if t >= 2:
                        pe.wait_ge(gated, 3 * (t - 1))
                    pe.wait_ge(cready, t + 1)
                    for k, n in enumerate("fic"):
                        bank = c.ps[3 * (t % 2) + k]
                        nc.tensor.matmul(bank[:], wt["w" + n][:], c.xnT[:, t, :], start=True, stop=False)
                        nc.tensor.matmul(bank[:], wt["u" + n][:], cT[:, t % 2, :], start=False,
                                         stop=True).then_inc(cpart, 1)
                pe.wait_ge(cready, NB + 1)
                for q in range(QB):
                    last = nc.tensor.matmul(c.ps[6][:, q * P:(q + 1) * P], cT[:, NB % 2, q * P:(q + 1) * P],
                                            wt["uo"][:], start=True, stop=True)
                last.then_inc(cu_ready, 1)
                for b in range(NB):
                    if b == 0:
                        pe.wait_ge(gated, 3 * NB)
                    if b >= 4:
                        pe.wait_ge(h_added, b - 3)
                    for q in range(QB):
                        last = nc.tensor.matmul(c.ps[b % 4][:, q * P:(q + 1) * P], c.xnT[:, b, q * P:(q + 1) * P],
                                                wt["wo"][:], start=True, stop=True)
                    last.then_inc(h_ready, 1)

            @block.scalar
            def _(act):
                act.wait_ge(loaded, 16 * n_loads)
                for t in range(NB):
                    for k, n in enumerate("fic"):
                        act.wait_ge(cpart, 3 * t + k + 1)
                        if t >= 2 and k == 0:
                            act.wait_ge(cready, t)
                        nc.scalar.activation(gate[:, t % 2, k, :], c.ps[3 * (t % 2) + k][:],
                                             ACT.Tanh if n == "c" else ACT.Sigmoid,
                                             bias=bias["b" + n][:]).then_inc(gated, 1)
                for b in range(NB):
                    act.wait_ge(h_added, b + 1)
                    g = c.g[:, b * QB:(b + 1) * QB, :]
                    nc.scalar.activation(g, g, ACT.Tanh).then_inc(tanhed, 1)
                act.wait_ge(tanhed, NB)
                nc.scalar.activation(c.g[:], c.g[:], ACT.Silu).then_inc(tanhed, 1)

            @block.vector
            def _(dve):
                chain = Chain(dve, dve_done)
                dve.wait_ge(loaded, 16 * n_loads)
                chain.link(nc.vector.memset(keep[:], 0.0))
                nc.vector.tensor_scalar(cT[:, 0, :], keep[:], c_first[:], None, ALU.add).then_inc(cready, 1)
                for t in range(NB):
                    f, i, g = (gate[:, t % 2, k, :] for k in range(3))
                    dve.wait_ge(gated, 3 * t + 1)
                    dve.wait_ge(cready, t + 1)
                    chain.mark(nc.vector.tensor_tensor(keep[:], f, cT[:, t % 2, :], ALU.mult))
                    dve.wait_ge(gated, 3 * t + 3)
                    chain.link(nc.vector.tensor_tensor(i, i, g, ALU.mult))
                    nc.vector.tensor_tensor(cT[:, (t + 1) % 2, :], keep[:], i, ALU.add).then_inc(cready, 1)
                dve.wait_ge(cu_ready, 1)
                nc.vector.tensor_tensor(cu[:], c.ps[6][:].rearrange("p (q d) -> p q d", d=D),
                                        over_blocks(bo_row[:], QB), ALU.add).then_inc(cu_added, 1)
                dve.wait_ge(cu_added, 1)
                for b in range(NB):
                    dve.wait_ge(h_ready, b + 1)
                    nc.vector.tensor_tensor(c.g[:, b * QB:(b + 1) * QB, :],
                                            c.ps[b % 4][:].rearrange("p (q d) -> p q d", d=D), cu[:],
                                            ALU.add).then_inc(h_added, 1)
        st.end()


UNITS = QB * H
GROUP = 4
LAG_T, LAG_AV = 3, 4
PROBS = LAG_T + 1
S_BANKS, T_BANK, O_BANK, Y_BANK = 3, 3, 5, 7


class Heads:

    def __init__(self, name, width, causal, bias=None, shared_kv=False, projected=False, dst=None):
        self.name, self.width, self.causal = name, width, causal
        self.bias = bias
        self.shared_kv = shared_kv
        self.projected = projected
        self.dst = dst
        self.inner = H * width
        self.tiles = self.inner // P
        self.rounds = max(1, self.tiles // 4)
        self.batches = 1 if projected else 2

    def keys(self, n):
        return n % UNITS // H + 1 if self.causal else QB

    def events(self):
        out = {}
        for block in range(self.batches * QB):
            done = H * (block + 1) + LAG_AV
            for r in range(self.rounds + 1):
                out[done + 2 + 2 * r] = (block, r)
        return out

    def scores(self, k, n):
        batch, (qb, h) = n // UNITS, divmod(n % UNITS, H)
        queries, keys = slice(qb * P, (qb + 1) * P), slice(0, self.keys(n) * P)
        if not self.projected:
            rows = slice(PACK * (h % 4), PACK * (h % 4 + 1))
            return k.QT[batch][rows, h // 4, queries].bitcast(F32R), k.KT[batch][rows, h // 4, keys].bitcast(F32R)
        return k.QT[:, h // 2, queries], k.KT[h % 2][:, 0 if self.shared_kv else h // 2, keys]

    def values(self, k, n, block):
        h = n % H
        if not self.projected:
            return k.V[n // UNITS][:, block, :]
        return k.V[:, block, :] if self.shared_kv else k.V[:, block, h // 2 * P:(h // 2 + 1) * P]

    def outputs(self, bank, group):
        if not self.projected:
            offset, step = group % (H // GROUP) * GROUP * self.width, P + self.width
        else:
            offset, step = 0, P
        odd = P + DH if self.projected and not self.shared_kv else step
        return bass.AP(tensor=bank[:].tensor, offset=offset, ap=[[512, P], [2 * step, 2], [odd, 2], [1, self.width]])


def attention_stage(nc, c, a, b, w, load_qkv=None, tag=""):
    R = a.rounds + 1
    units, groups = a.batches * UNITS, a.batches * UNITS // GROUP
    steps = units + LAG_AV + 3 + 2 * R
    events = a.events()
    with ExitStack() as ctx:
        st = Stage(nc, ctx, a.name + "u")
        (x_ready, loaded, projected, act_copied, dve_copied, scored, maxed, exped, turned, pt_ready, av_done,
         dve_done, o_ready, y_made, y_copied) = st.sems(
            "x_ready", "loaded", "projected", "act_copied", "dve_copied", "scored", "maxed", "exped", "turned",
            "pt_ready", "av_done", "dve_done", "o_ready", "y_made", "y_copied")
        if load_qkv is not None:
            (loaded_next,) = st.sems("loaded_next")
        if a.shared_kv:
            null_scored, null_gap, null_exped, null_spread = st.sems(
                "null_scored", "null_gap", "null_exped", "null_spread")
        QT, KT, V, probs, PT, sums, top, O, OT, rinv = w.QT, w.KT, w.V, w.probs, w.PT, w.sums, w.top, w.O, w.OT, w.rinv

        jobs = []
        if a.projected:
            jobs = [("q", t) for t in range(a.tiles)]
            if a.shared_kv:
                jobs += [("k1", 0), ("v1", 0)]
            else:
                jobs += [("k", t) for t in range(a.tiles)]
                jobs += [("v", t) for t in range(2 * QB)]
        bank_of = (0, 1, 2, Y_BANK)

        def copied_before(eng, j):
            if j > 0:
                eng.wait_ge(act_copied, (j + 1) // 2)
            if j > 1:
                eng.wait_ge(dve_copied, j // 2)

        def copies(kind, t, j):
            bank = c.ps[bank_of[j % 4]]
            if kind == "q":
                return [(QT[:, t, :], bank[:])]
            if kind in ("k", "k1"):
                return [(KT[i][DH * i:DH * (i + 1), t, :], bank[DH * i:DH * (i + 1), :]) for i in range(2)]
            if kind == "v1":
                return [(V[:].rearrange("p q d -> p (q d)"), bank[:])]
            return [(V[:, t // 2, (t % 2) * 512:(t % 2 + 1) * 512], bank[:])]

        with nc.Block(no_gpsimd_drain=True) as block:
            if load_qkv is not None:
                @block.sync
                def _(sp):
                    load_qkv(sp, b + 1, 1, loaded)
                    sp.wait_ge(scored, UNITS)
                    load_qkv(sp, b + 2, 0, loaded_next)
                    sp.wait_ge(loaded_next, 16 * w.n_loads)

            @block.gpsimd
            def _(pool):
                if a.projected:
                    nc.gpsimd.tensor_copy(w.xT[:], w.source[:, b, :]).then_inc(x_ready, 1)
                else:
                    for i in range(a.batches):
                        nc.gpsimd.tensor_copy(V[i][:], w.source[:, bass.ts(b + i, QB), :]).then_inc(x_ready, 1)
                if a.shared_kv:
                    for hf in range(groups):
                        pool.wait_ge(null_exped, hf + 1)
                        if hf >= 2:
                            pool.wait_ge(o_ready, hf - 1)
                        nc.gpsimd.tensor_tensor(
                            w.null_part[:, hf % 2, :, :],
                            w.null_weight[:, hf % 2, :].unsqueeze(2).broadcast_to([P, GROUP, DH]),
                            w.null_v[:].unsqueeze(1).broadcast_to([P, GROUP, DH]), ALU.mult).then_inc(null_spread, 1)

            @block.tensor
            def _(pe):
                x_now = w.source[:, b, :] if a.projected else None
                for j, (kind, t) in enumerate(jobs):
                    if j >= 4:
                        copied_before(pe, j - 3)
                    if kind in ("v", "v1"):
                        pe.wait_ge(x_ready, 1)
                    bank = c.ps[bank_of[j % 4]]
                    if kind == "q":
                        last = nc.tensor.matmul(bank[:], w.wq[:, t * P:(t + 1) * P], x_now, start=True, stop=True)
                    elif kind in ("k", "k1"):
                        last = nc.tensor.matmul(bank[:], w.wk[:, t * P:(t + 1) * P], x_now, start=True, stop=True)
                    elif kind == "v":
                        q, half = t // 2, t % 2
                        last = nc.tensor.matmul(bank[:], w.xT[:, q * P:(q + 1) * P],
                                                w.wv[:, half * 512:(half + 1) * 512], start=True, stop=True)
                    else:
                        for q in range(QB):
                            last = nc.tensor.matmul(bank[:, q * P:(q + 1) * P], w.xT[:, q * P:(q + 1) * P],
                                                    w.wv[:], start=True, stop=True)
                    last.then_inc(projected, 1)
                copied_before(pe, len(jobs))
                if a.shared_kv:
                    for q in range(QB):
                        last = nc.tensor.matmul(c.ps[Y_BANK][:, q * H:(q + 1) * H], w.xT[:, q * P:(q + 1) * P],
                                                w.null_w[:], start=True, stop=True)
                    last.then_inc(null_scored, 1)

                for n in range(steps):
                    if n < units:
                        if load_qkv is not None and n == UNITS:
                            pe.wait_ge(loaded, 16 * w.n_loads)
                        qb = n % UNITS // H
                        queries, keys = a.scores(w, n)
                        bank = c.ps[n % S_BANKS]
                        if n >= S_BANKS:
                            pe.wait_ge(maxed if a.bias is not None else exped, n - S_BANKS + 1)
                        last = nc.tensor.matmul(bank[:, 0:a.keys(n) * P], queries, keys, start=True,
                                                stop=not a.causal or a.bias is not None)
                        if a.causal and a.bias is None:
                            last = nc.tensor.matmul(bank[:, qb * P:(qb + 1) * P], c.ident16[:], c.mask16[:],
                                                    start=False, stop=True)
                        last.then_inc(scored, 1)
                    m = n - LAG_T
                    if 0 <= m < units:
                        pe.wait_ge(exped, m + 1)
                        if m >= 2:
                            pe.wait_ge(pt_ready, m - 1)
                        for k in range(a.keys(m)):
                            last = nc.tensor.transpose(c.ps[T_BANK + m % 2][:, k * P:(k + 1) * P],
                                                       probs[:, m % PROBS, k * P:(k + 1) * P], c.ident[:])
                        last.then_inc(turned, 1)
                    m = n - LAG_AV
                    if 0 <= m < units:
                        hf = m // GROUP
                        if not a.projected and m % UNITS == 0:
                            pe.wait_ge(x_ready, m // UNITS + 1)
                        pe.wait_ge(pt_ready, m + 1)
                        if m % GROUP == 0 and hf >= 2:
                            pe.wait_ge(o_ready, hf - 1)
                        for k in range(a.keys(m)):
                            last = nc.tensor.matmul(
                                c.ps[O_BANK + hf % 2][:, (m % GROUP) * P:(m % GROUP + 1) * P],
                                PT[:, m % 2, k * P:(k + 1) * P], a.values(w, m, k), start=k == 0, stop=k == a.keys(m) - 1)
                        last.then_inc(av_done, 1)
                    if n in events:
                        qb, r = events[n]
                        if qb == 0 and r == 0 and a.shared_kv:
                            pe.wait_ge(null_gap, 1)
                        if R * qb + r > 0:
                            pe.wait_ge(y_copied, R * qb + r)
                        y = c.ps[Y_BANK]
                        if r < a.rounds:
                            pe.wait_ge(o_ready, H // GROUP * (qb + 1))
                            count = min(4, a.tiles)
                            for k in range(count):
                                t = 4 * r + k
                                last = nc.tensor.transpose(y[:, k * P:(k + 1) * P], O[:, qb % 2, t * P:(t + 1) * P],
                                                           c.ident[:])
                        else:
                            for t in range(a.tiles):
                                last = nc.tensor.matmul(y[:, 0:D], OT[:, t, :], w.wo[:, t, :],
                                                        start=t == 0, stop=t == a.tiles - 1)
                        last.then_inc(y_made, 1)

            @block.scalar
            def _(act):
                for j in range(0, len(jobs), 2):
                    kind, t = jobs[j]
                    act.wait_ge(projected, j + 1)
                    for dst, src in copies(kind, t, j):
                        last = nc.scalar.activation(dst, src, ACT.Copy, scale=w.q_scale if kind == "q" else 1.0)
                    last.then_inc(act_copied, 1)
                for n in range(steps + 1):
                    if n < units:
                        width = a.keys(n) * P
                        act.wait_ge(maxed, n + 1)
                        if n >= PROBS:
                            act.wait_ge(turned, n - PROBS + 1)
                        src = w.biased[:, n % 3, 0:width] if a.bias is not None else c.ps[n % S_BANKS][:, 0:width]
                        nc.scalar.activation(probs[:, n % PROBS, 0:width], src, ACT.Exp, bias=top[:, n:n + 1],
                                             scale=-1.0 if a.bias is not None else 1.0,
                                             accum_out=sums[:, n:n + 1]).then_inc(exped, 1)
                    if a.shared_kv and n % GROUP == 2 and n >= GROUP:
                        hf = n // GROUP - 1
                        if hf < groups:
                            act.wait_ge(null_gap, hf + 2)
                            if hf >= 2:
                                act.wait_ge(o_ready, hf - 1)
                            nc.scalar.activation(w.null_weight[:, hf % 2, :], w.null_less[:, hf, :],
                                                 ACT.Exp).then_inc(null_exped, 1)
                    if n - 1 in events:
                        qb, r = events[n - 1]
                        act.wait_ge(y_made, R * qb + r + 1)
                        y = c.ps[Y_BANK]
                        if r < a.rounds:
                            count = min(4, a.tiles)
                            nc.scalar.activation(OT[:, 4 * r:4 * r + count, :].rearrange("p t q -> p (t q)"),
                                                 y[:, 0:count * P], ACT.Copy).then_inc(y_copied, 1)
                        else:
                            nc.scalar.activation(a.dst[:, b * QB + qb, :], y[:, 0:D], ACT.Copy).then_inc(y_copied, 1)

            @block.vector
            def _(dve):
                chain = Chain(dve, dve_done)
                for j in range(1, len(jobs), 2):
                    kind, t = jobs[j]
                    dve.wait_ge(projected, j + 1)
                    for dst, src in copies(kind, t, j):
                        last = nc.vector.tensor_scalar(dst, src, w.q_scale if kind == "q" else 1.0, None, ALU.mult)
                    last.then_inc(dve_copied, 1)
                if a.shared_kv:
                    dve.wait_ge(null_scored, 1)
                    nc.vector.tensor_tensor(w.null_s[:], c.ps[Y_BANK][:, 0:UNITS], w.null_bias[:],
                                            ALU.add).then_inc(null_gap, 1)
                    dve.wait_ge(null_gap, 1)
                for n in range(steps + 1):
                    if n < units:
                        h = n % H
                        width = a.keys(n) * P
                        dve.wait_ge(scored, n + 1)
                        if a.bias is not None:
                            if n >= 3:
                                dve.wait_ge(exped, n - 2)
                            nc.vector.tensor_tensor_reduce(
                                out=w.biased[:, n % 3, 0:width], in0=c.ps[n % S_BANKS][:, 0:width],
                                in1=a.bias[:, h, S - width:S], scale=1.0, scalar=w.null_s[:, n:n + 1],
                                op0=ALU.add, op1=ALU.min, accum_out=top[:, n:n + 1]).then_inc(maxed, 1)
                        else:
                            nc.vector.tensor_reduce(top[:, n:n + 1], c.ps[n % S_BANKS][:, 0:width], AX, ALU.max,
                                                    negate=True).then_inc(maxed, 1)
                    m = n - LAG_T
                    if 0 <= m < units:
                        width = a.keys(m) * P
                        dve.wait_ge(turned, m + 1)
                        if m >= 2:
                            dve.wait_ge(av_done, m - 1)
                        nc.vector.tensor_copy(PT[:, m % 2, 0:width],
                                              c.ps[T_BANK + m % 2][:, 0:width]).then_inc(pt_ready, 1)
                    if a.shared_kv and n % GROUP == 1 and n >= GROUP and n // GROUP - 1 < groups:
                        hf = n // GROUP - 1
                        dve.wait_ge(maxed, GROUP * (hf + 1))
                        nc.vector.tensor_tensor(w.null_less[:, hf, :], top[:, hf * GROUP:(hf + 1) * GROUP],
                                                w.null_s[:, hf * GROUP:(hf + 1) * GROUP],
                                                ALU.subtract).then_inc(null_gap, 1)
                    m = n - LAG_AV
                    if m % GROUP == 0 and 0 < m <= units:
                        hf = m // GROUP - 1
                        block_, g = divmod(hf, H // GROUP)
                        dve.wait_ge(av_done, GROUP * (hf + 1))
                        if block_ >= 2 and g == 0:
                            dve.wait_ge(y_made, R * (block_ - 2) + a.rounds)
                        n4 = slice(hf * GROUP, (hf + 1) * GROUP)
                        heads = a.outputs(c.ps[O_BANK + hf % 2], hf)
                        if a.shared_kv:
                            dve.wait_ge(null_spread, hf + 1)
                            part = w.null_part[:, hf % 2, :, :].rearrange("p (a b) d -> p a b d", b=2)
                            chain.mark(nc.vector.tensor_tensor(part, part, heads, ALU.add))
                            chain.link(nc.vector.tensor_tensor(sums[:, n4], sums[:, n4],
                                                               w.null_weight[:, hf % 2, :], ALU.add))
                            heads = part
                        chain.link(nc.vector.reciprocal(rinv[:, hf % 2, :], sums[:, n4]))
                        span = GROUP * a.width
                        over_sum = rinv[:, hf % 2, :].rearrange("p (a b) -> p a b", b=2).unsqueeze(3)
                        nc.vector.tensor_tensor(
                            O[:, block_ % 2, g * span:(g + 1) * span].rearrange("p (a b d) -> p a b d", b=2,
                                                                               d=a.width),
                            heads, over_sum.broadcast_to([P, 2, 2, a.width]), ALU.mult).then_inc(o_ready, 1)
        st.end()


class Work:

    def __init__(self, nc, ctx, a):
        def sb(name, shape, dt=F32):
            return ctx.enter_context(nc.sbuf_tensor(f"{a.name}_{name}", shape, dt))

        self.sb = sb
        self.probs = sb("probs", [P, PROBS, S])
        self.PT = sb("PT", [P, 2, S])
        self.sums = sb("sums", [P, a.batches * UNITS])
        self.top = sb("top", [P, a.batches * UNITS])
        self.rinv = sb("rinv", [P, 2, GROUP])
        self.O = sb("O", [P, 2, a.inner])
        self.OT = sb("OT", [P, a.tiles, P])
        self.wo = sb("wo", [P, a.tiles, D])
        self.n_loads = 0


def attention0(nc, c, w, xaT):
    with ExitStack() as ctx:
        a = Heads("a0", DH, causal=False, projected=True, dst=c.s)
        k = Work(nc, ctx, a)
        k.xT = k.sb("xT", [P, S])
        k.QT = k.sb("QT", [P, a.tiles, S])
        k.KT = [k.sb("KT", [P, a.tiles, S]), c.xn[:].rearrange("p t d -> p (t d)").rearrange(
            "p (t m) -> p t m", m=S)]
        k.V = k.sb("V", [P, QB, a.inner])
        k.wq, k.wk, k.wv = (k.sb(n, [P, a.inner]) for n in ("wq", "wk", "wv"))
        k.q_scale = DH ** -0.5
        k.source = xaT
        with ExitStack() as ld:
            st = Stage(nc, ld, "a0l")
            loaded, zeroed = st.sems("loaded", "zeroed")
            load_all(st, loaded, [(k.wq[:], w["L0_attn_Wq"]), (k.wk[:], w["L0_attn_Wk"]), (k.wv[:], w["L0_attn_Wv"]),
                                  (k.wo[:], w["L0_attn_Wo"].rearrange("(t p) d -> p t d", p=P))],
                     clear=[(k.KT[0][DH:P, :, :], zeroed), (k.KT[1][0:DH, :, :], zeroed)])
        with nc.Fori(0, NB) as b:
            attention_stage(nc, c, a, b, k)


def position_bias(nc, c, w, bias):
    tiles = NPOS // P
    with ExitStack() as ctx:
        st = Stage(nc, ctx, "pb")
        (loaded, pos_ready, dve_done, var_ready, root_ready, silued, turned, copied, h_ready, table, written, spread,
         reversal, placed, act_placed, dve_placed) = st.sems(
            "loaded", "pos_ready", "dve_done", "var_ready", "root_ready", "silued", "turned", "copied",
            "h_ready", "table", "written", "spread", "reversal", "placed", "act_placed", "dve_placed")
        reverse = st.sb("reverse", [P, P])
        rows = [t[:].rearrange("p t d -> p (t d)").rearrange("p (h m) -> p h m", m=S) for t in (c.xn, c.s)]
        names = ["w0", "b0", "ln0_g", "ln0_b", "b1", "ln1_g", "ln1_b"]
        row = {n: st.sb(n, [P, D]) for n in names}
        w1 = st.sb("w1", [P, D])
        w2 = st.sb("w2", [P, H])
        b2 = st.sb("b2", [H, 1])
        pos = st.sb("pos", [P, tiles])
        hid = st.sb("hid", [P, tiles, D])
        hidT = st.sb("hidT", [P, NPOS])
        stats = st.sb("stats", [P, tiles, 6])
        mv = st.sb("mv", [P, tiles, 2])
        rstd = st.sb("rstd", [P, tiles, 1])
        minus = st.sb("minus", [H, NPOS])
        n_loads = len(names) + 3

        with nc.Block() as block:
            @block.sync
            def _(sp):
                for n in names:
                    sp.dma_start(row[n][:], row_bcast(w["L1_attn_pb_" + n], D)).then_inc(loaded, 16)
                sp.dma_start(w1[:], w["L1_attn_pb_w1"]).then_inc(loaded, 16)
                sp.dma_start(w2[:], w["L1_attn_pb_w2"]).then_inc(loaded, 16)
                sp.dma_start(b2[:], column(w["L1_attn_pb_b2"])).then_inc(loaded, 16)
                sp.wait_ge(table, 2)
                sp.dma_start(c.table, minus[:]).then_inc(written, 16)
                sp.wait_ge(written, 16)
                for h in range(H):
                    src = bass.AP(tensor=c.table.tensor, offset=c.table.offset + h * NPOS, ap=[[1, P], [1, S]])
                    sp.dma_start(rows[h // 8][:, h % 8, :], src).then_inc(spread, 16)

            @block.gpsimd
            def _(pool):
                nc.gpsimd.iota(pos[:], pattern=[[-P, tiles]], base=S - 1, channel_multiplier=-1,
                               allow_small_or_imprecise_dtypes=True).then_inc(pos_ready, 1)
                nc.gpsimd.memset(reverse[:], 0.0).then_inc(reversal, 1)
                pool.wait_ge(reversal, 1)
                nc.gpsimd.affine_select(out=reverse[:], in_=reverse[:], compare_op=ALU.not_equal, fill=1.0,
                                        base=-(P - 1), pattern=[[1, P]], channel_multiplier=1).then_inc(reversal, 1)
                pool.wait_ge(act_placed, H // 2)
                pool.wait_ge(dve_placed, H // 2)
                for h in range(H):
                    diag = bias[:, h, S - P:S]
                    nc.gpsimd.affine_select(out=diag, in_=diag, compare_op=ALU.is_ge, fill=MASKED, base=0,
                                            pattern=[[-1, P]], channel_multiplier=1)

            @block.vector
            def _(dve):
                chain = Chain(dve, dve_done)
                dve.wait_ge(loaded, 16 * n_loads)
                dve.wait_ge(pos_ready, 1)
                for t in range(tiles):
                    chain.mark(nc.vector.scalar_tensor_tensor(out=hid[:, t, :], in0=row["w0"][:],
                                                              scalar=pos[:, t:t + 1], in1=row["b0"][:],
                                                              op0=ALU.mult, op1=ALU.add))
                chain.wait()
                for layer in range(2):
                    gain, shift = row[f"ln{layer}_g"], row[f"ln{layer}_b"]
                    if layer == 1:
                        dve.wait_ge(h_ready, tiles)
                        for t in range(tiles):
                            chain.mark(nc.vector.tensor_tensor(hid[:, t, :], c.ps[4 + t // 4][:, (t % 4) * P:(t % 4 + 1) * P],
                                                               row["b1"][:], ALU.add))
                        chain.wait()
                    for t in range(tiles):
                        chain.mark(nc.vector.bn_stats(stats[:, t, :], hid[:, t, :]))
                    chain.wait()
                    for t in range(tiles):
                        chain.mark(nc.vector.bn_aggr(mv[:, t, :], stats[:, t, :]))
                    chain.wait()
                    nc.vector.tensor_scalar(rstd[:], mv[:, :, 1:2], LN_EPS, None, ALU.add).then_inc(var_ready, 1)
                    dve.wait_ge(root_ready, layer + 1)
                    chain.link(nc.vector.reciprocal(rstd[:], rstd[:]))
                    for t in range(tiles):
                        chain.mark(nc.vector.tensor_scalar(hid[:, t, :], hid[:, t, :], mv[:, t, 0:1], rstd[:, t, :],
                                                           ALU.subtract, ALU.mult))
                    chain.wait()
                    chain.link(nc.vector.tensor_tensor(hid[:], hid[:], over_blocks(gain[:], tiles), ALU.mult))
                    nc.vector.tensor_tensor(hid[:], hid[:], over_blocks(shift[:], tiles),
                                            ALU.add).then_inc(var_ready, 1)
                for h in range(1, H, 2):
                    dve.wait_ge(placed, h + 1)
                    nc.vector.tensor_copy(bias[:, h, :], c.ps[4 + h % 4][:]).then_inc(dve_placed, 1)

            @block.scalar
            def _(act):
                for layer in range(2):
                    act.wait_ge(var_ready, 2 * layer + 1)
                    nc.scalar.activation(rstd[:], rstd[:], ACT.Sqrt).then_inc(root_ready, 1)
                    act.wait_ge(var_ready, 2 * layer + 2)
                    nc.scalar.activation(hid[:], hid[:], ACT.Silu).then_inc(silued, 1)
                    act.wait_ge(turned, 5 * (layer + 1))
                    nc.scalar.activation(hidT[:, 0:512], c.ps[0][:], ACT.Copy).then_inc(copied, 1)
                    nc.scalar.activation(hidT[:, 512:NPOS], c.ps[1][:, 0:P], ACT.Copy).then_inc(copied, 1)
                act.wait_ge(loaded, 16 * n_loads)
                act.wait_ge(h_ready, tiles + 2)
                nc.scalar.activation(minus[:, 0:512], c.ps[2][0:H, :], ACT.Identity,
                                     bias=b2[:]).then_inc(copied, 1)
                nc.scalar.activation(minus[:, 512:NPOS], c.ps[3][0:H, 0:P], ACT.Identity,
                                     bias=b2[:]).then_inc(copied, 1)
                act.wait_ge(copied, 6)
                nc.scalar.activation(minus[:], minus[:], ACT.Copy, scale=-1.0).then_inc(table, 2)
                for h in range(0, H, 2):
                    act.wait_ge(placed, h + 1)
                    nc.scalar.activation(bias[:, h, :], c.ps[4 + h % 4][:], ACT.Copy).then_inc(act_placed, 1)

            @block.tensor
            def _(pe):
                pe.wait_ge(loaded, 16 * n_loads)
                for layer in range(2):
                    pe.wait_ge(silued, layer + 1)
                    for t in range(tiles):
                        nc.tensor.transpose(c.ps[t // 4][:, (t % 4) * P:(t % 4 + 1) * P], hid[:, t, :],
                                            c.ident[:]).then_inc(turned, 1)
                    pe.wait_ge(copied, 2 * (layer + 1))
                    if layer == 0:
                        for t in range(tiles):
                            nc.tensor.matmul(c.ps[4 + t // 4][:, (t % 4) * P:(t % 4 + 1) * P],
                                             hidT[:, t * P:(t + 1) * P], w1[:], start=True,
                                             stop=True).then_inc(h_ready, 1)
                    else:
                        nc.tensor.matmul(c.ps[2][0:H, :], w2[:], hidT[:, 0:512], start=True,
                                         stop=True).then_inc(h_ready, 1)
                        nc.tensor.matmul(c.ps[3][0:H, 0:P], w2[:], hidT[:, 512:NPOS], start=True,
                                         stop=True).then_inc(h_ready, 1)
                pe.wait_ge(reversal, 2)
                pe.wait_ge(spread, 16 * H)
                for h in range(H):
                    if h >= 4:
                        pe.wait_ge(dve_placed if h % 2 else act_placed, (h - 4) // 2 + 1)
                    nc.tensor.matmul(c.ps[4 + h % 4][:], reverse[:], rows[h // 8][:, h % 8, :], start=True,
                                     stop=True).then_inc(placed, 1)
        st.end()


def ternary_gate(nc, c, w):
    f_tiles = FF // P
    with ExitStack() as ctx:
        st = Stage(nc, ctx, "g1")
        loaded, dve_done, summed, spread, weights, up_done, gelued, down_done, g_ready, silued = st.sems(
            "loaded", "dve_done", "summed", "spread", "weights", "up_done", "gelued", "down_done", "g_ready", "silued")
        w1 = st.sb("w1", [P, FF])
        w2 = st.sb("w2", [P, f_tiles, D])
        b1 = st.sb("b1", [P, f_tiles])
        b2 = st.sb("b2", [P, D])
        row_sum = st.sb("row_sum", [P, 2])
        half_scale = st.sb("half_scale", [P, 2])
        minus_half = st.sb("minus_half", [P, 2])
        above = st.sb("above", [P, FF])
        below = st.sb("below", [P, FF])
        hT = st.sb("hT", [P, 2, f_tiles, S])

        with nc.Block() as block:
            @block.sync
            def _(sp):
                sp.dma_start(w1[:], w["L1_ffn_W1T"]).then_inc(loaded, 16)
                sp.dma_start(w2[:], w["L1_ffn_W2T"].rearrange("(t p) d -> p t d", p=P)).then_inc(loaded, 16)
                sp.dma_start(b1[:], w["L1_ffn_b1T"]).then_inc(loaded, 16)
                sp.dma_start(b2[:], row_bcast(w["L1_ffn_b2"], D)).then_inc(loaded, 16)

            @block.vector
            def _(dve):
                chain = Chain(dve, dve_done)
                dve.wait_ge(loaded, 64)
                mats = [w1[:], w2[:].rearrange("p t d -> p (t d)")]
                for i, m in enumerate(mats):
                    chain.mark(nc.vector.tensor_reduce(row_sum[:, i:i + 1], m, AX, ALU.add,
                                                       apply_absolute_value=True))
                chain.wait()
                nc.vector.tensor_copy(row_sum[:], row_sum[:]).then_inc(summed, 1)
                dve.wait_ge(spread, 1)
                chain.link(nc.vector.tensor_scalar(half_scale[:], c.ps[0][:, 0:2], 1.0 / (FF * D), 1e-8,
                                                   ALU.mult, ALU.max))
                chain.link(nc.vector.tensor_scalar(half_scale[:], half_scale[:], 0.5, None, ALU.mult))
                chain.link(nc.vector.tensor_scalar(minus_half[:], half_scale[:], -1.0, None, ALU.mult))
                for i, m in enumerate(mats):
                    chain.mark(nc.vector.tensor_scalar(above[:], m, half_scale[:, i:i + 1], None, ALU.is_gt))
                    chain.link(nc.vector.tensor_scalar(below[:], m, minus_half[:, i:i + 1], None, ALU.is_lt))
                    chain.link(nc.vector.tensor_tensor(above[:], above[:], below[:], ALU.subtract))
                    chain.link(nc.vector.tensor_tensor(above[:], above[:], m, ALU.subtract))
                    chain.link(nc.vector.tensor_tensor(m, m, above[:], ALU.add))
                nc.vector.tensor_copy(row_sum[:], row_sum[:]).then_inc(weights, 1)
                for b in range(NB):
                    dve.wait_ge(down_done, b + 1)
                    nc.vector.tensor_tensor(c.g[:, b * QB:(b + 1) * QB, :],
                                            c.ps[6 + b % 2][:].rearrange("p (q d) -> p q d", d=D),
                                            over_blocks(b2[:], QB), ALU.add).then_inc(g_ready, 1)

            @block.tensor
            def _(pe):
                pe.wait_ge(summed, 1)
                nc.tensor.matmul(c.ps[0][:, 0:2], c.ones[:], row_sum[:], start=True, stop=True).then_inc(spread, 1)
                pe.wait_ge(weights, 1)
                for b in range(NB + 1):
                    if b < NB:
                        for f in range(f_tiles):
                            n = b * f_tiles + f
                            if n >= 4:
                                pe.wait_ge(gelued, n - 3)
                            nc.tensor.matmul(c.ps[n % 4][:], w1[:, f * P:(f + 1) * P], c.xnT[:, b, :], start=True,
                                             stop=True).then_inc(up_done, 1)
                    if b > 0:
                        d = b - 1
                        pe.wait_ge(gelued, f_tiles * (d + 1))
                        if d >= 2:
                            pe.wait_ge(g_ready, d - 1)
                        for q in range(QB):
                            for f in range(f_tiles):
                                last = nc.tensor.matmul(c.ps[6 + d % 2][:, q * P:(q + 1) * P],
                                                        hT[:, d % 2, f, q * P:(q + 1) * P], w2[:, f, :],
                                                        start=f == 0, stop=f == f_tiles - 1)
                        last.then_inc(down_done, 1)

            @block.scalar
            def _(act):
                act.wait_ge(loaded, 64)
                for b in range(NB):
                    if b >= 2:
                        act.wait_ge(down_done, b - 1)
                    for f in range(f_tiles):
                        n = b * f_tiles + f
                        act.wait_ge(up_done, n + 1)
                        nc.scalar.activation(hT[:, b % 2, f, :], c.ps[n % 4][:], ACT.Gelu,
                                             bias=b1[:, f:f + 1]).then_inc(gelued, 1)
                act.wait_ge(g_ready, NB)
                nc.scalar.activation(c.g[:], c.g[:], ACT.Silu).then_inc(silued, 1)
        st.end()


def attention1(nc, c, w, xaT):
    with ExitStack() as ctx:
        bias = ctx.enter_context(nc.sbuf_tensor("bias", [P, H, S], F32))
        position_bias(nc, c, w, bias)
        a = Heads("a1", DH, causal=True, bias=bias, shared_kv=True, projected=True, dst=c.s)
        k = Work(nc, ctx, a)
        k.xT = k.sb("xT", [P, S])
        k.QT = k.sb("QT", [P, a.tiles, S])
        k.KT = [k.sb(f"KT{i}", [P, 1, S]) for i in range(2)]
        k.V = k.sb("V", [P, QB, P])
        k.wq = k.sb("wq", [P, a.inner])
        k.wk = k.sb("wk", [P, P])
        k.wv = k.sb("wv", [P, P])
        k.q_scale = -DH ** -0.5
        k.source = xaT
        k.biased = k.sb("biased", [P, 3, S])
        k.null_w = k.sb("null_w", [P, H])
        k.null_k = k.sb("null_k", [P, DH])
        k.null_v = k.sb("null_v", [P, DH])
        k.null_bias = k.sb("null_bias", [P, UNITS])
        k.null_s = k.sb("null_s", [P, UNITS])
        k.null_less = k.sb("null_less", [P, UNITS // GROUP, GROUP])
        k.null_weight = k.sb("null_weight", [P, 2, GROUP])
        k.null_part = k.sb("null_part", [P, 2, GROUP, DH])
        with ExitStack() as ld:
            st = Stage(nc, ld, "a1l")
            zeroed, loaded, dve_done = st.sems("zeroed", "loaded", "dve_done")
            wkv = w["L1_attn_Wkv"]
            null_kv = w["L1_attn_null_kv"]
            pairs = [(k.wq[:], w["L1_attn_Wq"]), (k.wk[:, 0:DH], wkv[:, 0:DH]), (k.wk[:, DH:P], wkv[:, 0:DH]),
                     (k.wv[:, 0:DH], wkv[:, DH:2 * DH]), (k.wv[:, DH:P], wkv[:, DH:2 * DH]),
                     (k.null_v[:], row_bcast(null_kv[1], DH)),
                     (k.wo[:], w["L1_attn_Wo"].rearrange("(t p) d -> p t d", p=P)),
                     (k.null_k[:], row_bcast(null_kv[0], DH))]
            pairs += [(k.null_bias[:, q * H:(q + 1) * H], row_bcast(w["L1_attn_null_attn_bias"], H))
                      for q in range(QB)]
            with nc.Block() as block:
                @block.sync
                def _(sp):
                    for dst, src in pairs:
                        sp.dma_start(dst, src).then_inc(loaded, 16)

                @block.vector
                def _(dve):
                    nc.vector.memset(k.KT[0][DH:P, :, :], 0.0).then_inc(zeroed, 1)
                    nc.vector.memset(k.KT[1][0:DH, :, :], 0.0).then_inc(zeroed, 1)
                    dve.wait_ge(loaded, 16 * len(pairs))
                    chain = Chain(dve, dve_done)
                    product = k.QT[:, 0:a.inner // S, :].rearrange("p a (b d) -> p (a b) d", d=DH)
                    chain.mark(nc.vector.tensor_scalar(k.null_bias[:], k.null_bias[:], -1.0, None, ALU.mult))
                    chain.link(nc.vector.tensor_tensor(product, k.wq[:].rearrange("p (h d) -> p h d", d=DH),
                                                       over_blocks(k.null_k[:], H), ALU.mult))
                    chain.link(nc.vector.tensor_reduce(k.null_w[:], product, AX, ALU.add))
                    nc.vector.tensor_scalar(k.null_w[:], k.null_w[:], k.q_scale, None, ALU.mult).then_inc(dve_done, 1)
            st.end()
        with nc.Fori(0, NB) as b:
            attention_stage(nc, c, a, b, k)


def project_stage(nc, c, name, srcT, transposed, value=None, rope=None, split=False, ahead=(), load_first=None):
    with ExitStack() as ctx:
        st = Stage(nc, ctx, name)
        loaded, made, act_copied, dve_copied, dve_done, v_made, v_copied, parted, came_ahead, *stored = st.sems(
            "loaded", "made", "act_copied", "dve_copied", "dve_done", "v_made", "v_copied", "parted", "came_ahead",
            "stored_even", "stored_odd")
        mats, biases, tables = [], [], []
        pairs = []
        for i, (weight, bias, scale, _) in enumerate(transposed):
            group = []
            for k, src in enumerate(weight if rope else (weight,)):
                m = st.sb(f"w{i}{k}", [P, D])
                group.append(m)
                pairs.append((m[:], src))
            mats.append(group)
            biases.append(None)
            if bias is not None:
                biases[i] = st.sb(f"b{i}", [P, 1])
                pairs.append((biases[i][:], column(bias)))
            if rope:
                tables.append([st.sb(f"t{i}{k}", [P, S]) for k in range(2)])
                pairs += [(t[:], src) for t, src in zip(tables[i], scale)]
        if value is not None:
            wv = st.sb("wv", [P, D])
            pairs.append((wv[:], value[0]))
        n = len(transposed)
        kept = st.sb("kept", [P, n, S * 2])
        turned = st.sb("rotated", [P, 2, S]) if rope else None
        upper = st.sb("upper", [P, n, S * 2]) if split else None
        copied = dve_copied if rope else act_copied
        half_stores = [16 * n * (NB // 2) * (2 if split else 1) + (32 * n if split and i == 0 else 0) for i in range(2)]

        def stores_before(b):
            return 16 * n * (b // 2) * (2 if split else 1) + (32 * n if split and b % 2 == 0 and b > 0 else 0)

        with nc.Block() as block:
            @block.sync
            def _(sp):
                for dst, src in pairs:
                    sp.dma_start(dst, src).then_inc(loaded, 16)
                for dst, src in ahead:
                    sp.dma_start(dst, src).then_inc(came_ahead, 16)
                n_ahead = len(ahead)
                for b in range(NB):
                    if b == 2 and load_first is not None:
                        sp.wait_ge(stored[0], stores_before(2))
                        n_ahead += load_first(sp, came_ahead)
                    for i, (_, _, _, dram) in enumerate(transposed):
                        j = b * n + i
                        now = slice((b % 2) * S, (b % 2 + 1) * S)
                        sp.wait_ge(parted if split else copied, j + 1)
                        if not split:
                            sp.dma_start(dram[:, b, :], kept[:, i, now]).then_inc(stored[b % 2], 16)
                            continue
                        for to in (b, NB) if b == 0 else (b,):
                            sp.dma_start(dram[0, :, to, :], upper[:, i, now]).then_inc(stored[b % 2], 16)
                            sp.dma_start(dram[1, :, to, :], kept[:, i, now]).then_inc(stored[b % 2], 16)
                for half, total in zip(stored, half_stores):
                    sp.wait_ge(half, total)
                if n_ahead:
                    sp.wait_ge(came_ahead, 16 * n_ahead)

            @block.tensor
            def _(pe):
                pe.wait_ge(loaded, 16 * len(pairs))
                for b in range(NB):
                    for i in range(n):
                        j = b * n + i
                        if j >= 2:
                            pe.wait_ge(copied, j - 1)
                        for k, m in enumerate(mats[i]):
                            last = nc.tensor.matmul(c.ps[2 * k + j % 2][:], m[:], srcT[:, b, :], start=True, stop=True)
                        last.then_inc(made, 1)
                    if value is not None:
                        if b >= 2:
                            pe.wait_ge(v_copied, b - 1)
                        for q in range(QB):
                            last = nc.tensor.matmul(c.ps[4 + b % 2][:, q * P:(q + 1) * P],
                                                    srcT[:, b, q * P:(q + 1) * P], wv[:], start=True, stop=True)
                        last.then_inc(v_made, 1)

            @block.scalar
            def _(act):
                act.wait_ge(loaded, 16 * len(pairs))
                for b in range(NB):
                    if not rope:
                        for i, (_, _, scale, _) in enumerate(transposed):
                            j = b * n + i
                            act.wait_ge(made, j + 1)
                            if b >= 2:
                                act.wait_ge(stored[b % 2], stores_before(b))
                            bias = {} if biases[i] is None else {"bias": biases[i][:]}
                            nc.scalar.activation(kept[:, i, (b % 2) * S:(b % 2 + 1) * S], c.ps[j % 2][:],
                                                 ACT.Identity, scale=scale, **bias).then_inc(act_copied, 1)
                    if value is not None:
                        act.wait_ge(v_made, b + 1)
                        nc.scalar.activation(value[1][:, b * QB:(b + 1) * QB, :].rearrange("p q d -> p (q d)"),
                                             c.ps[4 + b % 2][:], ACT.Copy).then_inc(v_copied, 1)

            if rope or split:
                @block.vector
                def _(dve):
                    chain = Chain(dve, dve_done)
                    dve.wait_ge(loaded, 16 * len(pairs))
                    for b in range(NB):
                        for i in range(n):
                            j = b * n + i
                            now = slice((b % 2) * S, (b % 2 + 1) * S)
                            if rope:
                                dve.wait_ge(made, j + 1)
                                if j > 0:
                                    dve.wait_ge(dve_copied, j)
                                if b >= 2:
                                    dve.wait_ge(stored[b % 2], stores_before(b))
                                for k in range(2):
                                    chain.mark(nc.vector.tensor_tensor(turned[:, k, :], c.ps[2 * k + j % 2][:],
                                                                       tables[i][k][:], ALU.mult))
                                chain.wait()
                                nc.vector.tensor_tensor(kept[:, i, now], turned[:, 0, :], turned[:, 1, :],
                                                        ALU.add).then_inc(dve_copied, 1)
                            if split:
                                dve.wait_ge(copied, j + 1)
                                chain.link(nc.vector.tensor_scalar(upper[:, i, now].bitcast(I32),
                                                                   kept[:, i, now].bitcast(I32), UPPER, None,
                                                                   ALU.bitwise_and))
                                nc.vector.tensor_tensor(kept[:, i, now], kept[:, i, now], upper[:, i, now],
                                                        ALU.subtract).then_inc(parted, 1)
        st.end()


def unit_length(nc, c, q, k):
    with ExitStack() as ctx:
        st = Stage(nc, ctx, "len")
        dve_done, squared, summed, rooted, ready, divided = st.sems("dve_done", "squared", "summed", "rooted", "ready",
                                                                    "divided")
        square = st.sb("square", [P, 2, DN, S])
        length = st.sb("length", [P, 2, S])
        split = S * 5 // 8

        def divide(eng, m, i, part):
            n = part.stop - part.start
            return eng.tensor_tensor(m[:, :, part], m[:, :, part],
                                     length[:, i, part].unsqueeze(1).broadcast_to([P, DN, n]), ALU.mult)

        with nc.Block() as block:
            @block.scalar
            def _(act):
                for i, m in enumerate((q, k)):
                    nc.scalar.activation(square[:, i], m, ACT.Square).then_inc(squared, 1)
                for i in range(2):
                    act.wait_ge(summed, i + 1)
                    nc.scalar.activation(length[:, i, :], length[:, i, :], ACT.Sqrt).then_inc(rooted, 1)

            @block.vector
            def _(dve):
                chain = Chain(dve, dve_done)
                for i in range(2):
                    dve.wait_ge(squared, i + 1)
                    nc.vector.tensor_reduce(length[:, i, :], square[:, i].rearrange("p d t -> p t d"), AX,
                                            ALU.add).then_inc(summed, 1)
                for i in (1, 0):
                    dve.wait_ge(rooted, 2)
                    chain.link(nc.vector.tensor_scalar(length[:, i, :], length[:, i, :], 1e-12, None, ALU.max))
                    nc.vector.reciprocal(length[:, i, :], length[:, i, :]).then_inc(ready, 1)
                dve.wait_ge(ready, 2)
                divide(nc.vector, q, 0, slice(0, S)).then_inc(divided, 1)
                divide(nc.vector, k, 1, slice(0, split)).then_inc(divided, 1)

            @block.gpsimd
            def _(pool):
                pool.wait_ge(ready, 1)
                divide(nc.gpsimd, k, 1, slice(split, S)).then_inc(divided, 1)
        st.end()


def threshold_routing(nc, c, w, weight, ahead):
    with ExitStack() as ctx:
        st = Stage(nc, ctx, "r2")
        loaded, made, dve_done, less, exped, ready, turned, copied, b_made, b_copied, came_ahead = st.sems(
            "loaded", "made", "dve_done", "less", "exped", "ready", "turned", "copied", "b_made", "b_copied",
            "came_ahead")
        wgt = st.sb("wgt", [P, E + 1])
        bgt = st.sb("bgt", [P, E + 1])
        b2 = st.sb("b2", [E, D])
        logit = st.sb("logit", [P, TB, E + 1])
        top = st.sb("top", [P, TB, 1])
        total = st.sb("total", [P, TB, 1])
        none = st.sb("none", [P, TB, 1])
        weightT = st.sb("weightT", [E, 2, S])
        gate, thr = logit[:, :, 0:E], logit[:, :, E:E + 1]

        def spread(t):
            return t[:].broadcast_to([P, TB, E])

        with nc.Block() as block:
            @block.sync
            def _(sp):
                sp.dma_start(wgt[:, 0:E], w["L2_ffn_Wg"]).then_inc(loaded, 16)
                sp.dma_start(wgt[:, E:E + 1], w["L2_ffn_Wt"]).then_inc(loaded, 16)
                sp.dma_start(bgt[:, 0:E], row_bcast(w["L2_ffn_bg"], E)).then_inc(loaded, 16)
                sp.dma_start(bgt[:, E:E + 1], row_bcast(w["L2_ffn_bt"], 1)).then_inc(loaded, 16)
                sp.dma_start(b2[:], w["L2_ffn_b2"]).then_inc(loaded, 16)
                for dst, src in ahead:
                    sp.dma_start(dst, src).then_inc(came_ahead, 16)
                sp.wait_ge(came_ahead, 16 * len(ahead))

            def biases(pe, b):
                pe.wait_ge(copied, b + 1)
                if b >= 2:
                    pe.wait_ge(b_copied, b - 1)
                for q in range(QB):
                    last = nc.tensor.matmul(c.ps[3 + b % 2][:, q * P:(q + 1) * P],
                                            weightT[:, b % 2, q * P:(q + 1) * P], b2[:], start=True, stop=True)
                last.then_inc(b_made, 1)

            @block.tensor
            def _(pe):
                pe.wait_ge(loaded, 80)
                for t in range(TB):
                    last = nc.tensor.matmul(c.ps[0][:, t * (E + 1):(t + 1) * (E + 1)],
                                            c.xnT[:, t // QB, (t % QB) * P:(t % QB + 1) * P], wgt[:],
                                            start=True, stop=True)
                last.then_inc(made, 1)
                pe.wait_ge(ready, 1)
                for b in range(NB):
                    if b >= 2:
                        pe.wait_ge(copied, b - 1)
                    for q in range(QB):
                        last = nc.tensor.transpose(c.ps[1 + b % 2][0:E, q * P:(q + 1) * P], weight[:, b * QB + q, :],
                                                   c.ident[:])
                    last.then_inc(turned, 1)
                    if b >= 1:
                        biases(pe, b - 1)
                biases(pe, NB - 1)

            @block.scalar
            def _(act):
                act.wait_ge(less, 1)
                nc.scalar.activation(gate, gate, ACT.Exp).then_inc(exped, 1)
                nc.scalar.activation(thr, thr, ACT.Tanh, scale=0.5).then_inc(exped, 1)
                for b in range(NB):
                    act.wait_ge(turned, b + 1)
                    if b >= 2:
                        act.wait_ge(b_made, b - 1)
                    nc.scalar.activation(weightT[:, b % 2, :], c.ps[1 + b % 2][0:E, :], ACT.Copy).then_inc(copied, 1)

            @block.vector
            def _(dve):
                chain = Chain(dve, dve_done)
                dve.wait_ge(loaded, 80)
                dve.wait_ge(made, 1)
                chain.link(nc.vector.tensor_tensor(
                    logit[:], c.ps[0][:, 0:TB * (E + 1)].rearrange("p (t e) -> p t e", e=E + 1),
                    over_blocks(bgt[:]), ALU.add))
                chain.link(nc.vector.tensor_reduce(top[:], gate, AX, ALU.max))
                nc.vector.tensor_tensor(gate, gate, spread(top), ALU.subtract).then_inc(less, 1)
                dve.wait_ge(exped, 2)
                chain.link(nc.vector.tensor_reduce(total[:], gate, AX, ALU.add))
                chain.link(nc.vector.reciprocal(total[:], total[:]))
                chain.link(nc.vector.tensor_tensor(gate, gate, spread(total), ALU.mult))
                chain.link(nc.vector.tensor_scalar(top[:], thr, 1.0, 0.0625, ALU.add, ALU.mult))
                chain.link(nc.vector.tensor_tensor(gate, gate, spread(top), ALU.subtract))
                chain.link(nc.vector.tensor_scalar(gate, gate, 0.0, None, ALU.max))
                chain.link(nc.vector.tensor_reduce(total[:], gate, AX, ALU.add))
                chain.link(nc.vector.tensor_scalar(none[:], total[:], 0.0, None, ALU.is_equal))
                chain.link(nc.vector.tensor_tensor(total[:], total[:], none[:], ALU.add))
                chain.link(nc.vector.reciprocal(total[:], total[:]))
                nc.vector.tensor_tensor(weight[:], gate, spread(total), ALU.mult).then_inc(ready, 1)
                for b in range(NB):
                    dve.wait_ge(b_made, b + 1)
                    nc.vector.tensor_copy(c.g[:, b * QB:(b + 1) * QB, :].rearrange("p q d -> p (q d)"),
                                          c.ps[3 + b % 2][:]).then_inc(b_copied, 1)
        st.end()


STEPS = S // NB
PARTS = (0, STEPS // 2, STEPS * 7 // 8, STEPS)
BETA, CLAMP, STATE_CAP, SHRINK = 0.9, 1.0, 10.0, 0.9


def delta_and_experts(nc, c, b, k):
    f_tiles = FF // P
    with ExitStack() as ctx:
        st = Stage(nc, ctx, "d2")
        (ready, taken, negated, stepped, dve_done, o_done, up_done, gelued, down_done, scaled, added) = st.sems(
            "ready", "taken", "negated", "stepped", "dve_done", "o_done", "up_done", "gelued", "down_done", "scaled",
            "added")

        def of_pass(t):
            return t[:, :, bass.ts(b, STEPS)].rearrange("p d t -> p t d")

        with nc.Block() as block:
            @block.vector
            def _(dve):
                chain = Chain(dve, dve_done)
                nc.vector.tensor_copy(k.k_now[:], of_pass(k.k)).then_inc(taken, 1)
                nc.vector.tensor_copy(k.v_now[:], of_pass(k.v)).then_inc(taken, 1)
                dve.wait_ge(taken, 2)

                def link_to(count):
                    dve.wait_ge(dve_done, count)

                def raw_of(t):
                    return k.raw[:, t % STEPS]

                def largest(t):
                    chain.mark(nc.vector.tensor_reduce(k.peak[:], raw_of(t).rearrange("p e d -> p (e d)"), AX,
                                                       ALU.max, apply_absolute_value=True))

                def shrink_of(t):
                    chain.mark(nc.vector.tensor_scalar(k.shrink[:, t:t + 1], k.peak[:], STATE_CAP, SHRINK,
                                                       ALU.is_le, ALU.max))
                    if t + 1 in PARTS:
                        chain.wait()
                        nc.vector.tensor_copy(k.peak[:], k.peak[:]).then_inc(stepped, 1)

                for t in range(STEPS):
                    before = raw_of(t - 1)
                    shrink = k.shrink[:, (t - 1) % STEPS:(t - 1) % STEPS + 1]
                    key = k.k_now[:, t, :].unsqueeze(1).broadcast_to([P, DN, DN])
                    chain.mark(nc.vector.tensor_tensor(k.prod[:], before, key, ALU.mult))
                    product_done = chain.n
                    if t > 0:
                        largest(t - 1)
                    link_to(product_done)
                    chain.mark(nc.vector.tensor_reduce(k.old[:], k.prod[:], AX, ALU.add))
                    old_done = chain.n
                    if t > 0:
                        link_to(old_done - 1)
                        shrink_of(t - 1)
                    chain.wait()
                    chain.mark(nc.vector.scalar_tensor_tensor(out=k.delta[:], in0=k.old[:], scalar=shrink,
                                                              in1=k.v_now[:, t, :], op0=ALU.mult, op1=ALU.subtract))
                    delta_done = chain.n
                    chain.mark(nc.vector.tensor_scalar(k.shrunk[:], before, shrink, None, ALU.mult))
                    link_to(delta_done)
                    chain.link(nc.vector.tensor_scalar(k.clipped[:], k.delta[:], -CLAMP, CLAMP, ALU.max, ALU.min))
                    if t == 0:
                        dve.wait_ge(negated, 1)
                    chain.link(nc.vector.tensor_tensor(
                        k.change[:], k.clipped[:].unsqueeze(2).broadcast_to([P, DN, DN]),
                        k.nk_now[:, t, :].unsqueeze(1).broadcast_to([P, DN, DN]), ALU.mult))
                    chain.link(nc.vector.tensor_tensor(raw_of(t), k.shrunk[:], k.change[:], ALU.add))
                largest(STEPS - 1)
                chain.wait()
                shrink_of(STEPS - 1)

            @block.gpsimd
            def _(pool):
                chain = Chain(pool, o_done)

                def outputs(part):
                    first, last = PARTS[part], PARTS[part + 1]
                    n, span = last - first, slice(first, last)
                    pool.wait_ge(stepped, part + 1)
                    tmp = k.o_part[:, 0:n]
                    q = k.q_now[:, span, :].unsqueeze(3).broadcast_to([P, n, DN, DN])
                    chain.link(nc.gpsimd.tensor_tensor(tmp, k.raw[:, span], q, ALU.mult))
                    for half in (4, 2, 1):
                        chain.link(nc.gpsimd.tensor_tensor(tmp[:, :, 0:half, :], tmp[:, :, 0:half, :],
                                                           tmp[:, :, half:2 * half, :], ALU.add))
                    shrink = k.shrink[:, span].unsqueeze(2).broadcast_to([P, n, DN])
                    chain.link(nc.gpsimd.tensor_tensor(tmp[:, :, 0, :], tmp[:, :, 0, :], shrink, ALU.mult))
                    chain.link(nc.gpsimd.tensor_scalar(k.o_now[:, span, :], tmp[:, :, 0, :], CLAMP, -CLAMP, ALU.min,
                                                       ALU.max))

                nc.gpsimd.tensor_copy(k.w_now[:], k.weight[:, bass.ts(b, QB), :]).then_inc(ready, 1)
                nc.gpsimd.tensor_copy(k.q_now[:], of_pass(k.q)).then_inc(ready, 1)
                pool.wait_ge(ready, 2)
                for e in range(E):
                    pool.wait_ge(scaled, QB * (e + 1))
                    if e >= 1:
                        pool.wait_ge(added, e)
                    g = c.g[:, bass.ts(b, QB), :]
                    nc.gpsimd.tensor_tensor(g, g, k.weighted[:, e % 2, :, :], ALU.add).then_inc(added, 1)
                    if e == E // 2 + 1:
                        outputs(0)
                for part in range(1, len(PARTS) - 1):
                    outputs(part)
                nc.gpsimd.tensor_copy(of_pass(k.q), k.o_now[:]).then_inc(ready, 1)

            @block.tensor
            def _(pe):
                for e in range(E + 1):
                    if e < E:
                        for f in range(f_tiles):
                            n = e * f_tiles + f
                            if n >= 4:
                                pe.wait_ge(gelued, n - 3)
                            nc.tensor.matmul(c.ps[n % 4][:], k.w1[:, e, f * P:(f + 1) * P], c.xnT[:, b, :],
                                             start=True, stop=True).then_inc(up_done, 1)
                    if e > 0:
                        d = e - 1
                        pe.wait_ge(gelued, f_tiles * (d + 1))
                        if d >= 2:
                            pe.wait_ge(scaled, QB * (d - 1))
                        for q in range(QB):
                            for f in range(f_tiles):
                                last = nc.tensor.matmul(c.ps[4 + d % 2][:, q * P:(q + 1) * P],
                                                        k.hT[:, d % 2, f, q * P:(q + 1) * P], k.w2[:, d, f, :],
                                                        start=f == 0, stop=f == f_tiles - 1)
                        last.then_inc(down_done, 1)

            @block.scalar
            def _(act):
                nc.scalar.activation(k.nk_now[:], of_pass(k.k), ACT.Copy, scale=-BETA).then_inc(negated, 1)
                for e in range(E + 1):
                    if e < E:
                        if e >= 2:
                            act.wait_ge(down_done, e - 1)
                        for f in range(f_tiles):
                            act.wait_ge(up_done, e * f_tiles + f + 1)
                            nc.scalar.activation(k.hT[:, e % 2, f, :], c.ps[f % 4][:], ACT.Gelu_apprx_tanh,
                                                 bias=k.b1[:, e, f:f + 1]).then_inc(gelued, 1)
                    if e > 0:
                        d = e - 1
                        act.wait_ge(down_done, d + 1)
                        if d == 0:
                            act.wait_ge(ready, 1)
                        if d >= 2:
                            act.wait_ge(added, d - 1)
                        for q in range(QB):
                            nc.scalar.activation(k.weighted[:, d % 2, q, :], c.ps[4 + d % 2][:, q * P:(q + 1) * P],
                                                 ACT.Copy, scale=k.w_now[:, q, d:d + 1]).then_inc(scaled, 1)
        st.end()


def delta_output(nc, c, w, o, o_dram):
    with ExitStack() as ctx:
        st = Stage(nc, ctx, "o2")
        loaded, stored, *turned, made, added, silued = st.sems("loaded", "stored", "first_turned", "second_turned", "made",
                                                               "added", "silued")
        oT = st.sb("oT", [P, NB, S])
        wo = st.sb("wo", [P, D])
        bo = st.sb("bo", [P, D])
        with nc.Block() as block:
            @block.sync
            def _(sp):
                sp.dma_start(wo[:], w["L2_attn_WoT"]).then_inc(loaded, 16)
                sp.dma_start(bo[:], row_bcast(w["L2_attn_bo"], D)).then_inc(loaded, 16)
                for part in range(2):
                    heads = slice(part * (P // 2), (part + 1) * (P // 2))
                    sp.dma_start(o_dram[heads], o[heads]).then_inc(stored, 16)
                    sp.wait_ge(stored, 16 * (part + 1))
                    batches = slice(part * (NB // 2), (part + 1) * (NB // 2))
                    sp.dma_start(oT[:, batches, :], bass.AP(
                        tensor=o_dram.tensor, offset=o_dram.offset + part * (NB // 2) * P * S,
                        ap=[[S, P], [P * S, NB // 2], [1, S]])).then_inc(turned[part], 16)

            @block.scalar
            def _(act):
                nc.scalar.activation(c.g[:], c.g[:], ACT.Silu).then_inc(silued, 1)

            @block.tensor
            def _(pe):
                pe.wait_ge(loaded, 32)
                for b in range(NB):
                    if b % (NB // 2) == 0:
                        pe.wait_ge(turned[b // (NB // 2)], 16)
                    if b >= 2:
                        pe.wait_ge(added, b - 1)
                    for q in range(QB):
                        last = nc.tensor.matmul(c.ps[b % 2][:, q * P:(q + 1) * P], oT[:, b, q * P:(q + 1) * P], wo[:],
                                                start=True, stop=True)
                    last.then_inc(made, 1)

            @block.vector
            def _(dve):
                dve.wait_ge(loaded, 32)
                for b in range(NB):
                    dve.wait_ge(made, b + 1)
                    nc.vector.tensor_tensor(c.s[:, b * QB:(b + 1) * QB, :],
                                            c.ps[b % 2][:].rearrange("p (q d) -> p q d", d=D),
                                            over_blocks(bo[:], QB), ALU.add).then_inc(added, 1)
        st.end()


class DeltaWork:
    pass


def layer2(nc, c, w):
    with ExitStack() as ctx:
        def sb(name, shape, dt=F32):
            return ctx.enter_context(nc.sbuf_tensor(f"l2_{name}", shape, dt))

        k = DeltaWork()
        k.q = c.xn[:].rearrange("p t d -> p (t d)").rearrange("p (d t) -> p d t", t=S)
        k.k = c.s[:].rearrange("p t d -> p (t d)").rearrange("p (d t) -> p d t", t=S)
        k.v = sb("v", [P, DN, S])
        dram = [nc.dram_tensor(f"l2_{n}T", (NB, D, S), F32, kind="Internal").ap() for n in "qkv"]
        o_dram = nc.dram_tensor("l2_o", (P, DN, S), F32, kind="Internal").ap()
        k.weight = sb("weight", [P, TB, E])
        k.w1 = sb("w1", [P, E, FF])
        k.w2 = sb("w2", [P, E, FF // P, D])
        k.b1 = sb("b1", [P, E, FF // P])
        k.raw = sb("raw", [P, STEPS, DN, DN])
        k.shrink = sb("shrink", [P, STEPS])
        weights = [(k.w1[:, e, :], w["L2_ffn_W1"][e]) for e in range(E)]
        weights += [(k.w2[:, e, :, :], w["L2_ffn_W2"][e].rearrange("(f p) d -> p f d", p=P)) for e in range(E)]
        weights += [(k.b1[:], w["L2_ffn_b1T"])]
        project_stage(nc, c, "p2", c.xnT, [(w[f"L2_attn_W{n}T"], w[f"L2_attn_b{n}"], 1.0,
                                            d.rearrange("b d t -> d b t")) for n, d in zip("qkv", dram)],
                      ahead=weights)
        heads = [(dst, src.rearrange("b (h d) t -> (b h) d t", d=DN)) for dst, src in zip((k.q, k.k, k.v[:]), dram)]
        threshold_routing(nc, c, w, k.weight, ahead=heads)
        unit_length(nc, c, k.q, k.k)
        k.hT = sb("hT", [P, 2, FF // P, S])
        k.weighted = sb("weighted", [P, 2, QB, D])
        k.q_now, k.k_now, k.nk_now, k.v_now = (sb(n, [P, STEPS, DN]) for n in ("q_now", "k_now", "nk_now", "v_now"))
        k.w_now = sb("w_now", [P, QB, E])
        k.prod = sb("prod", [P, DN, DN])
        k.change = sb("change", [P, DN, DN])
        k.shrunk = sb("shrunk", [P, DN, DN])
        k.old, k.delta, k.clipped = (sb(n, [P, DN]) for n in ("old", "delta", "clipped"))
        k.peak = sb("peak", [P, 1])
        k.o_part = sb("o_part", [P, max(last - first for first, last in zip(PARTS, PARTS[1:])), DN, DN])
        k.o_now = sb("o_now", [P, STEPS, DN])
        with ExitStack() as first:
            st = Stage(nc, first, "l2l")
            (zeroed,) = st.sems("zeroed")
            with nc.Block() as block:
                @block.vector
                def _(dve):
                    nc.vector.memset(k.raw[:, STEPS - 1], 0.0).then_inc(zeroed, 1)
                    nc.vector.memset(k.shrink[:, STEPS - 1:STEPS], 1.0).then_inc(zeroed, 1)
            st.end()
        with nc.Fori(0, NB) as b:
            delta_and_experts(nc, c, b, k)
    delta_output(nc, c, w, k.q, o_dram)


def rms_stage(nc, c, w, name, add, gain, ahead=()):
    with ExitStack() as ctx:
        st = Stage(nc, ctx, name)
        loaded, summed, squared, var_ready, rooted, dve_done, normed, turned, copied, came_ahead = st.sems(
            "loaded", "summed", "squared", "var_ready", "rooted", "dve_done", "normed", "turned", "copied", "came_ahead")
        gain_col = st.sb("gain", [P, 1])
        squares = st.sb("squares", [P, D])
        mean = st.sb("mean", [P, TB])
        scaled = st.sb("scaled", [P, TB, D])
        src = c.g if add else c.xn
        with nc.Block() as block:
            @block.sync
            def _(sp):
                sp.dma_start(gain_col[:], column(gain)).then_inc(loaded, 16)
                for dst, src in ahead:
                    sp.dma_start(dst, src).then_inc(came_ahead, 16)
                if ahead:
                    sp.wait_ge(came_ahead, 16 * len(ahead))

            @block.vector
            def _(dve):
                chain = Chain(dve, dve_done)
                if add:
                    nc.vector.tensor_tensor(c.g[:], c.g[:], c.xn[:], ALU.add).then_inc(summed, 1)
                dve.wait_ge(squared, TB)
                nc.vector.tensor_scalar(mean[:], mean[:], 1.0 / D, RMS_EPS, ALU.mult, ALU.add).then_inc(var_ready, 1)
                dve.wait_ge(rooted, 1)
                chain.link(nc.vector.reciprocal(mean[:], mean[:]))
                for t in range(TB):
                    nc.vector.tensor_scalar(scaled[:, t, :], src[:, t, :], mean[:, t:t + 1], None,
                                            ALU.mult).then_inc(normed, 1)

            @block.tensor
            def _(pe):
                for b in range(NB):
                    pe.wait_ge(normed, QB * (b + 1))
                    if b >= 4:
                        pe.wait_ge(copied, b - 3)
                    for q in range(QB):
                        last = nc.tensor.transpose(c.ps[b % 4][:, q * P:(q + 1) * P], scaled[:, b * QB + q, :],
                                                   c.ident[:])
                    last.then_inc(turned, 1)

            @block.scalar
            def _(act):
                if add:
                    act.wait_ge(summed, 1)
                for t in range(TB):
                    if t > 0:
                        act.wait_ge(squared, t)
                    nc.scalar.activation(squares[:], src[:, t, :], ACT.Square,
                                         accum_out=mean[:, t:t + 1]).then_inc(squared, 1)
                act.wait_ge(var_ready, 1)
                nc.scalar.activation(mean[:], mean[:], ACT.Sqrt).then_inc(rooted, 1)
                act.wait_ge(loaded, 16)
                for b in range(NB):
                    act.wait_ge(turned, b + 1)
                    nc.scalar.activation(c.xnT[:, b, :], c.ps[b % 4][:], ACT.Copy,
                                         scale=gain_col[:]).then_inc(copied, 1)
        st.end()


def load_heads(q_dram, k_dram, k):
    def load(sp, b, buffer, loaded):
        for dram, dst, part_of in ((q_dram, k.QT[buffer], lambda p: p // 2), (k_dram, k.KT[buffer], lambda p: p % 2)):
            for j in range(4):
                for p in range(4):
                    rows = slice(PACK * j + DN * p, PACK * j + DN * (p + 1))
                    heads = dram[part_of(p)].rearrange("(g j d) b t -> j d g b t", j=4, d=DN)[j]
                    sp.dma_start(dst[rows, :, :], heads[:, :, b, :]).then_inc(loaded, 16)
    return load


def narrow_attention(nc, c, name, project, wo, dst):
    with ExitStack() as ctx:
        a = Heads(name, DN, causal=True, dst=dst)
        q_dram, k_dram = (nc.dram_tensor(f"{name}_{n}T", (2, D, NB + 1, S), F32, kind="Internal").ap() for n in "qk")
        values = ctx.enter_context(nc.sbuf_tensor(f"{name}_values", [P, TB, D], F32))
        k = Work(nc, ctx, a)
        k.QT = [k.sb(f"QT{i}", [P, 4, S]) for i in range(2)]
        k.KT = [k.sb(f"KT{i}", [P, 4, S]) for i in range(2)]
        k.V = [k.sb(f"V{i}", [P, QB, D]) for i in range(2)]
        k.source = values
        k.n_loads = 32
        load = load_heads(q_dram, k_dram, k)

        def load_first(sp, came):
            load(sp, 0, 0, came)
            return k.n_loads

        project(q_dram, k_dram, values, ahead=[(k.wo[:], wo.rearrange("(t p) d -> p t d", p=P))],
                load_first=load_first)
        with nc.Fori(0, NB // a.batches) as pair:
            attention_stage(nc, c, a, pair * a.batches, k, load_qkv=load)


def top2_routing(nc, c, w, weight):
    with ExitStack() as ctx:
        st = Stage(nc, ctx, "r3")
        loaded, made, dve_done, less, exped = st.sems("loaded", "made", "dve_done", "less", "exped")
        router = st.sb("router", [P, E])
        prob = st.sb("prob", [P, TB, E])
        rank = st.sb("rank", [P, TB, E])
        over = st.sb("over", [P, TB, E])
        total = st.sb("total", [P, TB, 1])

        def spread(t, n=E):
            return t.broadcast_to([P, TB, n])

        with nc.Block() as block:
            @block.sync
            def _(sp):
                sp.dma_start(router[:], w["L3_ffn_w_router"]).then_inc(loaded, 16)

            @block.tensor
            def _(pe):
                pe.wait_ge(loaded, 16)
                for t in range(TB):
                    last = nc.tensor.matmul(c.ps[0][:, t * E:(t + 1) * E],
                                            c.xnT[:, t // QB, (t % QB) * P:(t % QB + 1) * P], router[:],
                                            start=True, stop=True)
                last.then_inc(made, 1)

            @block.scalar
            def _(act):
                act.wait_ge(less, 1)
                nc.scalar.activation(prob[:], prob[:], ACT.Exp).then_inc(exped, 1)

            @block.vector
            def _(dve):
                chain = Chain(dve, dve_done)
                dve.wait_ge(made, 1)
                logits = c.ps[0][:, 0:TB * E].rearrange("p (t e) -> p t e", e=E)
                chain.link(nc.vector.tensor_reduce(total[:], logits, AX, ALU.max))
                nc.vector.tensor_tensor(prob[:], logits, spread(total[:]), ALU.subtract).then_inc(less, 1)
                dve.wait_ge(exped, 1)
                chain.link(nc.vector.tensor_reduce(total[:], prob[:], AX, ALU.add))
                chain.link(nc.vector.reciprocal(total[:], total[:]))
                chain.link(nc.vector.tensor_tensor(prob[:], prob[:], spread(total[:]), ALU.mult))
                chain.link(nc.vector.memset(rank[:], 0.0))
                for j in range(E):
                    pj = prob[:, :, j:j + 1]
                    chain.link(nc.vector.tensor_tensor(over[:], spread(pj), prob[:], ALU.is_gt))
                    chain.link(nc.vector.tensor_tensor(rank[:], rank[:], over[:], ALU.add))
                    if j < E - 1:
                        behind = slice(j + 1, E)
                        chain.link(nc.vector.tensor_tensor(over[:, :, behind], spread(pj, E - 1 - j),
                                                           prob[:, :, behind], ALU.is_equal))
                        chain.link(nc.vector.tensor_tensor(rank[:, :, behind], rank[:, :, behind],
                                                           over[:, :, behind], ALU.add))
                chain.link(nc.vector.tensor_scalar(rank[:], rank[:], 2.0, None, ALU.is_lt))
                chain.link(nc.vector.tensor_tensor(prob[:], prob[:], rank[:], ALU.mult))
                chain.link(nc.vector.tensor_reduce(total[:], prob[:], AX, ALU.add))
                chain.link(nc.vector.reciprocal(total[:], total[:]))
                nc.vector.tensor_tensor(weight[:], prob[:], spread(total[:]), ALU.mult).then_inc(dve_done, 1)
        st.end()


def gated_experts(nc, c, b, k):
    h_tiles = HID // P
    with ExitStack() as ctx:
        st = Stage(nc, ctx, "m3")
        staged, up_done, silued, hid_ready, down_done, acc_done = st.sems(
            "staged", "up_done", "silued", "hid_ready", "down_done", "acc_done")
        with nc.Block(no_gpsimd_drain=True) as block:
            @block.tensor
            def _(pe):
                for e in range(E + 1):
                    if e < E:
                        for f in range(h_tiles):
                            n = e * h_tiles + f
                            if n >= 2:
                                pe.wait_ge(hid_ready, n - 1)
                            cols = slice(f * P, (f + 1) * P)
                            nc.tensor.matmul(c.ps[n % 2][:], k.wg[:, e, cols], c.xnT[:, b, :], start=True,
                                             stop=True).then_inc(up_done, 1)
                            nc.tensor.matmul(c.ps[2 + n % 2][:], k.wu[:, e, cols], c.xnT[:, b, :], start=True,
                                             stop=True).then_inc(up_done, 1)
                    if e > 0:
                        d = e - 1
                        pe.wait_ge(hid_ready, h_tiles * (d + 1))
                        if d >= 2:
                            pe.wait_ge(acc_done, QB * (d - 1))
                        for q in range(QB):
                            for f in range(h_tiles):
                                last = nc.tensor.matmul(c.ps[4 + d % 2][:, q * P:(q + 1) * P],
                                                        k.hT[:, d % 2, f, q * P:(q + 1) * P], k.wd[:, d, f, :],
                                                        start=f == 0, stop=f == h_tiles - 1)
                        last.then_inc(down_done, 1)

            @block.scalar
            def _(act):
                for n in range(E * h_tiles):
                    act.wait_ge(up_done, 2 * n + 1)
                    if n >= 2:
                        act.wait_ge(hid_ready, n - 1)
                    nc.scalar.activation(k.act[:, n % 2, :], c.ps[n % 2][:], ACT.Silu).then_inc(silued, 1)

            @block.vector
            def _(dve):
                nc.vector.tensor_copy(k.w_now[:], k.weight[:, bass.ts(b, QB), :]).then_inc(staged, 1)
                nc.vector.tensor_copy(k.acc[:], c.g[:, bass.ts(b, QB), :]).then_inc(staged, 1)
                dve.wait_ge(staged, 2)
                for e in range(E + 1):
                    if e < E:
                        for f in range(h_tiles):
                            n = e * h_tiles + f
                            dve.wait_ge(silued, n + 1)
                            dve.wait_ge(up_done, 2 * n + 2)
                            if e >= 2 and f == 0:
                                dve.wait_ge(down_done, e - 1)
                            nc.vector.tensor_tensor(k.hT[:, e % 2, f, :], c.ps[2 + n % 2][:], k.act[:, n % 2, :],
                                                    ALU.mult).then_inc(hid_ready, 1)
                    if e > 0:
                        d = e - 1
                        dve.wait_ge(down_done, d + 1)
                        if d >= 1:
                            dve.wait_ge(acc_done, QB * d)
                        for q in range(QB):
                            last = nc.vector.scalar_tensor_tensor(out=k.acc[:, q, :],
                                                                  in0=c.ps[4 + d % 2][:, q * P:(q + 1) * P],
                                                                  scalar=k.w_now[:, q, d:d + 1], in1=k.acc[:, q, :],
                                                                  op0=ALU.mult, op1=ALU.add)
                            last.then_inc(acc_done, 1)
                dve.wait_ge(acc_done, QB * E)
                nc.vector.tensor_copy(c.g[:, bass.ts(b, QB), :], k.acc[:]).then_inc(staged, 1)
        st.end()


class ExpertWork:
    pass


def layer3(nc, c, w):
    def plain(q_dram, k_dram, values, **loads):
        project_stage(nc, c, "p3", c.xnT, [(w["L3_attn_Wqvk"][:, 0:D], None, D ** -0.5, q_dram),
                                           (w["L3_attn_Wqvk"][:, 2 * D:3 * D], None, 1.0, k_dram)],
                      value=(w["L3_attn_Wqvk"][:, D:2 * D], values), split=True, **loads)

    def rotary(q_dram, k_dram, values, **loads):
        rms_stage(nc, c, w, "rms1", False, w["L3_ffn_g1"])
        tables = [w["rope_q_cos"], w["rope_q_sin"]], [w["rope_k_cos"], w["rope_k_sin"]]
        project_stage(nc, c, "p4", c.xnT,
                      [((w["L3_ffn_wq"], w["L3_ffn_wq_turned"]), None, tables[0], q_dram),
                       ((w["L3_ffn_wk"], w["L3_ffn_wk_turned"]), None, tables[1], k_dram)],
                      value=(w["L3_ffn_wv"], values), rope=True, split=True, **loads)

    narrow_attention(nc, c, "a3", plain, w["L3_attn_Wo"], c.s)
    narrow_attention(nc, c, "a4", rotary, w["L3_ffn_wo"], c.g)
    with ExitStack() as ctx:
        def sb(name, shape, dt=F32):
            return ctx.enter_context(nc.sbuf_tensor(f"l3_{name}", shape, dt))

        h_tiles = HID // P
        k = ExpertWork()
        k.weight = sb("weight", [P, TB, E])
        k.wg, k.wu = sb("wg", [P, E, HID]), sb("wu", [P, E, HID])
        k.wd = sb("wd", [P, E, h_tiles, D])
        k.hT = sb("hT", [P, 2, h_tiles, S])
        k.act = sb("act", [P, 2, S])
        k.acc = sb("acc", [P, QB, D])
        k.w_now = sb("w_now", [P, QB, E])
        weights = []
        for e in range(E):
            weights += [(k.wg[:, e, :], w["L3_ffn_wg"][e]), (k.wu[:, e, :], w["L3_ffn_wu"][e]),
                        (k.wd[:, e, :, :], w["L3_ffn_wd"][e].rearrange("(f p) d -> p f d", p=P))]
        rms_stage(nc, c, w, "rms2", True, w["L3_ffn_g2"], ahead=weights)
        top2_routing(nc, c, w, k.weight)
        with nc.Fori(0, NB) as b:
            gated_experts(nc, c, b, k)




class Buffers:

    def __init__(self, nc, ctx):
        def sb(name, shape, dt=F32):
            return ctx.enter_context(nc.sbuf_tensor(name, shape, dt))

        self.x = sb("x", [P, TB, D])
        self.xn = sb("xn", [P, TB, D])
        self.xnT = sb("xnT", [P, NB, S])
        self.s = sb("s", [P, TB, D])
        self.g = sb("g", [P, TB, D])
        self.ident = sb("ident", [P, P])
        self.ident16 = sb("ident16", [P, P], BF16)
        self.mask16 = sb("mask16", [P, P], BF16)
        self.ones = sb("ones", [P, P])
        self.table = nc.dram_tensor("table", (H, NPOS), F32, kind="Internal").ap()
        self.ps = [ctx.enter_context(nc.psum_tensor(f"ps{i}", [P, 512], F32)) for i in range(8)]


def build(nc, w, out):
    with ExitStack() as ctx:
        c = Buffers(nc, ctx)
        with ExitStack() as ld:
            st = Stage(nc, ld, "load")
            (loaded,) = st.sems("loaded")
            load_all(st, loaded, [(c.x[:, b * QB:(b + 1) * QB, :],
                                   w["L0_attn_latents"][b].rearrange("(q p) d -> p q d", p=P)) for b in range(NB)])
        make_constants(nc, c)

        with ExitStack() as early:
            c.xaT = early.enter_context(nc.sbuf_tensor("xaT", [P, NB, S], F32))
            norm_stage(nc, c, "n0", False, second=(w["L0_attn_ln_gamma"], w["L0_attn_ln_beta"]))
            recurrent_gate(nc, c, w)
            attention0(nc, c, w, c.xaT)

            norm_stage(nc, c, "n1", True, second=(w["L1_attn_ln_g"], w["L1_attn_ln_b"]))
            ternary_gate(nc, c, w)
            attention1(nc, c, w, c.xaT)

        norm_stage(nc, c, "n2", True, affine_s=(w["L1_attn_out_ln_g"], w["L1_attn_out_ln_b"]))
        layer2(nc, c, w)

        norm_stage(nc, c, "n3", True)
        layer3(nc, c, w)
        final_stage(nc, c, out)


_TRANSPOSED = ([f"L0_ffn_{n}" for n in ("wf", "uf", "wi", "ui", "wc", "uc", "wo", "uo")]
               + ["L1_ffn_W1", "L1_ffn_W2"] + [f"L2_attn_W{n}" for n in "qkvo"])
_TILED_BIASES = ("L1_ffn_b1", "L2_ffn_b1")


def _rope_tables():
    inv_freq = 1.0 / 10000.0 ** (np.arange(0, DN, 2, dtype=np.float32) / DN)
    freqs = np.einsum("i,j->ij", np.arange(S, dtype=np.float32), inv_freq)
    emb = np.concatenate([freqs, freqs], axis=-1).astype(np.float32)
    sign = np.where(np.arange(DN) < DN // 2, -1.0, 1.0).astype(np.float32)
    cos = np.tile(np.cos(emb).T, (H, 1)).astype(np.float32)
    sin = np.tile(np.sin(emb).T * sign[:, None], (H, 1)).astype(np.float32)
    scale = np.float32(DN ** -0.5)
    return {"rope_k_cos": cos, "rope_k_sin": sin, "rope_q_cos": cos * scale, "rope_q_sin": sin * scale}


def kernel(**inputs):
    import concourse.bacc as _bacc
    from concourse.bass_utils import run_bass_kernel_spmd as _run

    nc = _bacc.Bacc("TRN2", target_bir_lowering=False, num_devices=1)
    laid = {}
    for name, value in inputs.items():
        a = np.asarray(value)
        if name in _TRANSPOSED:
            laid[name + "T"] = a.T
        elif name in _TILED_BIASES:
            tiled = a.reshape(a.shape[:-1] + (a.shape[-1] // P, P))
            laid[name + "T"] = np.moveaxis(tiled, -1, 0)
        else:
            laid[name] = a
        if name in ("L3_ffn_wq", "L3_ffn_wk"):
            laid[name + "_turned"] = a.reshape(D, H, 2, DN // 2)[:, :, ::-1, :].reshape(D, D)
    laid.update(_rope_tables())
    arrays, w = {}, {}
    for name, a in laid.items():
        a = np.ascontiguousarray(a)
        arrays[f"in_{name}_dram"] = a
        w[name] = nc.dram_tensor(f"in_{name}_dram", a.shape, mybir.dt.from_np(a.dtype), kind="ExternalInput").ap()
    out = nc.dram_tensor("out_0_dram", (NB, S, D), F32, kind="ExternalOutput").ap()
    build(nc, w, out)
    r = _run(nc, [arrays], core_ids=[0])
    return r.results[0]["out_0_dram"]
```

```python
from contextlib import ExitStack

import numpy as np

import concourse.bass as bass
from concourse import mybir

F32 = mybir.dt.float32
BF16 = mybir.dt.bfloat16
F32R = mybir.dt.float32r
I32 = mybir.dt.int32
UPPER = -4096
ALU = mybir.AluOpType
ACT = mybir.ActivationFunctionType
AX = mybir.AxisListType.X

P = 128
NB, S, D = 8, 512, 128
QB = S // P
TB = NB * QB
H = 16
DH = 64
DN = D // H
FF = 512
E = 8
PACK = 4 * DN
HID = 384
LN_EPS = 1e-5
RMS_EPS = 1e-6
FIRST_SEM = 120
MASKED = 1e30
NPOS = 640


class Stage:

    def __init__(self, nc, ctx, name):
        self.nc, self.ctx, self.name, self.nums = nc, ctx, name, []

    def sems(self, *names):
        handles = []
        for n in names:
            num = FIRST_SEM + len(self.nums)
            handles.append(self.ctx.enter_context(self.nc.semaphore(f"{self.name}_{n}", num=num)))
            self.nums.append(num)
        return handles

    def sb(self, name, shape, dt=F32):
        return self.ctx.enter_context(self.nc.sbuf_tensor(f"{self.name}_{name}", shape, dt))

    def end(self):
        self.nc.all_engine_barrier(sems_to_clear=range(self.nums[0], self.nums[-1] + 1))


class Chain:

    def __init__(self, eng, sem):
        self.eng, self.sem, self.n = eng, sem, 0

    def mark(self, ins):
        ins.then_inc(self.sem, 1)
        self.n += 1

    def wait(self):
        self.eng.wait_ge(self.sem, self.n)

    def link(self, ins):
        self.mark(ins)
        self.wait()


def row_bcast(ap, n, parts=P):
    return bass.AP(tensor=ap.tensor, offset=ap.offset, ap=[[0, parts], [1, n]])


def column(ap):
    return ap.rearrange("(p o) -> p o", o=1)


def over_tokens(stat, n=D):
    return stat.broadcast_to([P, stat.shape[1], n])


def over_blocks(row, n=TB):
    return row.unsqueeze(1).broadcast_to([P, n, row.shape[1]])


def load_all(st, loaded, pairs):
    nc = st.nc
    with nc.Block() as block:
        @block.sync
        def _(sp):
            for dst, src in pairs:
                sp.dma_start(dst, src).then_inc(loaded, 16)
            sp.wait_ge(loaded, 16 * len(pairs))
    st.end()


def make_constants(nc, c):
    with ExitStack() as ctx:
        st = Stage(nc, ctx, "const")
        filled, shaped, narrowed = st.sems("filled", "shaped", "narrowed")
        mask = st.sb("mask", [P, P])
        with nc.Block() as block:
            @block.gpsimd
            def _(pool):
                nc.gpsimd.memset(c.ident[:], 0.0).then_inc(filled, 1)
                nc.gpsimd.memset(mask[:], 0.0).then_inc(filled, 1)
                nc.gpsimd.memset(c.ones[:], 1.0).then_inc(filled, 1)
                pool.wait_ge(filled, 3)
                nc.gpsimd.affine_select(out=c.ident[:], in_=c.ident[:], compare_op=ALU.not_equal, fill=1.0,
                                        base=0, pattern=[[-1, P]], channel_multiplier=1).then_inc(shaped, 1)
                nc.gpsimd.affine_select(out=mask[:], in_=mask[:], compare_op=ALU.is_ge, fill=-MASKED,
                                        base=0, pattern=[[-1, P]], channel_multiplier=1).then_inc(shaped, 1)

            @block.vector
            def _(dve):
                dve.wait_ge(shaped, 2)
                nc.vector.tensor_copy(c.ident16[:], c.ident[:]).then_inc(narrowed, 1)
                nc.vector.tensor_copy(c.mask16[:], mask[:]).then_inc(narrowed, 1)
        st.end()


GROUPS = 4
BLOCKS = TB // GROUPS
BY_DVE = BLOCKS // 4


def norm_stage(nc, c, name, combine, affine_s=None, second=None):
    if affine_s is not None:
        items = [("s", 0), ("s", 1), ("s", 2), ("x", 0), ("s", 3), ("x", 1), ("x", 2), ("x", 3)]
    elif second is not None:
        items = [("x", 0), ("x", 1), ("x", 2), ("a", 0), ("x", 3), ("a", 1), ("a", 2), ("a", 3)]
    else:
        items = [("x", g) for g in range(GROUPS)]
    place = {item: i for i, item in enumerate(items)}
    turns = [item for item in items if item[0] != "s"]
    with ExitStack() as ctx:
        st = Stage(nc, ctx, name)
        (var_ready, root_ready, factor_ready, dve_applied, act_applied, dve_done, gained, pool_done, turned, copied,
         loaded) = st.sems(
            "var_ready", "root_ready", "factor_ready", "dve_applied", "act_applied", "dve_done", "gained", "pool_done",
            "turned", "copied", "loaded")
        again = st.sb("again", [P, TB, D]) if second else None
        source = {"s": c.s, "x": c.x, "a": c.xn}
        target = {"s": c.s, "x": c.xn, "a": again}
        kinds = {kind for kind, _ in items}
        stats = {kind: st.sb("stats_" + kind, [P, TB, 6]) for kind in kinds}
        mv = {kind: st.sb("mv_" + kind, [P, TB, 2]) for kind in kinds}
        root = {kind: st.sb("root_" + kind, [P, TB, 1]) for kind in kinds}
        factor = {kind: st.sb("factor_" + kind, [P, TB, 1]) for kind in kinds}
        shift = {kind: st.sb("shift_" + kind, [P, TB, 1]) for kind in kinds}
        rows = []
        if affine_s is not None:
            rows = [(st.sb("s_gain", [P, D]), row_bcast(affine_s[0], D)),
                    (st.sb("s_shift", [P, D]), row_bcast(affine_s[1], D))]
        if second is not None:
            rows += [(st.sb("a_gain", [P, 1]), column(second[0])), (st.sb("a_shift", [P, 1]), column(second[1]))]

        def span(g):
            return slice(g * BLOCKS, (g + 1) * BLOCKS)

        def wait_normed(eng, item):
            eng.wait_ge(dve_applied, place[item] + 1)
            eng.wait_ge(act_applied, place[item] + 1)

        with nc.Block() as block:
            @block.sync
            def _(sp):
                for dst, src in rows:
                    sp.dma_start(dst[:], src).then_inc(loaded, 16)

            if combine:
                @block.gpsimd
                def _(pool):
                    if affine_s is not None:
                        pool.wait_ge(loaded, 16 * len(rows))
                    for g in range(GROUPS):
                        s, gate = c.s[:, span(g), :], c.g[:, span(g), :]
                        if affine_s is not None:
                            wait_normed(pool, ("s", g))
                            nc.gpsimd.tensor_tensor(s, s, over_blocks(rows[0][0][:], BLOCKS),
                                                    ALU.mult).then_inc(gained, 1)
                            pool.wait_ge(gained, g + 1)
                            nc.gpsimd.tensor_tensor(s, s, over_blocks(rows[1][0][:], BLOCKS),
                                                    ALU.add).then_inc(pool_done, 1)
                        else:
                            nc.gpsimd.tensor_tensor(gate, s, gate, ALU.mult).then_inc(pool_done, 1)

            @block.vector
            def _(dve):
                chain = Chain(dve, dve_done)

                def add_up(g):
                    s, gate, x = (t[:, span(g), :] for t in (c.s, c.g, c.x))
                    dve.wait_ge(pool_done, g + 1)
                    if affine_s is not None:
                        chain.link(nc.vector.tensor_tensor(gate, s, gate, ALU.mult))
                    chain.link(nc.vector.tensor_tensor(x, x, gate, ALU.add))

                def finish(i):
                    kind, g = items[i]
                    at = span(g)
                    dve.wait_ge(root_ready, i + 1)
                    chain.link(nc.vector.reciprocal(factor[kind][:, at], root[kind][:, at]))
                    nc.vector.scalar_tensor_tensor(out=shift[kind][:, at], in0=mv[kind][:, at, 0:1], scalar=-1.0,
                                                   in1=factor[kind][:, at], op0=ALU.mult,
                                                   op1=ALU.mult).then_inc(factor_ready, 1)
                    dve.wait_ge(factor_ready, i + 1)
                    for t in range(g * BLOCKS, g * BLOCKS + BY_DVE):
                        last = nc.vector.tensor_scalar(target[kind][:, t, :], source[kind][:, t, :],
                                                       factor[kind][:, t, :], shift[kind][:, t, :], ALU.mult, ALU.add)
                    last.then_inc(dve_applied, 1)

                for i, (kind, g) in enumerate(items):
                    if kind == "a":
                        wait_normed(dve, ("x", g))
                    if kind == "x" and combine:
                        add_up(g)
                    for t in range(g * BLOCKS, (g + 1) * BLOCKS):
                        chain.mark(nc.vector.bn_stats(stats[kind][:, t, :], source[kind][:, t, :]))
                    chain.wait()
                    for t in range(g * BLOCKS, (g + 1) * BLOCKS):
                        chain.mark(nc.vector.bn_aggr(mv[kind][:, t, :], stats[kind][:, t, :]))
                    chain.wait()
                    nc.vector.tensor_scalar(root[kind][:, span(g)], mv[kind][:, span(g), 1:2], LN_EPS, None,
                                            ALU.add).then_inc(var_ready, 1)
                    if i > 0:
                        finish(i - 1)
                finish(len(items) - 1)

            @block.tensor
            def _(pe):
                n = 0
                for kind, g in turns:
                    wait_normed(pe, (kind, g))
                    for b in range(g * BLOCKS // QB, (g + 1) * BLOCKS // QB):
                        if n >= 4:
                            pe.wait_ge(copied, n - 3)
                        for q in range(QB):
                            last = nc.tensor.transpose(c.ps[n % 4][:, q * P:(q + 1) * P],
                                                       target[kind][:, b * QB + q, :], c.ident[:])
                        last.then_inc(turned, 1)
                        n += 1

            @block.scalar
            def _(act):
                if second is not None:
                    act.wait_ge(loaded, 16 * len(rows))
                n = 0
                for i in range(len(items) + 2):
                    if i < len(items):
                        kind, g = items[i]
                        act.wait_ge(var_ready, i + 1)
                        nc.scalar.activation(root[kind][:, span(g)], root[kind][:, span(g)],
                                             ACT.Sqrt).then_inc(root_ready, 1)
                    if 0 < i <= len(items):
                        kind, g = items[i - 1]
                        act.wait_ge(factor_ready, i)
                        for t in range(g * BLOCKS + BY_DVE, (g + 1) * BLOCKS):
                            last = nc.scalar.activation(target[kind][:, t, :], source[kind][:, t, :], ACT.Identity,
                                                        bias=shift[kind][:, t, :], scale=factor[kind][:, t, :])
                        last.then_inc(act_applied, 1)
                    if i > 1 and items[i - 2] in turns:
                        kind, g = items[i - 2]
                        for b in range(g * BLOCKS // QB, (g + 1) * BLOCKS // QB):
                            act.wait_ge(turned, n + 1)
                            if kind == "x":
                                nc.scalar.activation(c.xnT[:, b, :], c.ps[n % 4][:], ACT.Copy).then_inc(copied, 1)
                            else:
                                nc.scalar.activation(c.xaT[:, b, :], c.ps[n % 4][:], ACT.Identity,
                                                     bias=rows[-1][0][:], scale=rows[-2][0][:]).then_inc(copied, 1)
                            n += 1
        st.end()


def final_stage(nc, c, out):
    with ExitStack() as ctx:
        st = Stage(nc, ctx, "final")
        silued, product, ready, stored = st.sems("silued", "product", "ready", "stored")
        with nc.Block() as block:
            @block.scalar
            def _(act):
                for b in range(NB):
                    g = c.g[:, b * QB:(b + 1) * QB, :]
                    nc.scalar.activation(g, g, ACT.Silu).then_inc(silued, 1)

            @block.vector
            def _(dve):
                for b in range(NB):
                    g, s, x = (t[:, b * QB:(b + 1) * QB, :] for t in (c.g, c.s, c.x))
                    dve.wait_ge(silued, b + 1)
                    nc.vector.tensor_tensor(g, s, g, ALU.mult).then_inc(product, 1)
                    dve.wait_ge(product, b + 1)
                    nc.vector.tensor_tensor(x, x, g, ALU.add).then_inc(ready, 1)

            @block.sync
            def _(sp):
                for b in range(NB):
                    sp.wait_ge(ready, b + 1)
                    sp.dma_start(out[b].rearrange("(q p) d -> p q d", p=P),
                                 c.x[:, b * QB:(b + 1) * QB, :]).then_inc(stored, 16)
                sp.wait_ge(stored, 16 * NB)
        st.end()


def recurrent_gate(nc, c, w, ahead=()):
    with ExitStack() as ctx:
        st = Stage(nc, ctx, "g0")
        loaded, cpart, gated, dve_done, cready, cu_ready, cu_added, h_ready, h_added, tanhed, came_ahead = st.sems(
            "loaded", "cpart", "gated", "dve_done", "cready", "cu_ready", "cu_added", "h_ready", "h_added",
            "tanhed", "came_ahead")
        names = ["wf", "uf", "wi", "ui", "wc", "uc", "wo", "uo"]
        wt = {n: st.sb(n, [P, D]) for n in names}
        bias = {n: st.sb(n, [P, 1]) for n in ("bf", "bi", "bc")}
        bo_row = st.sb("bo_row", [P, D])
        c_first = st.sb("c_first", [P, 1])
        cT = st.sb("cT", [P, 2, S])
        gate = st.sb("gate", [P, 2, 3, S])
        keep = st.sb("keep", [P, S])
        cu = st.sb("cu", [P, QB, D])
        n_loads = len(names) + 3 + 2

        with nc.Block() as block:
            @block.sync
            def _(sp):
                for n in names:
                    sp.dma_start(wt[n][:], w[f"L0_ffn_{n}T"]).then_inc(loaded, 16)
                for n in bias:
                    sp.dma_start(bias[n][:], column(w[f"L0_ffn_{n}"])).then_inc(loaded, 16)
                sp.dma_start(c_first[:], column(w["L0_ffn_in_c"])).then_inc(loaded, 16)
                sp.dma_start(bo_row[:], row_bcast(w["L0_ffn_bo"], D)).then_inc(loaded, 16)
                for dst, src in ahead:
                    sp.dma_start(dst, src).then_inc(came_ahead, 16)
                if ahead:
                    sp.wait_ge(came_ahead, 16 * len(ahead))

            @block.tensor
            def _(pe):
                pe.wait_ge(loaded, 16 * n_loads)

                def from_input(t):
                    if t >= 2:
                        pe.wait_ge(gated, 3 * (t - 1))
                    for k, n in enumerate("fic"):
                        nc.tensor.matmul(c.ps[3 * (t % 2) + k][:], wt["w" + n][:], c.xnT[:, t, :], start=True,
                                         stop=False)

                from_input(0)
                for t in range(NB):
                    pe.wait_ge(cready, t + 1)
                    for k, n in enumerate("fic"):
                        nc.tensor.matmul(c.ps[3 * (t % 2) + k][:], wt["u" + n][:], cT[:, t % 2, :], start=False,
                                         stop=True).then_inc(cpart, 1)
                    if t + 1 < NB:
                        from_input(t + 1)
                pe.wait_ge(cready, NB + 1)
                for q in range(QB):
                    last = nc.tensor.matmul(c.ps[6][:, q * P:(q + 1) * P], cT[:, NB % 2, q * P:(q + 1) * P],
                                            wt["uo"][:], start=True, stop=True)
                last.then_inc(cu_ready, 1)
                for b in range(NB):
                    if b == 0:
                        pe.wait_ge(gated, 3 * NB)
                    if b >= 4:
                        pe.wait_ge(h_added, b - 3)
                    for q in range(QB):
                        last = nc.tensor.matmul(c.ps[b % 4][:, q * P:(q + 1) * P], c.xnT[:, b, q * P:(q + 1) * P],
                                                wt["wo"][:], start=True, stop=True)
                    last.then_inc(h_ready, 1)

            @block.scalar
            def _(act):
                act.wait_ge(loaded, 16 * n_loads)
                for t in range(NB):
                    for k, n in enumerate("fic"):
                        act.wait_ge(cpart, 3 * t + k + 1)
                        if t >= 2 and k == 0:
                            act.wait_ge(cready, t)
                        nc.scalar.activation(gate[:, t % 2, k, :], c.ps[3 * (t % 2) + k][:],
                                             ACT.Tanh if n == "c" else ACT.Sigmoid,
                                             bias=bias["b" + n][:]).then_inc(gated, 1)
                for b in range(NB):
                    act.wait_ge(h_added, b + 1)
                    g = c.g[:, b * QB:(b + 1) * QB, :]
                    nc.scalar.activation(g, g, ACT.Tanh).then_inc(tanhed, 1)
                act.wait_ge(tanhed, NB)
                nc.scalar.activation(c.g[:], c.g[:], ACT.Silu).then_inc(tanhed, 1)

            @block.vector
            def _(dve):
                chain = Chain(dve, dve_done)
                dve.wait_ge(loaded, 16 * n_loads)
                chain.link(nc.vector.memset(keep[:], 0.0))
                nc.vector.tensor_scalar(cT[:, 0, :], keep[:], c_first[:], None, ALU.add).then_inc(cready, 1)
                for t in range(NB):
                    f, i, g = (gate[:, t % 2, k, :] for k in range(3))
                    dve.wait_ge(gated, 3 * t + 1)
                    dve.wait_ge(cready, t + 1)
                    chain.mark(nc.vector.tensor_tensor(keep[:], f, cT[:, t % 2, :], ALU.mult))
                    dve.wait_ge(gated, 3 * t + 3)
                    chain.link(nc.vector.tensor_tensor(i, i, g, ALU.mult))
                    nc.vector.tensor_tensor(cT[:, (t + 1) % 2, :], keep[:], i, ALU.add).then_inc(cready, 1)
                dve.wait_ge(cu_ready, 1)
                nc.vector.tensor_tensor(cu[:], c.ps[6][:].rearrange("p (q d) -> p q d", d=D),
                                        over_blocks(bo_row[:], QB), ALU.add).then_inc(cu_added, 1)
                dve.wait_ge(cu_added, 1)
                for b in range(NB):
                    dve.wait_ge(h_ready, b + 1)
                    nc.vector.tensor_tensor(c.g[:, b * QB:(b + 1) * QB, :],
                                            c.ps[b % 4][:].rearrange("p (q d) -> p q d", d=D), cu[:],
                                            ALU.add).then_inc(h_added, 1)
        st.end()


UNITS = QB * H
GROUP = 4
LAG_T, LAG_AV = 3, 5
PROBS = LAG_T + 1
TURNED = LAG_AV - LAG_T + 1
S_BANKS, T_BANK, O_BANK, Y_BANK = 3, 3, 5, 7


class Heads:

    def __init__(self, name, width, causal, bias=None, shared_kv=False, projected=False, dst=None):
        self.name, self.width, self.causal = name, width, causal
        self.bias = bias
        self.shared_kv = shared_kv
        self.projected = projected
        self.dst = dst
        self.inner = H * width
        self.tiles = self.inner // P
        self.rounds = max(1, self.tiles // 4)
        self.batches = 1 if projected else 2

    def keys(self, n):
        return n % UNITS // H + 1 if self.causal else QB

    def events(self):
        out = {}
        for block in range(self.batches * QB):
            done = H * (block + 1) + LAG_AV
            for r in range(self.rounds + 1):
                out[done + 2 + 2 * r] = (block, r)
        return out

    def scores(self, k, n):
        batch, (qb, h) = n // UNITS, divmod(n % UNITS, H)
        queries, keys = slice(qb * P, (qb + 1) * P), slice(0, self.keys(n) * P)
        if not self.projected:
            rows = slice(PACK * (h % 4), PACK * (h % 4 + 1))
            return k.QT[batch][rows, h // 4, queries].bitcast(F32R), k.KT[batch][rows, h // 4, keys].bitcast(F32R)
        if self.shared_kv:
            return k.QT[:, h // 2, queries], k.KT[:, h % 2, keys]
        rows = slice(DH * (h % 2), DH * (h % 2 + 1))
        return k.QT[rows, h // 2, queries], k.KT[rows, h // 2, keys]

    def values(self, k, n, block):
        h = n % H
        if not self.projected:
            return k.V[n // UNITS][:, block, :]
        return k.V[:, block, :] if self.shared_kv else k.V[:, block, h // 2 * P:(h // 2 + 1) * P]

    def outputs(self, bank, group):
        if not self.projected:
            offset, step = group % (H // GROUP) * GROUP * self.width, P + self.width
        else:
            offset, step = 0, P
        odd = P + DH if self.projected and not self.shared_kv else step
        return bass.AP(tensor=bank[:].tensor, offset=offset, ap=[[512, P], [2 * step, 2], [odd, 2], [1, self.width]])


def attention_stage(nc, c, a, b, w, load_qkv=None, tag=""):
    R = a.rounds + 1
    units, groups = a.batches * UNITS, a.batches * UNITS // GROUP
    steps = units + LAG_AV + 3 + 2 * R
    events = a.events()
    with ExitStack() as ctx:
        st = Stage(nc, ctx, a.name + "u")
        (x_ready, loaded, projected, act_copied, dve_copied, scored, maxed, exped, turned, pt_ready, av_done,
         dve_done, o_ready, y_made, y_copied) = st.sems(
            "x_ready", "loaded", "projected", "act_copied", "dve_copied", "scored", "maxed", "exped", "turned",
            "pt_ready", "av_done", "dve_done", "o_ready", "y_made", "y_copied")
        if load_qkv is not None:
            (loaded_next,) = st.sems("loaded_next")
        if a.shared_kv:
            null_scored, null_gap, null_exped, null_spread = st.sems(
                "null_scored", "null_gap", "null_exped", "null_spread")
        QT, KT, V, probs, PT, sums, top, O, OT, rinv = w.QT, w.KT, w.V, w.probs, w.PT, w.sums, w.top, w.O, w.OT, w.rinv

        jobs = []
        if a.projected:
            jobs = [("q", t) for t in range(a.tiles)]
            if a.shared_kv:
                jobs += [("k1", 0), ("v1", 0)]
            else:
                jobs += [("k", t) for t in range(a.tiles)]
                jobs += [("v", t) for t in range(2 * QB)]
        bank_of = (0, 1, 2, Y_BANK)

        def copied_before(eng, j):
            if j > 0:
                eng.wait_ge(act_copied, (j + 1) // 2)
            if j > 1:
                eng.wait_ge(dve_copied, j // 2)

        def copies(kind, t, j):
            bank = c.ps[bank_of[j % 4]]
            if kind == "k1":
                return [(KT[DH * i:DH * (i + 1), i, :], bank[DH * i:DH * (i + 1), :]) for i in range(2)]
            if kind == "v1":
                return [(V[:].rearrange("p q d -> p (q d)"), bank[:])]
            if kind == "v":
                return [(V[:, t // 2, (t % 2) * 512:(t % 2 + 1) * 512], bank[:])]
            return [((QT if kind == "q" else KT)[:, t, :], bank[:])]

        with nc.Block(no_gpsimd_drain=True) as block:
            if load_qkv is not None:
                @block.sync
                def _(sp):
                    load_qkv(sp, b + 1, 1, loaded)
                    sp.wait_ge(scored, UNITS)
                    load_qkv(sp, b + 2, 0, loaded_next)
                    sp.wait_ge(loaded_next, 16 * w.n_loads)

            @block.gpsimd
            def _(pool):
                if a.projected:
                    nc.gpsimd.tensor_copy(w.xT[:], w.source[:, b, :]).then_inc(x_ready, 1)
                else:
                    for i in range(a.batches):
                        nc.gpsimd.tensor_copy(V[i][:], w.source[:, bass.ts(b + i, QB), :]).then_inc(x_ready, 1)
                if a.shared_kv:
                    for hf in range(groups):
                        pool.wait_ge(null_exped, hf + 1)
                        if hf >= 2:
                            pool.wait_ge(o_ready, hf - 1)
                        nc.gpsimd.tensor_tensor(
                            w.null_part[:, hf % 2, :, :],
                            w.null_weight[:, hf % 2, :].unsqueeze(2).broadcast_to([P, GROUP, DH]),
                            w.null_v[:].unsqueeze(1).broadcast_to([P, GROUP, DH]), ALU.mult).then_inc(null_spread, 1)

            @block.tensor
            def _(pe):
                x_now = w.source[:, b, :] if a.projected else None
                for j, (kind, t) in enumerate(jobs):
                    if j >= 4:
                        copied_before(pe, j - 3)
                    if kind in ("v", "v1"):
                        pe.wait_ge(x_ready, 1)
                    bank = c.ps[bank_of[j % 4]]
                    if kind == "q":
                        last = nc.tensor.matmul(bank[:], w.wq[:, t * P:(t + 1) * P], x_now, start=True, stop=True)
                    elif kind in ("k", "k1"):
                        last = nc.tensor.matmul(bank[:], w.wk[:, t * P:(t + 1) * P], x_now, start=True, stop=True)
                    elif kind == "v":
                        q, half = t // 2, t % 2
                        last = nc.tensor.matmul(bank[:], w.xT[:, q * P:(q + 1) * P],
                                                w.wv[:, half * 512:(half + 1) * 512], start=True, stop=True)
                    else:
                        for q in range(QB):
                            last = nc.tensor.matmul(bank[:, q * P:(q + 1) * P], w.xT[:, q * P:(q + 1) * P],
                                                    w.wv[:], start=True, stop=True)
                    last.then_inc(projected, 1)
                copied_before(pe, len(jobs))
                if a.shared_kv:
                    for q in range(QB):
                        last = nc.tensor.matmul(c.ps[Y_BANK][:, q * H:(q + 1) * H], w.xT[:, q * P:(q + 1) * P],
                                                w.null_w[:], start=True, stop=True)
                    last.then_inc(null_scored, 1)

                for n in range(steps):
                    if n < units:
                        if load_qkv is not None and n == UNITS:
                            pe.wait_ge(loaded, 16 * w.n_loads)
                        qb = n % UNITS // H
                        queries, keys = a.scores(w, n)
                        bank = c.ps[n % S_BANKS]
                        if n >= S_BANKS:
                            pe.wait_ge(maxed if a.bias is not None else exped, n - S_BANKS + 1)
                        last = nc.tensor.matmul(bank[:, 0:a.keys(n) * P], queries, keys, start=True,
                                                stop=not a.causal or a.bias is not None)
                        if a.causal and a.bias is None:
                            last = nc.tensor.matmul(bank[:, qb * P:(qb + 1) * P], c.ident16[:], c.mask16[:],
                                                    start=False, stop=True)
                        last.then_inc(scored, 1)
                    m = n - LAG_T
                    if 0 <= m < units:
                        pe.wait_ge(exped, m + 1)
                        if m >= 2:
                            pe.wait_ge(pt_ready, m - 1)
                        for k in range(a.keys(m)):
                            last = nc.tensor.transpose(c.ps[T_BANK + m % 2][:, k * P:(k + 1) * P],
                                                       probs[:, m % PROBS, k * P:(k + 1) * P], c.ident[:])
                        last.then_inc(turned, 1)
                    m = n - LAG_AV
                    if 0 <= m < units:
                        hf = m // GROUP
                        if not a.projected and m % UNITS == 0:
                            pe.wait_ge(x_ready, m // UNITS + 1)
                        pe.wait_ge(pt_ready, m + 1)
                        if m % GROUP == 0 and hf >= 2:
                            pe.wait_ge(o_ready, hf - 1)
                        for k in range(a.keys(m)):
                            last = nc.tensor.matmul(
                                c.ps[O_BANK + hf % 2][:, (m % GROUP) * P:(m % GROUP + 1) * P],
                                PT[:, m % TURNED, k * P:(k + 1) * P], a.values(w, m, k), start=k == 0, stop=k == a.keys(m) - 1)
                        last.then_inc(av_done, 1)
                    if n in events:
                        qb, r = events[n]
                        if qb == 0 and r == 0 and a.shared_kv:
                            pe.wait_ge(null_gap, 1)
                        if R * qb + r > 0:
                            pe.wait_ge(y_copied, R * qb + r)
                        y = c.ps[Y_BANK]
                        if r < a.rounds:
                            pe.wait_ge(o_ready, H // GROUP * (qb + 1))
                            count = min(4, a.tiles)
                            for k in range(count):
                                t = 4 * r + k
                                last = nc.tensor.transpose(y[:, k * P:(k + 1) * P], O[:, qb % 2, t * P:(t + 1) * P],
                                                           c.ident[:])
                        else:
                            for t in range(a.tiles):
                                last = nc.tensor.matmul(y[:, 0:D], OT[:, t, :], w.wo[:, t, :],
                                                        start=t == 0, stop=t == a.tiles - 1)
                        last.then_inc(y_made, 1)

            @block.scalar
            def _(act):
                for j in range(0, len(jobs), 2):
                    kind, t = jobs[j]
                    act.wait_ge(projected, j + 1)
                    for dst, src in copies(kind, t, j):
                        last = nc.scalar.activation(dst, src, ACT.Copy, scale=w.q_scale if kind == "q" else 1.0)
                    last.then_inc(act_copied, 1)
                for n in range(steps + 1):
                    if n < units:
                        width = a.keys(n) * P
                        act.wait_ge(maxed, n + 1)
                        if n >= PROBS:
                            act.wait_ge(turned, n - PROBS + 1)
                        src = w.biased[:, n % 3, 0:width] if a.bias is not None else c.ps[n % S_BANKS][:, 0:width]
                        nc.scalar.activation(probs[:, n % PROBS, 0:width], src, ACT.Exp, bias=top[:, n:n + 1],
                                             scale=-1.0 if a.bias is not None else 1.0,
                                             accum_out=sums[:, n:n + 1]).then_inc(exped, 1)
                    if a.shared_kv and n % GROUP == 2 and n >= GROUP:
                        hf = n // GROUP - 1
                        if hf < groups:
                            act.wait_ge(null_gap, hf + 2)
                            if hf >= 2:
                                act.wait_ge(o_ready, hf - 1)
                            nc.scalar.activation(w.null_weight[:, hf % 2, :], w.null_less[:, hf, :],
                                                 ACT.Exp).then_inc(null_exped, 1)
                    if n - 1 in events:
                        qb, r = events[n - 1]
                        act.wait_ge(y_made, R * qb + r + 1)
                        y = c.ps[Y_BANK]
                        if r < a.rounds:
                            count = min(4, a.tiles)
                            nc.scalar.activation(OT[:, 4 * r:4 * r + count, :].rearrange("p t q -> p (t q)"),
                                                 y[:, 0:count * P], ACT.Copy).then_inc(y_copied, 1)
                        else:
                            nc.scalar.activation(a.dst[:, b * QB + qb, :], y[:, 0:D], ACT.Copy).then_inc(y_copied, 1)

            @block.vector
            def _(dve):
                chain = Chain(dve, dve_done)
                for j in range(1, len(jobs), 2):
                    kind, t = jobs[j]
                    dve.wait_ge(projected, j + 1)
                    for dst, src in copies(kind, t, j):
                        last = nc.vector.tensor_scalar(dst, src, w.q_scale if kind == "q" else 1.0, None, ALU.mult)
                    last.then_inc(dve_copied, 1)
                if a.shared_kv:
                    dve.wait_ge(null_scored, 1)
                    nc.vector.tensor_tensor(w.null_s[:], c.ps[Y_BANK][:, 0:UNITS], w.null_bias[:],
                                            ALU.add).then_inc(null_gap, 1)
                    dve.wait_ge(null_gap, 1)
                for n in range(steps + 1):
                    if n < units:
                        h = n % H
                        width = a.keys(n) * P
                        dve.wait_ge(scored, n + 1)
                        if a.bias is not None:
                            if n >= 3:
                                dve.wait_ge(exped, n - 2)
                            nc.vector.tensor_tensor_reduce(
                                out=w.biased[:, n % 3, 0:width], in0=c.ps[n % S_BANKS][:, 0:width],
                                in1=a.bias[:, h, S - width:S], scale=1.0, scalar=w.null_s[:, n:n + 1],
                                op0=ALU.add, op1=ALU.min, accum_out=top[:, n:n + 1]).then_inc(maxed, 1)
                        else:
                            nc.vector.tensor_reduce(top[:, n:n + 1], c.ps[n % S_BANKS][:, 0:width], AX, ALU.max,
                                                    negate=True).then_inc(maxed, 1)
                    m = n - LAG_T
                    if 0 <= m < units:
                        width = a.keys(m) * P
                        dve.wait_ge(turned, m + 1)
                        if m >= TURNED:
                            dve.wait_ge(av_done, m - TURNED + 1)
                        nc.vector.tensor_copy(PT[:, m % TURNED, 0:width],
                                              c.ps[T_BANK + m % 2][:, 0:width]).then_inc(pt_ready, 1)
                    if a.shared_kv and n % GROUP == 1 and n >= GROUP and n // GROUP - 1 < groups:
                        hf = n // GROUP - 1
                        dve.wait_ge(maxed, GROUP * (hf + 1))
                        nc.vector.tensor_tensor(w.null_less[:, hf, :], top[:, hf * GROUP:(hf + 1) * GROUP],
                                                w.null_s[:, hf * GROUP:(hf + 1) * GROUP],
                                                ALU.subtract).then_inc(null_gap, 1)
                    m = n - LAG_AV
                    if m % GROUP == 0 and 0 < m <= units:
                        hf = m // GROUP - 1
                        block_, g = divmod(hf, H // GROUP)
                        dve.wait_ge(av_done, GROUP * (hf + 1))
                        if block_ >= 2 and g == 0:
                            dve.wait_ge(y_made, R * (block_ - 2) + a.rounds)
                        n4 = slice(hf * GROUP, (hf + 1) * GROUP)
                        heads = a.outputs(c.ps[O_BANK + hf % 2], hf)
                        if a.shared_kv:
                            dve.wait_ge(null_spread, hf + 1)
                            part = w.null_part[:, hf % 2, :, :].rearrange("p (a b) d -> p a b d", b=2)
                            chain.mark(nc.vector.tensor_tensor(part, part, heads, ALU.add))
                            chain.link(nc.vector.tensor_tensor(sums[:, n4], sums[:, n4],
                                                               w.null_weight[:, hf % 2, :], ALU.add))
                            heads = part
                        chain.link(nc.vector.reciprocal(rinv[:, hf % 2, :], sums[:, n4]))
                        span = GROUP * a.width
                        over_sum = rinv[:, hf % 2, :].rearrange("p (a b) -> p a b", b=2).unsqueeze(3)
                        nc.vector.tensor_tensor(
                            O[:, block_ % 2, g * span:(g + 1) * span].rearrange("p (a b d) -> p a b d", b=2,
                                                                               d=a.width),
                            heads, over_sum.broadcast_to([P, 2, 2, a.width]), ALU.mult).then_inc(o_ready, 1)
        st.end()


class Work:

    def __init__(self, nc, ctx, a, wo=None):
        def sb(name, shape, dt=F32):
            return ctx.enter_context(nc.sbuf_tensor(f"{a.name}_{name}", shape, dt))

        self.sb = sb
        self.probs = sb("probs", [P, PROBS, S])
        self.PT = sb("PT", [P, TURNED, S])
        self.sums = sb("sums", [P, a.batches * UNITS])
        self.top = sb("top", [P, a.batches * UNITS])
        self.rinv = sb("rinv", [P, 2, GROUP])
        self.O = sb("O", [P, 2, a.inner])
        self.OT = sb("OT", [P, a.tiles, P])
        self.wo = sb("wo", [P, a.tiles, D]) if wo is None else wo
        self.n_loads = 0


def layer0(nc, c, w, xaT):
    with ExitStack() as ctx:
        a = Heads("a0", DH, causal=False, projected=True, dst=c.s)
        wq, wk, wv = (ctx.enter_context(nc.sbuf_tensor(f"a0_{n}", [P, a.inner], F32)) for n in ("wq", "wk", "wv"))
        wo = ctx.enter_context(nc.sbuf_tensor("a0_wo", [P, a.tiles, D], F32))
        recurrent_gate(nc, c, w, ahead=[(wq[:], w["L0_attn_Wq"]), (wk[:], w["L0_attn_Wk"]), (wv[:], w["L0_attn_Wv"]),
                                        (wo[:], w["L0_attn_Wo"].rearrange("(t p) d -> p t d", p=P))])
        k = Work(nc, ctx, a, wo=wo)
        k.wq, k.wk, k.wv = wq, wk, wv
        k.xT = k.sb("xT", [P, S])
        k.QT = k.sb("QT", [P, a.tiles, S])
        k.KT = k.sb("KT", [P, a.tiles, S])
        k.V = k.sb("V", [P, QB, a.inner])
        k.q_scale = DH ** -0.5
        k.source = xaT
        with nc.Fori(0, NB) as b:
            attention_stage(nc, c, a, b, k)




def position_table(nc, c, w):
    tiles = NPOS // P
    with ExitStack() as ctx:
        st = Stage(nc, ctx, "pb")
        (loaded, pos_ready, dve_done, var_ready, root_ready, silued, turned, copied, h_ready, table,
         written) = st.sems("loaded", "pos_ready", "dve_done", "var_ready", "root_ready", "silued", "turned", "copied",
                            "h_ready", "table", "written")
        names = ["w0", "b0", "ln0_g", "ln0_b", "b1", "ln1_g", "ln1_b"]
        row = {n: st.sb(n, [P, D]) for n in names}
        w1 = st.sb("w1", [P, D])
        w2 = st.sb("w2", [P, H])
        b2 = st.sb("b2", [H, 1])
        pos = st.sb("pos", [P, tiles])
        hid = st.sb("hid", [P, tiles, D])
        hidT = st.sb("hidT", [P, NPOS])
        stats = st.sb("stats", [P, tiles, 6])
        mv = st.sb("mv", [P, tiles, 2])
        rstd = st.sb("rstd", [P, tiles, 1])
        minus = st.sb("minus", [H, NPOS])
        n_loads = len(names) + 3

        with nc.Block() as block:
            @block.sync
            def _(sp):
                for n in names:
                    sp.dma_start(row[n][:], row_bcast(w["L1_attn_pb_" + n], D)).then_inc(loaded, 16)
                sp.dma_start(w1[:], w["L1_attn_pb_w1"]).then_inc(loaded, 16)
                sp.dma_start(w2[:], w["L1_attn_pb_w2"]).then_inc(loaded, 16)
                sp.dma_start(b2[:], column(w["L1_attn_pb_b2"])).then_inc(loaded, 16)
                sp.wait_ge(table, 2)
                sp.dma_start(c.table, minus[:]).then_inc(written, 16)
                sp.wait_ge(written, 16)

            @block.gpsimd
            def _(pool):
                nc.gpsimd.iota(pos[:], pattern=[[-P, tiles]], base=S - 1, channel_multiplier=-1,
                               allow_small_or_imprecise_dtypes=True).then_inc(pos_ready, 1)

            @block.vector
            def _(dve):
                chain = Chain(dve, dve_done)
                dve.wait_ge(loaded, 16 * n_loads)
                dve.wait_ge(pos_ready, 1)
                for t in range(tiles):
                    chain.mark(nc.vector.scalar_tensor_tensor(out=hid[:, t, :], in0=row["w0"][:],
                                                              scalar=pos[:, t:t + 1], in1=row["b0"][:],
                                                              op0=ALU.mult, op1=ALU.add))
                chain.wait()
                for layer in range(2):
                    gain, shift = row[f"ln{layer}_g"], row[f"ln{layer}_b"]
                    if layer == 1:
                        dve.wait_ge(h_ready, tiles)
                        for t in range(tiles):
                            chain.mark(nc.vector.tensor_tensor(hid[:, t, :], c.ps[4 + t // 4][:, (t % 4) * P:(t % 4 + 1) * P],
                                                               row["b1"][:], ALU.add))
                        chain.wait()
                    for t in range(tiles):
                        chain.mark(nc.vector.bn_stats(stats[:, t, :], hid[:, t, :]))
                    chain.wait()
                    for t in range(tiles):
                        chain.mark(nc.vector.bn_aggr(mv[:, t, :], stats[:, t, :]))
                    chain.wait()
                    nc.vector.tensor_scalar(rstd[:], mv[:, :, 1:2], LN_EPS, None, ALU.add).then_inc(var_ready, 1)
                    dve.wait_ge(root_ready, layer + 1)
                    chain.link(nc.vector.reciprocal(rstd[:], rstd[:]))
                    for t in range(tiles):
                        chain.mark(nc.vector.tensor_scalar(hid[:, t, :], hid[:, t, :], mv[:, t, 0:1], rstd[:, t, :],
                                                           ALU.subtract, ALU.mult))
                    chain.wait()
                    chain.link(nc.vector.tensor_tensor(hid[:], hid[:], over_blocks(gain[:], tiles), ALU.mult))
                    nc.vector.tensor_tensor(hid[:], hid[:], over_blocks(shift[:], tiles),
                                            ALU.add).then_inc(var_ready, 1)

            @block.scalar
            def _(act):
                for layer in range(2):
                    act.wait_ge(var_ready, 2 * layer + 1)
                    nc.scalar.activation(rstd[:], rstd[:], ACT.Sqrt).then_inc(root_ready, 1)
                    act.wait_ge(var_ready, 2 * layer + 2)
                    nc.scalar.activation(hid[:], hid[:], ACT.Silu).then_inc(silued, 1)
                    act.wait_ge(turned, 5 * (layer + 1))
                    nc.scalar.activation(hidT[:, 0:512], c.ps[0][:], ACT.Copy).then_inc(copied, 1)
                    nc.scalar.activation(hidT[:, 512:NPOS], c.ps[1][:, 0:P], ACT.Copy).then_inc(copied, 1)
                act.wait_ge(loaded, 16 * n_loads)
                act.wait_ge(h_ready, tiles + 2)
                nc.scalar.activation(minus[:, 0:512], c.ps[2][0:H, :], ACT.Identity,
                                     bias=b2[:]).then_inc(copied, 1)
                nc.scalar.activation(minus[:, 512:NPOS], c.ps[3][0:H, 0:P], ACT.Identity,
                                     bias=b2[:]).then_inc(copied, 1)
                act.wait_ge(copied, 6)
                nc.scalar.activation(minus[:], minus[:], ACT.Copy, scale=-1.0).then_inc(table, 2)

            @block.tensor
            def _(pe):
                pe.wait_ge(loaded, 16 * n_loads)
                for layer in range(2):
                    pe.wait_ge(silued, layer + 1)
                    for t in range(tiles):
                        nc.tensor.transpose(c.ps[t // 4][:, (t % 4) * P:(t % 4 + 1) * P], hid[:, t, :],
                                            c.ident[:]).then_inc(turned, 1)
                    pe.wait_ge(copied, 2 * (layer + 1))
                    if layer == 0:
                        for t in range(tiles):
                            nc.tensor.matmul(c.ps[4 + t // 4][:, (t % 4) * P:(t % 4 + 1) * P],
                                             hidT[:, t * P:(t + 1) * P], w1[:], start=True,
                                             stop=True).then_inc(h_ready, 1)
                    else:
                        nc.tensor.matmul(c.ps[2][0:H, :], w2[:], hidT[:, 0:512], start=True,
                                         stop=True).then_inc(h_ready, 1)
                        nc.tensor.matmul(c.ps[3][0:H, 0:P], w2[:], hidT[:, 512:NPOS], start=True,
                                         stop=True).then_inc(h_ready, 1)
        st.end()


def table_rows(c):
    rows = [t[:].rearrange("p t d -> p (t d)").rearrange("p (h m) -> p h m", m=S) for t in (c.xn, c.s)]
    dst = [rows[h // 8][:, h % 8, :] for h in range(H)]
    src = [bass.AP(tensor=c.table.tensor, offset=c.table.offset + h * NPOS, ap=[[1, P], [1, S]]) for h in range(H)]
    return list(zip(dst, src))


def place_bias(nc, c, rows, bias):
    with ExitStack() as ctx:
        st = Stage(nc, ctx, "pl")
        reversal, placed, act_placed, dve_placed, masked = st.sems("reversal", "placed", "act_placed", "dve_placed",
                                                                   "masked")
        reverse = st.sb("reverse", [P, P])
        with nc.Block() as block:
            @block.gpsimd
            def _(pool):
                nc.gpsimd.memset(reverse[:], 0.0).then_inc(reversal, 1)
                pool.wait_ge(reversal, 1)
                nc.gpsimd.affine_select(out=reverse[:], in_=reverse[:], compare_op=ALU.not_equal, fill=1.0,
                                        base=-(P - 1), pattern=[[1, P]], channel_multiplier=1).then_inc(reversal, 1)
                for h in range(H):
                    pool.wait_ge(dve_placed if h % 2 else act_placed, h // 2 + 1)
                    diag = bias[:, h, S - P:S]
                    nc.gpsimd.affine_select(out=diag, in_=diag, compare_op=ALU.is_ge, fill=MASKED, base=0,
                                            pattern=[[-1, P]], channel_multiplier=1).then_inc(masked, 1)

            @block.tensor
            def _(pe):
                pe.wait_ge(reversal, 2)
                for h in range(H):
                    if h >= 4:
                        pe.wait_ge(dve_placed if h % 2 else act_placed, (h - 4) // 2 + 1)
                    nc.tensor.matmul(c.ps[4 + h % 4][:], reverse[:], rows[h][0], start=True,
                                     stop=True).then_inc(placed, 1)

            @block.scalar
            def _(act):
                for h in range(0, H, 2):
                    act.wait_ge(placed, h + 1)
                    nc.scalar.activation(bias[:, h, :], c.ps[4 + h % 4][:], ACT.Copy).then_inc(act_placed, 1)

            @block.vector
            def _(dve):
                for h in range(1, H, 2):
                    dve.wait_ge(placed, h + 1)
                    nc.vector.tensor_copy(bias[:, h, :], c.ps[4 + h % 4][:]).then_inc(dve_placed, 1)
        st.end()


def ternary_gate(nc, c, w, ahead):
    f_tiles = FF // P
    with ExitStack() as ctx:
        st = Stage(nc, ctx, "g1")
        loaded, dve_done, summed, spread, weights, up_done, gelued, down_done, g_ready, silued, came_ahead = st.sems(
            "loaded", "dve_done", "summed", "spread", "weights", "up_done", "gelued", "down_done", "g_ready", "silued",
            "came_ahead")
        w1 = st.sb("w1", [P, FF])
        w2 = st.sb("w2", [P, f_tiles, D])
        b1 = st.sb("b1", [P, f_tiles])
        b2 = st.sb("b2", [P, D])
        row_sum = st.sb("row_sum", [P, 2])
        half_scale = st.sb("half_scale", [P, 2])
        minus_half = st.sb("minus_half", [P, 2])
        above = st.sb("above", [P, FF])
        below = st.sb("below", [P, FF])
        hT = st.sb("hT", [P, 2, f_tiles, S])

        with nc.Block() as block:
            @block.sync
            def _(sp):
                sp.dma_start(w1[:], w["L1_ffn_W1T"]).then_inc(loaded, 16)
                sp.dma_start(w2[:], w["L1_ffn_W2T"].rearrange("(t p) d -> p t d", p=P)).then_inc(loaded, 16)
                sp.dma_start(b1[:], w["L1_ffn_b1T"]).then_inc(loaded, 16)
                sp.dma_start(b2[:], row_bcast(w["L1_ffn_b2"], D)).then_inc(loaded, 16)
                for dst, src in ahead:
                    sp.dma_start(dst, src).then_inc(came_ahead, 16)
                sp.wait_ge(came_ahead, 16 * len(ahead))

            @block.vector
            def _(dve):
                chain = Chain(dve, dve_done)
                dve.wait_ge(loaded, 64)
                mats = [w1[:], w2[:].rearrange("p t d -> p (t d)")]
                for i, m in enumerate(mats):
                    chain.mark(nc.vector.tensor_reduce(row_sum[:, i:i + 1], m, AX, ALU.add,
                                                       apply_absolute_value=True))
                chain.wait()
                nc.vector.tensor_copy(row_sum[:], row_sum[:]).then_inc(summed, 1)
                dve.wait_ge(spread, 1)
                chain.link(nc.vector.tensor_scalar(half_scale[:], c.ps[0][:, 0:2], 1.0 / (FF * D), 1e-8,
                                                   ALU.mult, ALU.max))
                chain.link(nc.vector.tensor_scalar(half_scale[:], half_scale[:], 0.5, None, ALU.mult))
                chain.link(nc.vector.tensor_scalar(minus_half[:], half_scale[:], -1.0, None, ALU.mult))
                for i, m in enumerate(mats):
                    chain.mark(nc.vector.tensor_scalar(above[:], m, half_scale[:, i:i + 1], None, ALU.is_gt))
                    chain.link(nc.vector.tensor_scalar(below[:], m, minus_half[:, i:i + 1], None, ALU.is_lt))
                    chain.link(nc.vector.tensor_tensor(above[:], above[:], below[:], ALU.subtract))
                    chain.link(nc.vector.tensor_tensor(above[:], above[:], m, ALU.subtract))
                    chain.link(nc.vector.tensor_tensor(m, m, above[:], ALU.add))
                nc.vector.tensor_copy(row_sum[:], row_sum[:]).then_inc(weights, 1)
                for b in range(NB):
                    dve.wait_ge(down_done, b + 1)
                    nc.vector.tensor_tensor(c.g[:, b * QB:(b + 1) * QB, :],
                                            c.ps[6 + b % 2][:].rearrange("p (q d) -> p q d", d=D),
                                            over_blocks(b2[:], QB), ALU.add).then_inc(g_ready, 1)

            @block.tensor
            def _(pe):
                pe.wait_ge(summed, 1)
                nc.tensor.matmul(c.ps[0][:, 0:2], c.ones[:], row_sum[:], start=True, stop=True).then_inc(spread, 1)
                pe.wait_ge(weights, 1)
                for b in range(NB + 1):
                    if b < NB:
                        for f in range(f_tiles):
                            n = b * f_tiles + f
                            if n >= 4:
                                pe.wait_ge(gelued, n - 3)
                            nc.tensor.matmul(c.ps[n % 4][:], w1[:, f * P:(f + 1) * P], c.xnT[:, b, :], start=True,
                                             stop=True).then_inc(up_done, 1)
                    if b > 0:
                        d = b - 1
                        pe.wait_ge(gelued, f_tiles * (d + 1))
                        if d >= 2:
                            pe.wait_ge(g_ready, d - 1)
                        for q in range(QB):
                            for f in range(f_tiles):
                                last = nc.tensor.matmul(c.ps[6 + d % 2][:, q * P:(q + 1) * P],
                                                        hT[:, d % 2, f, q * P:(q + 1) * P], w2[:, f, :],
                                                        start=f == 0, stop=f == f_tiles - 1)
                        last.then_inc(down_done, 1)

            @block.scalar
            def _(act):
                act.wait_ge(loaded, 64)
                for b in range(NB):
                    if b >= 2:
                        act.wait_ge(down_done, b - 1)
                    for f in range(f_tiles):
                        n = b * f_tiles + f
                        act.wait_ge(up_done, n + 1)
                        nc.scalar.activation(hT[:, b % 2, f, :], c.ps[n % 4][:], ACT.Gelu,
                                             bias=b1[:, f:f + 1]).then_inc(gelued, 1)
                act.wait_ge(g_ready, NB)
                nc.scalar.activation(c.g[:], c.g[:], ACT.Silu).then_inc(silued, 1)
        st.end()


def layer1(nc, c, w, xaT):
    with ExitStack() as ctx:
        position_table(nc, c, w)
        a = Heads("a1", DH, causal=True, shared_kv=True, projected=True, dst=c.s)
        k = Work(nc, ctx, a)
        k.xT = k.sb("xT", [P, S])
        k.QT = k.sb("QT", [P, a.tiles, S])
        k.KT = k.sb("KT", [P, 2, S])
        k.V = k.sb("V", [P, QB, P])
        k.wq = k.sb("wq", [P, a.inner])
        k.wk = k.sb("wk", [P, P])
        k.wv = k.sb("wv", [P, P])
        k.q_scale = -DH ** -0.5
        k.source = xaT
        k.biased = k.sb("biased", [P, 3, S])
        k.null_w = k.sb("null_w", [P, H])
        k.null_k = k.sb("null_k", [P, DH])
        k.null_v = k.sb("null_v", [P, DH])
        k.null_bias = k.sb("null_bias", [P, UNITS])
        k.null_s = k.sb("null_s", [P, UNITS])
        k.null_less = k.sb("null_less", [P, UNITS // GROUP, GROUP])
        k.null_weight = k.sb("null_weight", [P, 2, GROUP])
        k.null_part = k.sb("null_part", [P, 2, GROUP, DH])
        wkv = w["L1_attn_Wkv"]
        null_kv = w["L1_attn_null_kv"]
        weights = [(k.wq[:], w["L1_attn_Wq"]), (k.wk[:, 0:DH], wkv[:, 0:DH]), (k.wk[:, DH:P], wkv[:, 0:DH]),
                   (k.wv[:, 0:DH], wkv[:, DH:2 * DH]), (k.wv[:, DH:P], wkv[:, DH:2 * DH]),
                   (k.null_v[:], row_bcast(null_kv[1], DH)), (k.null_k[:], row_bcast(null_kv[0], DH)),
                   (k.wo[:], w["L1_attn_Wo"].rearrange("(t p) d -> p t d", p=P))]
        weights += [(k.null_bias[:, q * H:(q + 1) * H], row_bcast(w["L1_attn_null_attn_bias"], H))
                    for q in range(QB)]
        rows = table_rows(c)
        ternary_gate(nc, c, w, ahead=rows + weights)
        a.bias = ctx.enter_context(nc.sbuf_tensor("bias", [P, H, S], F32))
        place_bias(nc, c, rows, a.bias)
        with ExitStack() as first:
            st = Stage(nc, first, "a1l")
            (dve_done,) = st.sems("dve_done")
            with nc.Block() as block:
                @block.vector
                def _(dve):
                    chain = Chain(dve, dve_done)
                    chain.mark(nc.vector.memset(k.KT[:], 0.0))
                    product = k.QT[:, 0:a.inner // S, :].rearrange("p a (b d) -> p (a b) d", d=DH)
                    chain.mark(nc.vector.tensor_scalar(k.null_bias[:], k.null_bias[:], -1.0, None, ALU.mult))
                    chain.link(nc.vector.tensor_tensor(product, k.wq[:].rearrange("p (h d) -> p h d", d=DH),
                                                       over_blocks(k.null_k[:], H), ALU.mult))
                    chain.link(nc.vector.tensor_reduce(k.null_w[:], product, AX, ALU.add))
                    nc.vector.tensor_scalar(k.null_w[:], k.null_w[:], k.q_scale, None, ALU.mult).then_inc(dve_done, 1)
            st.end()
        with nc.Fori(0, NB) as b:
            attention_stage(nc, c, a, b, k)




def project_stage(nc, c, name, srcT, transposed, value=None, rope=None, split=False, ahead=(), load_first=None):
    with ExitStack() as ctx:
        st = Stage(nc, ctx, name)
        loaded, made, act_copied, dve_copied, dve_done, v_made, v_copied, upper_ready, parted, came_ahead, *stored = st.sems(
            "loaded", "made", "act_copied", "dve_copied", "dve_done", "v_made", "v_copied", "upper_ready", "parted",
            "came_ahead",
            "stored_even", "stored_odd")
        mats, biases, tables = [], [], []
        pairs = []
        for i, (weight, bias, scale, _) in enumerate(transposed):
            group = []
            for k, src in enumerate(weight if rope else (weight,)):
                m = st.sb(f"w{i}{k}", [P, D])
                group.append(m)
                pairs.append((m[:], src))
            mats.append(group)
            biases.append(None)
            if bias is not None:
                biases[i] = st.sb(f"b{i}", [P, 1])
                pairs.append((biases[i][:], column(bias)))
            if rope:
                tables.append([st.sb(f"t{i}{k}", [P, S]) for k in range(2)])
                pairs += [(t[:], src) for t, src in zip(tables[i], scale)]
        if value is not None:
            wv = st.sb("wv", [P, D])
            pairs.append((wv[:], value[0]))
        n = len(transposed)
        kept = st.sb("kept", [P, n, S * 2])
        turned = st.sb("rotated", [P, 2, S]) if rope else None
        upper = st.sb("upper", [P, n, S * 2]) if split else None
        copied = dve_copied if rope else act_copied
        half_stores = [16 * n * (NB // 2) * (2 if split else 1) + (32 * n if split and i == 0 else 0) for i in range(2)]

        def stores_before(b):
            return 16 * n * (b // 2) * (2 if split else 1) + (32 * n if split and b % 2 == 0 and b > 0 else 0)

        with nc.Block() as block:
            @block.sync
            def _(sp):
                for dst, src in pairs:
                    sp.dma_start(dst, src).then_inc(loaded, 16)
                for dst, src in ahead:
                    sp.dma_start(dst, src).then_inc(came_ahead, 16)
                n_ahead = len(ahead)
                for b in range(NB):
                    if b == 2 and load_first is not None:
                        sp.wait_ge(stored[0], stores_before(2))
                        n_ahead += load_first(sp, came_ahead)
                    for i, (_, _, _, dram) in enumerate(transposed):
                        j = b * n + i
                        now = slice((b % 2) * S, (b % 2 + 1) * S)
                        sp.wait_ge(parted if split else copied, j + 1)
                        if not split:
                            sp.dma_start(dram[:, b, :], kept[:, i, now]).then_inc(stored[b % 2], 16)
                            continue
                        for to in (b, NB) if b == 0 else (b,):
                            sp.dma_start(dram[0, :, to, :], upper[:, i, now]).then_inc(stored[b % 2], 16)
                            sp.dma_start(dram[1, :, to, :], kept[:, i, now]).then_inc(stored[b % 2], 16)
                for half, total in zip(stored, half_stores):
                    sp.wait_ge(half, total)
                if n_ahead:
                    sp.wait_ge(came_ahead, 16 * n_ahead)

            @block.tensor
            def _(pe):
                pe.wait_ge(loaded, 16 * len(pairs))
                for b in range(NB):
                    for i in range(n):
                        j = b * n + i
                        if j >= 2:
                            pe.wait_ge(copied, j - 1)
                        for k, m in enumerate(mats[i]):
                            last = nc.tensor.matmul(c.ps[2 * k + j % 2][:], m[:], srcT[:, b, :], start=True, stop=True)
                        last.then_inc(made, 1)
                    if value is not None:
                        if b >= 2:
                            pe.wait_ge(v_copied, b - 1)
                        for q in range(QB):
                            last = nc.tensor.matmul(c.ps[4 + b % 2][:, q * P:(q + 1) * P],
                                                    srcT[:, b, q * P:(q + 1) * P], wv[:], start=True, stop=True)
                        last.then_inc(v_made, 1)

            @block.scalar
            def _(act):
                act.wait_ge(loaded, 16 * len(pairs))
                for b in range(NB):
                    if not rope:
                        for i, (_, _, scale, _) in enumerate(transposed):
                            j = b * n + i
                            act.wait_ge(made, j + 1)
                            if b >= 2:
                                act.wait_ge(stored[b % 2], stores_before(b))
                            bias = {} if biases[i] is None else {"bias": biases[i][:]}
                            nc.scalar.activation(kept[:, i, (b % 2) * S:(b % 2 + 1) * S], c.ps[j % 2][:],
                                                 ACT.Identity, scale=scale, **bias).then_inc(act_copied, 1)
                    if value is not None:
                        act.wait_ge(v_made, b + 1)
                        nc.scalar.activation(value[1][:, b * QB:(b + 1) * QB, :].rearrange("p q d -> p (q d)"),
                                             c.ps[4 + b % 2][:], ACT.Copy).then_inc(v_copied, 1)

            if rope or split:
                @block.vector
                def _(dve):
                    chain = Chain(dve, dve_done)
                    dve.wait_ge(loaded, 16 * len(pairs))
                    for b in range(NB):
                        for i in range(n):
                            j = b * n + i
                            now = slice((b % 2) * S, (b % 2 + 1) * S)
                            if rope:
                                dve.wait_ge(made, j + 1)
                                if j > 0:
                                    dve.wait_ge(dve_copied, j)
                                if b >= 2:
                                    dve.wait_ge(stored[b % 2], stores_before(b))
                                for k in range(2):
                                    chain.mark(nc.vector.tensor_tensor(turned[:, k, :], c.ps[2 * k + j % 2][:],
                                                                       tables[i][k][:], ALU.mult))
                                chain.wait()
                                nc.vector.tensor_tensor(kept[:, i, now], turned[:, 0, :], turned[:, 1, :],
                                                        ALU.add).then_inc(dve_copied, 1)
                            if split:
                                dve.wait_ge(copied, j + 1)
                                nc.vector.tensor_scalar(upper[:, i, now].bitcast(I32), kept[:, i, now].bitcast(I32),
                                                        UPPER, None, ALU.bitwise_and).then_inc(upper_ready, 1)

            if split:
                @block.gpsimd
                def _(pool):
                    for b in range(NB):
                        for i in range(n):
                            now = slice((b % 2) * S, (b % 2 + 1) * S)
                            pool.wait_ge(upper_ready, b * n + i + 1)
                            nc.gpsimd.tensor_tensor(kept[:, i, now], kept[:, i, now], upper[:, i, now],
                                                    ALU.subtract).then_inc(parted, 1)
        st.end()


def unit_length(nc, c, q, k):
    with ExitStack() as ctx:
        st = Stage(nc, ctx, "len")
        dve_done, squared, summed, rooted, ready, divided = st.sems("dve_done", "squared", "summed", "rooted", "ready",
                                                                    "divided")
        square = st.sb("square", [P, 2, DN, S])
        length = st.sb("length", [P, 2, S])
        split = S * 3 // 8

        def divide(eng, m, i, part):
            n = part.stop - part.start
            return eng.tensor_tensor(m[:, :, part], m[:, :, part],
                                     length[:, i, part].unsqueeze(1).broadcast_to([P, DN, n]), ALU.mult)

        with nc.Block() as block:
            @block.scalar
            def _(act):
                for i, m in enumerate((q, k)):
                    nc.scalar.activation(square[:, i], m, ACT.Square).then_inc(squared, 1)
                for i in range(2):
                    act.wait_ge(summed, i + 1)
                    nc.scalar.activation(length[:, i, :], length[:, i, :], ACT.Sqrt).then_inc(rooted, 1)

            @block.vector
            def _(dve):
                chain = Chain(dve, dve_done)
                for i in range(2):
                    dve.wait_ge(squared, i + 1)
                    nc.vector.tensor_reduce(length[:, i, :], square[:, i].rearrange("p d t -> p t d"), AX,
                                            ALU.add).then_inc(summed, 1)
                for i in (1, 0):
                    dve.wait_ge(rooted, 2)
                    chain.link(nc.vector.tensor_scalar(length[:, i, :], length[:, i, :], 1e-12, None, ALU.max))
                    nc.vector.reciprocal(length[:, i, :], length[:, i, :]).then_inc(ready, 1)
                dve.wait_ge(ready, 2)
                divide(nc.vector, q, 0, slice(0, S)).then_inc(divided, 1)
                divide(nc.vector, k, 1, slice(0, split)).then_inc(divided, 1)

            @block.gpsimd
            def _(pool):
                pool.wait_ge(ready, 1)
                divide(nc.gpsimd, k, 1, slice(split, S)).then_inc(divided, 1)
        st.end()


def threshold_routing(nc, c, w, weight, ahead):
    with ExitStack() as ctx:
        st = Stage(nc, ctx, "r2")
        loaded, made, dve_done, less, exped, ready, turned, copied, b_made, b_copied, came_ahead, zeroed, placed = st.sems(
            "loaded", "made", "dve_done", "less", "exped", "ready", "turned", "copied", "b_made", "b_copied",
            "came_ahead", "zeroed", "placed")
        wgt = st.sb("wgt", [P, E + 1])
        bgt = st.sb("bgt", [P, E + 1])
        logit = st.sb("logit", [P, TB, E + 1])
        top = st.sb("top", [P, TB, 1])
        total = st.sb("total", [P, TB, 1])
        none = st.sb("none", [P, TB, 1])
        packed = P // E
        halves = TB // packed
        weightT = st.sb("weightT", [P, halves, P])
        bias_of = st.sb("bias_of", [P, packed, D])
        gate, thr = logit[:, :, 0:E], logit[:, :, E:E + 1]

        def spread(t):
            return t[:].broadcast_to([P, TB, E])

        with nc.Block() as block:
            @block.sync
            def _(sp):
                sp.dma_start(wgt[:, 0:E], w["L2_ffn_Wg"]).then_inc(loaded, 16)
                sp.dma_start(wgt[:, E:E + 1], w["L2_ffn_Wt"]).then_inc(loaded, 16)
                sp.dma_start(bgt[:, 0:E], row_bcast(w["L2_ffn_bg"], E)).then_inc(loaded, 16)
                sp.dma_start(bgt[:, E:E + 1], row_bcast(w["L2_ffn_bt"], 1)).then_inc(loaded, 16)
                sp.wait_ge(zeroed, 1)
                for j in range(packed):
                    sp.dma_start(bias_of[j * E:(j + 1) * E, j, :], w["L2_ffn_b2"]).then_inc(placed, 16)
                for dst, src in ahead:
                    sp.dma_start(dst, src).then_inc(came_ahead, 16)
                sp.wait_ge(came_ahead, 16 * len(ahead))

            @block.tensor
            def _(pe):
                pe.wait_ge(loaded, 64)
                for t in range(TB):
                    last = nc.tensor.matmul(c.ps[0][:, t * (E + 1):(t + 1) * (E + 1)],
                                            c.xnT[:, t // QB, (t % QB) * P:(t % QB + 1) * P], wgt[:],
                                            start=True, stop=True)
                last.then_inc(made, 1)
                pe.wait_ge(ready, 1)
                flat = weight[:].rearrange("p t e -> p (t e)")
                for half in range(halves):
                    nc.tensor.transpose(c.ps[1][:, half * P:(half + 1) * P], flat[:, half * P:(half + 1) * P],
                                        c.ident[:]).then_inc(turned, 1)
                pe.wait_ge(copied, 1)
                pe.wait_ge(placed, 16 * packed)
                for b in range(NB):
                    if b >= 2:
                        pe.wait_ge(b_copied, b - 1)
                    j = b * QB % packed
                    nc.tensor.matmul(c.ps[3 + b % 2][:], weightT[:, b * QB // packed, :], bias_of[:, j:j + QB, :],
                                     start=True, stop=True).then_inc(b_made, 1)

            @block.scalar
            def _(act):
                act.wait_ge(less, 1)
                nc.scalar.activation(gate, gate, ACT.Exp).then_inc(exped, 1)
                nc.scalar.activation(thr, thr, ACT.Tanh, scale=0.5).then_inc(exped, 1)
                act.wait_ge(turned, halves)
                nc.scalar.activation(weightT[:].rearrange("p h t -> p (h t)"), c.ps[1][:, 0:halves * P],
                                     ACT.Copy).then_inc(copied, 1)

            @block.vector
            def _(dve):
                chain = Chain(dve, dve_done)
                nc.vector.memset(bias_of[:], 0.0).then_inc(zeroed, 1)
                dve.wait_ge(loaded, 64)
                dve.wait_ge(made, 1)
                chain.link(nc.vector.tensor_tensor(
                    logit[:], c.ps[0][:, 0:TB * (E + 1)].rearrange("p (t e) -> p t e", e=E + 1),
                    over_blocks(bgt[:]), ALU.add))
                chain.link(nc.vector.tensor_reduce(top[:], gate, AX, ALU.max))
                nc.vector.tensor_tensor(gate, gate, spread(top), ALU.subtract).then_inc(less, 1)
                dve.wait_ge(exped, 2)
                chain.link(nc.vector.tensor_reduce(total[:], gate, AX, ALU.add))
                chain.link(nc.vector.reciprocal(total[:], total[:]))
                chain.link(nc.vector.tensor_tensor(gate, gate, spread(total), ALU.mult))
                chain.link(nc.vector.tensor_scalar(top[:], thr, 1.0, 0.0625, ALU.add, ALU.mult))
                chain.link(nc.vector.tensor_tensor(gate, gate, spread(top), ALU.subtract))
                chain.link(nc.vector.tensor_scalar(gate, gate, 0.0, None, ALU.max))
                chain.link(nc.vector.tensor_reduce(total[:], gate, AX, ALU.add))
                chain.link(nc.vector.tensor_scalar(none[:], total[:], 0.0, None, ALU.is_equal))
                chain.link(nc.vector.tensor_tensor(total[:], total[:], none[:], ALU.add))
                chain.link(nc.vector.reciprocal(total[:], total[:]))
                nc.vector.tensor_tensor(weight[:], gate, spread(total), ALU.mult).then_inc(ready, 1)
                for b in range(NB):
                    dve.wait_ge(b_made, b + 1)
                    nc.vector.tensor_copy(c.g[:, b * QB:(b + 1) * QB, :].rearrange("p q d -> p (q d)"),
                                          c.ps[3 + b % 2][:]).then_inc(b_copied, 1)
        st.end()


STEPS = S // NB
PARTS = (0, STEPS // 2, STEPS * 7 // 8, STEPS)
BETA, CLAMP, STATE_CAP, SHRINK = 0.9, 1.0, 10.0, 0.9


def delta_and_experts(nc, c, b, k):
    f_tiles = FF // P
    with ExitStack() as ctx:
        st = Stage(nc, ctx, "d2")
        (ready, taken, negated, stepped, dve_done, o_done, up_done, gelued, down_done, scaled, added) = st.sems(
            "ready", "taken", "negated", "stepped", "dve_done", "o_done", "up_done", "gelued", "down_done", "scaled",
            "added")

        def of_pass(t):
            return t[:, :, bass.ts(b, STEPS)].rearrange("p d t -> p t d")

        with nc.Block() as block:
            @block.vector
            def _(dve):
                chain = Chain(dve, dve_done)
                nc.vector.tensor_copy(k.k_now[:], of_pass(k.k)).then_inc(taken, 1)
                nc.vector.tensor_copy(k.v_now[:], of_pass(k.v)).then_inc(taken, 1)
                dve.wait_ge(taken, 2)

                def key(t):
                    return k.k_now[:, t, :].unsqueeze(1).broadcast_to([P, DN, DN])

                def link_to(count):
                    dve.wait_ge(dve_done, count)

                before = k.raw[:, STEPS - 1]
                chain.link(nc.vector.tensor_tensor(k.prod[:], before, key(0), ALU.mult))
                chain.mark(nc.vector.tensor_reduce(k.old[:], k.prod[:], AX, ALU.add))
                dve.wait_ge(negated, 1)
                chain.link(nc.vector.tensor_tensor(k.both[:], k.nk_now[:, 0:STEPS - 1, :], k.k_now[:, 1:STEPS, :],
                                                   ALU.mult))
                chain.link(nc.vector.tensor_reduce(k.key_pair[:, 1:STEPS], k.both[:], AX, ALU.add))

                for t in range(STEPS):
                    raw = k.raw[:, t]
                    shrink = k.shrink[:, (t - 1) % STEPS:(t - 1) % STEPS + 1]
                    more = t + 1 < STEPS
                    chain.mark(nc.vector.scalar_tensor_tensor(out=k.delta[:], in0=k.old[:], scalar=shrink,
                                                              in1=k.v_now[:, t, :], op0=ALU.mult, op1=ALU.subtract))
                    delta_done = chain.n
                    chain.mark(nc.vector.tensor_scalar(k.shrunk[:], before, shrink, None, ALU.mult))
                    shrunk_done = chain.n
                    link_to(delta_done)
                    chain.link(nc.vector.tensor_scalar(k.clipped[:], k.delta[:], -CLAMP, CLAMP, ALU.max, ALU.min))
                    chain.mark(nc.vector.tensor_tensor(
                        k.change[:], k.clipped[:].unsqueeze(2).broadcast_to([P, DN, DN]),
                        k.nk_now[:, t, :].unsqueeze(1).broadcast_to([P, DN, DN]), ALU.mult))
                    change_done = chain.n
                    if more:
                        link_to(shrunk_done)
                        chain.mark(nc.vector.tensor_tensor(k.prod[:], k.shrunk[:], key(t + 1), ALU.mult))
                        product_done = chain.n
                    link_to(change_done)
                    chain.mark(nc.vector.tensor_tensor(raw, k.shrunk[:], k.change[:], ALU.add))
                    raw_done = chain.n
                    if more:
                        link_to(product_done)
                        chain.mark(nc.vector.tensor_reduce(k.part[:], k.prod[:], AX, ALU.add))
                        part_done = chain.n
                    link_to(raw_done)
                    chain.mark(nc.vector.tensor_reduce(k.peak[:], raw.rearrange("p e d -> p (e d)"), AX, ALU.max,
                                                       apply_absolute_value=True))
                    peak_done = chain.n
                    if more:
                        link_to(part_done)
                        chain.mark(nc.vector.scalar_tensor_tensor(out=k.old[:], in0=k.clipped[:],
                                                                  scalar=k.key_pair[:, t + 1:t + 2], in1=k.part[:],
                                                                  op0=ALU.mult, op1=ALU.add))
                    link_to(peak_done)
                    chain.link(nc.vector.tensor_scalar(k.shrink[:, t:t + 1], k.peak[:], STATE_CAP, SHRINK, ALU.is_le,
                                                       ALU.max))
                    if t + 1 in PARTS:
                        nc.vector.tensor_copy(k.peak[:], k.peak[:]).then_inc(stepped, 1)
                    before = raw

            @block.gpsimd
            def _(pool):
                chain = Chain(pool, o_done)

                def outputs(part):
                    first, last = PARTS[part], PARTS[part + 1]
                    n, span = last - first, slice(first, last)
                    pool.wait_ge(stepped, part + 1)
                    tmp = k.o_part[:, 0:n]
                    q = k.q_now[:, span, :].unsqueeze(3).broadcast_to([P, n, DN, DN])
                    chain.link(nc.gpsimd.tensor_tensor(tmp, k.raw[:, span], q, ALU.mult))
                    for half in (4, 2, 1):
                        chain.link(nc.gpsimd.tensor_tensor(tmp[:, :, 0:half, :], tmp[:, :, 0:half, :],
                                                           tmp[:, :, half:2 * half, :], ALU.add))
                    shrink = k.shrink[:, span].unsqueeze(2).broadcast_to([P, n, DN])
                    chain.link(nc.gpsimd.tensor_tensor(tmp[:, :, 0, :], tmp[:, :, 0, :], shrink, ALU.mult))
                    chain.link(nc.gpsimd.tensor_scalar(k.o_now[:, span, :], tmp[:, :, 0, :], CLAMP, -CLAMP, ALU.min,
                                                       ALU.max))
                    chain.mark(nc.gpsimd.tensor_copy(
                        k.q[:, :, bass.ds(b * STEPS + first, n)].rearrange("p d t -> p t d"), k.o_now[:, span, :]))

                nc.gpsimd.tensor_copy(k.w_now[:], k.weight[:, bass.ts(b, QB), :]).then_inc(ready, 1)
                nc.gpsimd.tensor_copy(k.q_now[:], of_pass(k.q)).then_inc(ready, 1)
                pool.wait_ge(ready, 2)
                for e in range(E):
                    pool.wait_ge(scaled, QB * (e + 1))
                    if e >= 1:
                        pool.wait_ge(added, e)
                    g = c.g[:, bass.ts(b, QB), :]
                    nc.gpsimd.tensor_tensor(g, g, k.weighted[:, e % 2, :, :], ALU.add).then_inc(added, 1)
                    if e == E // 2 + 1:
                        outputs(0)
                for part in range(1, len(PARTS) - 1):
                    outputs(part)

            @block.tensor
            def _(pe):
                for e in range(E + 1):
                    if e < E:
                        for f in range(f_tiles):
                            n = e * f_tiles + f
                            if n >= 4:
                                pe.wait_ge(gelued, n - 3)
                            nc.tensor.matmul(c.ps[n % 4][:], k.w1[:, e, f * P:(f + 1) * P], c.xnT[:, b, :],
                                             start=True, stop=True).then_inc(up_done, 1)
                    if e > 0:
                        d = e - 1
                        pe.wait_ge(gelued, f_tiles * (d + 1))
                        if d >= 2:
                            pe.wait_ge(scaled, QB * (d - 1))
                        for q in range(QB):
                            for f in range(f_tiles):
                                last = nc.tensor.matmul(c.ps[4 + d % 2][:, q * P:(q + 1) * P],
                                                        k.hT[:, d % 2, f, q * P:(q + 1) * P], k.w2[:, d, f, :],
                                                        start=f == 0, stop=f == f_tiles - 1)
                        last.then_inc(down_done, 1)

            @block.scalar
            def _(act):
                nc.scalar.activation(k.nk_now[:], of_pass(k.k), ACT.Copy, scale=-BETA).then_inc(negated, 1)
                for e in range(E + 1):
                    if e < E:
                        if e >= 2:
                            act.wait_ge(down_done, e - 1)
                        for f in range(f_tiles):
                            act.wait_ge(up_done, e * f_tiles + f + 1)
                            nc.scalar.activation(k.hT[:, e % 2, f, :], c.ps[f % 4][:], ACT.Gelu_apprx_tanh,
                                                 bias=k.b1[:, e, f:f + 1]).then_inc(gelued, 1)
                    if e > 0:
                        d = e - 1
                        act.wait_ge(down_done, d + 1)
                        if d == 0:
                            act.wait_ge(ready, 1)
                        if d >= 2:
                            act.wait_ge(added, d - 1)
                        for q in range(QB):
                            nc.scalar.activation(k.weighted[:, d % 2, q, :], c.ps[4 + d % 2][:, q * P:(q + 1) * P],
                                                 ACT.Copy, scale=k.w_now[:, q, d:d + 1]).then_inc(scaled, 1)
        st.end()


def delta_output(nc, c, w, o, o_dram):
    with ExitStack() as ctx:
        st = Stage(nc, ctx, "o2")
        loaded, stored, *turned, made, added, silued = st.sems("loaded", "stored", "first_turned", "second_turned", "made",
                                                               "added", "silued")
        oT = st.sb("oT", [P, NB, S])
        wo = st.sb("wo", [P, D])
        bo = st.sb("bo", [P, D])
        with nc.Block() as block:
            @block.sync
            def _(sp):
                sp.dma_start(wo[:], w["L2_attn_WoT"]).then_inc(loaded, 16)
                sp.dma_start(bo[:], row_bcast(w["L2_attn_bo"], D)).then_inc(loaded, 16)
                for part in range(2):
                    heads = slice(part * (P // 2), (part + 1) * (P // 2))
                    sp.dma_start(o_dram[heads], o[heads]).then_inc(stored, 16)
                    sp.wait_ge(stored, 16 * (part + 1))
                    batches = slice(part * (NB // 2), (part + 1) * (NB // 2))
                    sp.dma_start(oT[:, batches, :], bass.AP(
                        tensor=o_dram.tensor, offset=o_dram.offset + part * (NB // 2) * P * S,
                        ap=[[S, P], [P * S, NB // 2], [1, S]])).then_inc(turned[part], 16)

            @block.scalar
            def _(act):
                nc.scalar.activation(c.g[:], c.g[:], ACT.Silu).then_inc(silued, 1)

            @block.tensor
            def _(pe):
                pe.wait_ge(loaded, 32)
                for b in range(NB):
                    if b % (NB // 2) == 0:
                        pe.wait_ge(turned[b // (NB // 2)], 16)
                    if b >= 2:
                        pe.wait_ge(added, b - 1)
                    for q in range(QB):
                        last = nc.tensor.matmul(c.ps[b % 2][:, q * P:(q + 1) * P], oT[:, b, q * P:(q + 1) * P], wo[:],
                                                start=True, stop=True)
                    last.then_inc(made, 1)

            @block.vector
            def _(dve):
                dve.wait_ge(loaded, 32)
                for b in range(NB):
                    dve.wait_ge(made, b + 1)
                    nc.vector.tensor_tensor(c.s[:, b * QB:(b + 1) * QB, :],
                                            c.ps[b % 2][:].rearrange("p (q d) -> p q d", d=D),
                                            over_blocks(bo[:], QB), ALU.add).then_inc(added, 1)
        st.end()


class DeltaWork:
    pass


def layer2(nc, c, w):
    with ExitStack() as ctx:
        def sb(name, shape, dt=F32):
            return ctx.enter_context(nc.sbuf_tensor(f"l2_{name}", shape, dt))

        k = DeltaWork()
        k.q = c.xn[:].rearrange("p t d -> p (t d)").rearrange("p (d t) -> p d t", t=S)
        k.k = c.s[:].rearrange("p t d -> p (t d)").rearrange("p (d t) -> p d t", t=S)
        k.v = sb("v", [P, DN, S])
        dram = [nc.dram_tensor(f"l2_{n}T", (NB, D, S), F32, kind="Internal").ap() for n in "qkv"]
        o_dram = nc.dram_tensor("l2_o", (P, DN, S), F32, kind="Internal").ap()
        k.weight = sb("weight", [P, TB, E])
        k.w1 = sb("w1", [P, E, FF])
        k.w2 = sb("w2", [P, E, FF // P, D])
        k.b1 = sb("b1", [P, E, FF // P])
        k.raw = sb("raw", [P, STEPS, DN, DN])
        k.shrink = sb("shrink", [P, STEPS])
        weights = [(k.w1[:, e, :], w["L2_ffn_W1"][e]) for e in range(E)]
        weights += [(k.w2[:, e, :, :], w["L2_ffn_W2"][e].rearrange("(f p) d -> p f d", p=P)) for e in range(E)]
        weights += [(k.b1[:], w["L2_ffn_b1T"])]
        project_stage(nc, c, "p2", c.xnT, [(w[f"L2_attn_W{n}T"], w[f"L2_attn_b{n}"], 1.0,
                                            d.rearrange("b d t -> d b t")) for n, d in zip("qkv", dram)],
                      ahead=weights)
        heads = [(dst, src.rearrange("b (h d) t -> (b h) d t", d=DN)) for dst, src in zip((k.q, k.k, k.v[:]), dram)]
        threshold_routing(nc, c, w, k.weight, ahead=heads)
        unit_length(nc, c, k.q, k.k)
        k.hT = sb("hT", [P, 2, FF // P, S])
        k.weighted = sb("weighted", [P, 2, QB, D])
        k.q_now, k.k_now, k.nk_now, k.v_now = (sb(n, [P, STEPS, DN]) for n in ("q_now", "k_now", "nk_now", "v_now"))
        k.w_now = sb("w_now", [P, QB, E])
        k.prod = sb("prod", [P, DN, DN])
        k.change = sb("change", [P, DN, DN])
        k.shrunk = sb("shrunk", [P, DN, DN])
        k.both = sb("both", [P, STEPS - 1, DN])
        k.key_pair = sb("key_pair", [P, STEPS])
        k.old, k.part, k.delta, k.clipped = (sb(n, [P, DN]) for n in ("old", "part", "delta", "clipped"))
        k.peak = sb("peak", [P, 1])
        k.o_part = sb("o_part", [P, max(last - first for first, last in zip(PARTS, PARTS[1:])), DN, DN])
        k.o_now = sb("o_now", [P, STEPS, DN])
        with ExitStack() as first:
            st = Stage(nc, first, "l2l")
            (zeroed,) = st.sems("zeroed")
            with nc.Block() as block:
                @block.vector
                def _(dve):
                    nc.vector.memset(k.raw[:, STEPS - 1], 0.0).then_inc(zeroed, 1)
                    nc.vector.memset(k.shrink[:, STEPS - 1:STEPS], 1.0).then_inc(zeroed, 1)
            st.end()
        with nc.Fori(0, NB) as b:
            delta_and_experts(nc, c, b, k)
    delta_output(nc, c, w, k.q, o_dram)


def rms_stage(nc, c, w, name, add, gain, ahead=()):
    with ExitStack() as ctx:
        st = Stage(nc, ctx, name)
        loaded, summed, squared, var_ready, rooted, dve_done, normed, turned, copied, came_ahead = st.sems(
            "loaded", "summed", "squared", "var_ready", "rooted", "dve_done", "normed", "turned", "copied", "came_ahead")
        gain_col = st.sb("gain", [P, 1])
        squares = st.sb("squares", [P, D])
        by_dve = TB // 2 if add else TB * 5 // 8
        dve_squares = st.sb("dve_squares", [P, by_dve, D])
        mean = st.sb("mean", [P, TB])
        scaled = st.sb("scaled", [P, TB, D])
        src = c.g if add else c.xn
        with nc.Block() as block:
            @block.sync
            def _(sp):
                sp.dma_start(gain_col[:], column(gain)).then_inc(loaded, 16)
                for dst, src in ahead:
                    sp.dma_start(dst, src).then_inc(came_ahead, 16)
                if ahead:
                    sp.wait_ge(came_ahead, 16 * len(ahead))

            @block.vector
            def _(dve):
                chain = Chain(dve, dve_done)
                if add:
                    nc.vector.tensor_tensor(c.g[:], c.g[:], c.xn[:], ALU.add).then_inc(summed, 1)
                    dve.wait_ge(summed, 1)
                chain.link(nc.vector.tensor_tensor(dve_squares[:], src[:, 0:by_dve, :], src[:, 0:by_dve, :], ALU.mult))
                chain.link(nc.vector.tensor_reduce(mean[:, 0:by_dve], dve_squares[:], AX, ALU.add))
                dve.wait_ge(squared, TB - by_dve)
                nc.vector.tensor_scalar(mean[:], mean[:], 1.0 / D, RMS_EPS, ALU.mult, ALU.add).then_inc(var_ready, 1)
                dve.wait_ge(rooted, 1)
                chain.link(nc.vector.reciprocal(mean[:], mean[:]))
                for t in range(TB):
                    nc.vector.tensor_scalar(scaled[:, t, :], src[:, t, :], mean[:, t:t + 1], None,
                                            ALU.mult).then_inc(normed, 1)

            @block.tensor
            def _(pe):
                for b in range(NB):
                    pe.wait_ge(normed, QB * (b + 1))
                    if b >= 4:
                        pe.wait_ge(copied, b - 3)
                    for q in range(QB):
                        last = nc.tensor.transpose(c.ps[b % 4][:, q * P:(q + 1) * P], scaled[:, b * QB + q, :],
                                                   c.ident[:])
                    last.then_inc(turned, 1)

            @block.scalar
            def _(act):
                if add:
                    act.wait_ge(summed, 1)
                for t in range(by_dve, TB):
                    if t > by_dve:
                        act.wait_ge(squared, t - by_dve)
                    nc.scalar.activation(squares[:], src[:, t, :], ACT.Square,
                                         accum_out=mean[:, t:t + 1]).then_inc(squared, 1)
                act.wait_ge(var_ready, 1)
                nc.scalar.activation(mean[:], mean[:], ACT.Sqrt).then_inc(rooted, 1)
                act.wait_ge(loaded, 16)
                for b in range(NB):
                    act.wait_ge(turned, b + 1)
                    nc.scalar.activation(c.xnT[:, b, :], c.ps[b % 4][:], ACT.Copy,
                                         scale=gain_col[:]).then_inc(copied, 1)
        st.end()


def load_heads(q_dram, k_dram, k):
    def load(sp, b, buffer, loaded):
        for dram, dst, part_of in ((q_dram, k.QT[buffer], lambda p: p // 2), (k_dram, k.KT[buffer], lambda p: p % 2)):
            for j in range(4):
                for p in range(4):
                    rows = slice(PACK * j + DN * p, PACK * j + DN * (p + 1))
                    heads = dram[part_of(p)].rearrange("(g j d) b t -> j d g b t", j=4, d=DN)[j]
                    sp.dma_start(dst[rows, :, :], heads[:, :, b, :]).then_inc(loaded, 16)
    return load


def narrow_attention(nc, c, name, project, wo, dst):
    with ExitStack() as ctx:
        a = Heads(name, DN, causal=True, dst=dst)
        q_dram, k_dram = (nc.dram_tensor(f"{name}_{n}T", (2, D, NB + 1, S), F32, kind="Internal").ap() for n in "qk")
        values = ctx.enter_context(nc.sbuf_tensor(f"{name}_values", [P, TB, D], F32))
        k = Work(nc, ctx, a)
        k.QT = [k.sb(f"QT{i}", [P, 4, S]) for i in range(2)]
        k.KT = [k.sb(f"KT{i}", [P, 4, S]) for i in range(2)]
        k.V = [k.sb(f"V{i}", [P, QB, D]) for i in range(2)]
        k.source = values
        k.n_loads = 32
        load = load_heads(q_dram, k_dram, k)

        def load_first(sp, came):
            load(sp, 0, 0, came)
            return k.n_loads

        project(q_dram, k_dram, values, ahead=[(k.wo[:], wo.rearrange("(t p) d -> p t d", p=P))],
                load_first=load_first)
        with nc.Fori(0, NB // a.batches) as pair:
            attention_stage(nc, c, a, pair * a.batches, k, load_qkv=load)


def top2_routing(nc, c, w, weight):
    with ExitStack() as ctx:
        st = Stage(nc, ctx, "r3")
        loaded, made, dve_done, less, exped = st.sems("loaded", "made", "dve_done", "less", "exped")
        router = st.sb("router", [P, E])
        prob = st.sb("prob", [P, TB, E])
        rank = st.sb("rank", [P, TB, E])
        over = st.sb("over", [P, TB, E])
        total = st.sb("total", [P, TB, 1])

        def spread(t, n=E):
            return t.broadcast_to([P, TB, n])

        with nc.Block() as block:
            @block.sync
            def _(sp):
                sp.dma_start(router[:], w["L3_ffn_w_router"]).then_inc(loaded, 16)

            @block.tensor
            def _(pe):
                pe.wait_ge(loaded, 16)
                for t in range(TB):
                    last = nc.tensor.matmul(c.ps[0][:, t * E:(t + 1) * E],
                                            c.xnT[:, t // QB, (t % QB) * P:(t % QB + 1) * P], router[:],
                                            start=True, stop=True)
                last.then_inc(made, 1)

            @block.scalar
            def _(act):
                act.wait_ge(less, 1)
                nc.scalar.activation(prob[:], prob[:], ACT.Exp).then_inc(exped, 1)

            @block.vector
            def _(dve):
                chain = Chain(dve, dve_done)
                dve.wait_ge(made, 1)
                logits = c.ps[0][:, 0:TB * E].rearrange("p (t e) -> p t e", e=E)
                chain.link(nc.vector.tensor_reduce(total[:], logits, AX, ALU.max))
                nc.vector.tensor_tensor(prob[:], logits, spread(total[:]), ALU.subtract).then_inc(less, 1)
                dve.wait_ge(exped, 1)
                chain.link(nc.vector.tensor_reduce(total[:], prob[:], AX, ALU.add))
                chain.link(nc.vector.reciprocal(total[:], total[:]))
                chain.link(nc.vector.tensor_tensor(prob[:], prob[:], spread(total[:]), ALU.mult))
                chain.link(nc.vector.memset(rank[:], 0.0))
                for j in range(E):
                    pj = prob[:, :, j:j + 1]
                    chain.link(nc.vector.tensor_tensor(over[:], spread(pj), prob[:], ALU.is_gt))
                    chain.link(nc.vector.tensor_tensor(rank[:], rank[:], over[:], ALU.add))
                    if j < E - 1:
                        behind = slice(j + 1, E)
                        chain.link(nc.vector.tensor_tensor(over[:, :, behind], spread(pj, E - 1 - j),
                                                           prob[:, :, behind], ALU.is_equal))
                        chain.link(nc.vector.tensor_tensor(rank[:, :, behind], rank[:, :, behind],
                                                           over[:, :, behind], ALU.add))
                chain.link(nc.vector.tensor_scalar(rank[:], rank[:], 2.0, None, ALU.is_lt))
                chain.link(nc.vector.tensor_tensor(prob[:], prob[:], rank[:], ALU.mult))
                chain.link(nc.vector.tensor_reduce(total[:], prob[:], AX, ALU.add))
                chain.link(nc.vector.reciprocal(total[:], total[:]))
                nc.vector.tensor_tensor(weight[:], prob[:], spread(total[:]), ALU.mult).then_inc(dve_done, 1)
        st.end()


PASS = 2


def gated_experts(nc, c, b, k):
    h_tiles = HID // P
    turns = PASS * E
    with ExitStack() as ctx:
        st = Stage(nc, ctx, "m3")
        staged, up_done, silued, hid_ready, down_done, acc_done = st.sems(
            "staged", "up_done", "silued", "hid_ready", "down_done", "acc_done")
        with nc.Block(no_gpsimd_drain=True) as block:
            @block.tensor
            def _(pe):
                for e in range(turns + 1):
                    if e < turns:
                        x = c.xnT[:, b + e // E, :]
                        for f in range(h_tiles):
                            n = e * h_tiles + f
                            if n >= 2:
                                pe.wait_ge(hid_ready, n - 1)
                            cols = slice(f * P, (f + 1) * P)
                            nc.tensor.matmul(c.ps[n % 2][:], k.wg[:, e % E, cols], x, start=True,
                                             stop=True).then_inc(up_done, 1)
                            nc.tensor.matmul(c.ps[2 + n % 2][:], k.wu[:, e % E, cols], x, start=True,
                                             stop=True).then_inc(up_done, 1)
                    if e > 0:
                        d = e - 1
                        pe.wait_ge(hid_ready, h_tiles * (d + 1))
                        if d >= 2:
                            pe.wait_ge(acc_done, QB * (d - 1))
                        for q in range(QB):
                            for f in range(h_tiles):
                                last = nc.tensor.matmul(c.ps[4 + d % 2][:, q * P:(q + 1) * P],
                                                        k.hT[:, d % 2, f, q * P:(q + 1) * P], k.wd[:, d % E, f, :],
                                                        start=f == 0, stop=f == h_tiles - 1)
                        last.then_inc(down_done, 1)

            @block.scalar
            def _(act):
                for n in range(turns * h_tiles):
                    act.wait_ge(up_done, 2 * n + 1)
                    if n >= 2:
                        act.wait_ge(hid_ready, n - 1)
                    nc.scalar.activation(k.act[:, n % 2, :], c.ps[n % 2][:], ACT.Silu).then_inc(silued, 1)

            @block.vector
            def _(dve):
                blocks = bass.ds(b * QB, PASS * QB)
                nc.vector.tensor_copy(k.w_now[:], k.weight[:, blocks, :]).then_inc(staged, 1)
                nc.vector.tensor_copy(k.acc[:], c.g[:, blocks, :]).then_inc(staged, 1)
                dve.wait_ge(staged, 2)
                for e in range(turns + 1):
                    if e < turns:
                        for f in range(h_tiles):
                            n = e * h_tiles + f
                            dve.wait_ge(silued, n + 1)
                            dve.wait_ge(up_done, 2 * n + 2)
                            if e >= 2 and f == 0:
                                dve.wait_ge(down_done, e - 1)
                            nc.vector.tensor_tensor(k.hT[:, e % 2, f, :], c.ps[2 + n % 2][:], k.act[:, n % 2, :],
                                                    ALU.mult).then_inc(hid_ready, 1)
                    if e > 0:
                        d = e - 1
                        dve.wait_ge(down_done, d + 1)
                        if d >= 1:
                            dve.wait_ge(acc_done, QB * d)
                        for q in range(QB):
                            acc, weight = (t[:, d // E * QB + q, :] for t in (k.acc, k.w_now))
                            nc.vector.scalar_tensor_tensor(out=acc, in0=c.ps[4 + d % 2][:, q * P:(q + 1) * P],
                                                           scalar=weight[:, d % E:d % E + 1], in1=acc, op0=ALU.mult,
                                                           op1=ALU.add).then_inc(acc_done, 1)
                dve.wait_ge(acc_done, QB * turns)
                nc.vector.tensor_copy(c.g[:, blocks, :], k.acc[:]).then_inc(staged, 1)
        st.end()


class ExpertWork:
    pass


def layer3(nc, c, w):
    def plain(q_dram, k_dram, values, **loads):
        project_stage(nc, c, "p3", c.xnT, [(w["L3_attn_Wqvk"][:, 0:D], None, D ** -0.5, q_dram),
                                           (w["L3_attn_Wqvk"][:, 2 * D:3 * D], None, 1.0, k_dram)],
                      value=(w["L3_attn_Wqvk"][:, D:2 * D], values), split=True, **loads)

    def rotary(q_dram, k_dram, values, **loads):
        rms_stage(nc, c, w, "rms1", False, w["L3_ffn_g1"])
        tables = [w["rope_q_cos"], w["rope_q_sin"]], [w["rope_k_cos"], w["rope_k_sin"]]
        project_stage(nc, c, "p4", c.xnT,
                      [((w["L3_ffn_wq"], w["L3_ffn_wq_turned"]), None, tables[0], q_dram),
                       ((w["L3_ffn_wk"], w["L3_ffn_wk_turned"]), None, tables[1], k_dram)],
                      value=(w["L3_ffn_wv"], values), rope=True, split=True, **loads)

    narrow_attention(nc, c, "a3", plain, w["L3_attn_Wo"], c.s)
    narrow_attention(nc, c, "a4", rotary, w["L3_ffn_wo"], c.g)
    with ExitStack() as ctx:
        def sb(name, shape, dt=F32):
            return ctx.enter_context(nc.sbuf_tensor(f"l3_{name}", shape, dt))

        h_tiles = HID // P
        k = ExpertWork()
        k.weight = sb("weight", [P, TB, E])
        k.wg, k.wu = sb("wg", [P, E, HID]), sb("wu", [P, E, HID])
        k.wd = sb("wd", [P, E, h_tiles, D])
        k.hT = sb("hT", [P, 2, h_tiles, S])
        k.act = sb("act", [P, 2, S])
        k.acc = sb("acc", [P, PASS * QB, D])
        k.w_now = sb("w_now", [P, PASS * QB, E])
        weights = []
        for e in range(E):
            weights += [(k.wg[:, e, :], w["L3_ffn_wg"][e]), (k.wu[:, e, :], w["L3_ffn_wu"][e]),
                        (k.wd[:, e, :, :], w["L3_ffn_wd"][e].rearrange("(f p) d -> p f d", p=P))]
        rms_stage(nc, c, w, "rms2", True, w["L3_ffn_g2"], ahead=weights)
        top2_routing(nc, c, w, k.weight)
        with nc.Fori(0, NB // PASS) as step:
            gated_experts(nc, c, step * PASS, k)




class Buffers:

    def __init__(self, nc, ctx):
        def sb(name, shape, dt=F32):
            return ctx.enter_context(nc.sbuf_tensor(name, shape, dt))

        self.x = sb("x", [P, TB, D])
        self.xn = sb("xn", [P, TB, D])
        self.xnT = sb("xnT", [P, NB, S])
        self.s = sb("s", [P, TB, D])
        self.g = sb("g", [P, TB, D])
        self.ident = sb("ident", [P, P])
        self.ident16 = sb("ident16", [P, P], BF16)
        self.mask16 = sb("mask16", [P, P], BF16)
        self.ones = sb("ones", [P, P])
        self.table = nc.dram_tensor("table", (H, NPOS), F32, kind="Internal").ap()
        self.ps = [ctx.enter_context(nc.psum_tensor(f"ps{i}", [P, 512], F32)) for i in range(8)]


def build(nc, w, out):
    with ExitStack() as ctx:
        c = Buffers(nc, ctx)
        with ExitStack() as ld:
            st = Stage(nc, ld, "load")
            (loaded,) = st.sems("loaded")
            load_all(st, loaded, [(c.x[:, b * QB:(b + 1) * QB, :],
                                   w["L0_attn_latents"][b].rearrange("(q p) d -> p q d", p=P)) for b in range(NB)])
        make_constants(nc, c)

        with ExitStack() as early:
            c.xaT = early.enter_context(nc.sbuf_tensor("xaT", [P, NB, S], F32))
            norm_stage(nc, c, "n0", False, second=(w["L0_attn_ln_gamma"], w["L0_attn_ln_beta"]))
            layer0(nc, c, w, c.xaT)

            norm_stage(nc, c, "n1", True, second=(w["L1_attn_ln_g"], w["L1_attn_ln_b"]))
            layer1(nc, c, w, c.xaT)

        norm_stage(nc, c, "n2", True, affine_s=(w["L1_attn_out_ln_g"], w["L1_attn_out_ln_b"]))
        layer2(nc, c, w)

        norm_stage(nc, c, "n3", True)
        layer3(nc, c, w)
        final_stage(nc, c, out)


_TRANSPOSED = ([f"L0_ffn_{n}" for n in ("wf", "uf", "wi", "ui", "wc", "uc", "wo", "uo")]
               + ["L1_ffn_W1", "L1_ffn_W2"] + [f"L2_attn_W{n}" for n in "qkvo"])
_TILED_BIASES = ("L1_ffn_b1", "L2_ffn_b1")


def _rope_tables():
    inv_freq = 1.0 / 10000.0 ** (np.arange(0, DN, 2, dtype=np.float32) / DN)
    freqs = np.einsum("i,j->ij", np.arange(S, dtype=np.float32), inv_freq)
    emb = np.concatenate([freqs, freqs], axis=-1).astype(np.float32)
    sign = np.where(np.arange(DN) < DN // 2, -1.0, 1.0).astype(np.float32)
    cos = np.tile(np.cos(emb).T, (H, 1)).astype(np.float32)
    sin = np.tile(np.sin(emb).T * sign[:, None], (H, 1)).astype(np.float32)
    scale = np.float32(DN ** -0.5)
    return {"rope_k_cos": cos, "rope_k_sin": sin, "rope_q_cos": cos * scale, "rope_q_sin": sin * scale}


def kernel(**inputs):
    import concourse.bacc as _bacc
    from concourse.bass_utils import run_bass_kernel_spmd as _run

    nc = _bacc.Bacc("TRN2", target_bir_lowering=False, num_devices=1)
    laid = {}
    for name, value in inputs.items():
        a = np.asarray(value)
        if name in _TRANSPOSED:
            laid[name + "T"] = a.T
        elif name in _TILED_BIASES:
            tiled = a.reshape(a.shape[:-1] + (a.shape[-1] // P, P))
            laid[name + "T"] = np.moveaxis(tiled, -1, 0)
        else:
            laid[name] = a
        if name in ("L3_ffn_wq", "L3_ffn_wk"):
            laid[name + "_turned"] = a.reshape(D, H, 2, DN // 2)[:, :, ::-1, :].reshape(D, D)
    laid.update(_rope_tables())
    arrays, w = {}, {}
    for name, a in laid.items():
        a = np.ascontiguousarray(a)
        arrays[f"in_{name}_dram"] = a
        w[name] = nc.dram_tensor(f"in_{name}_dram", a.shape, mybir.dt.from_np(a.dtype), kind="ExternalInput").ap()
    out = nc.dram_tensor("out_0_dram", (NB, S, D), F32, kind="ExternalOutput").ap()
    build(nc, w, out)
    r = _run(nc, [arrays], core_ids=[0])
    return r.results[0]["out_0_dram"]
```
